# Optimizing a Trainium2 kernel written in Bass

```python
import numpy as np
import jax
import jax.numpy as jnp

def _softmax(x, axis=-1):
    return jax.nn.softmax(x, axis=axis)

def _gelu(x):
    return jax.nn.gelu(x, approximate=True)

def _silu(x):
    return jax.nn.silu(x)

def _sigmoid(x):
    return jax.nn.sigmoid(x)

def _layernorm(x, axis=-1, eps=1e-05):
    m = jnp.mean(x, axis=axis, keepdims=True)
    v = jnp.var(x, axis=axis, keepdims=True)
    return (x - m) / jnp.sqrt(v + eps)

def _scatter_add(tgt, idx, src, axis=0):
    return tgt.at[idx].add(src)

def _segment_sum(src, seg, n):
    return jax.ops.segment_sum(src, seg, n)
kernel_name = 'mk_recurrent_d2_jaxref_r4_d5a787'

def setup_inputs(seed: int=0):
    np.random.seed(seed)
    _w = jnp.asarray

    def _L0_attn_setup():
        import jax, jax.numpy as jnp
        import numpy as np
        D_MODEL = 512
        H = 16
        DK = D_MODEL // H
        CHUNK = 64
        B = 2
        T = 1024

        def apply_rope(x):
            d = x.shape[-1]
            t = x.shape[2]
            half = d // 2
            inv_freq = 1.0 / 10000.0 ** (jnp.arange(half, dtype=x.dtype) / half)
            ang = jnp.arange(t, dtype=x.dtype)[:, None] * inv_freq[None, :]
            sin = jnp.sin(ang)[None, None]
            cos = jnp.cos(ang)[None, None]
            x1, x2 = (x[..., :half], x[..., half:])
            return jnp.concatenate([x1 * cos - x2 * sin, x1 * sin + x2 * cos], axis=-1)
        key = jax.random.key(seed)
        ks = jax.random.split(key, 11)
        d = D_MODEL
        w = lambda k: jax.random.normal(k, (d, d), jnp.float32) * 0.02
        b = lambda k: jax.random.normal(k, (d,), jnp.float32) * 0.02
        x = jax.random.normal(ks[0], (B, T, d), jnp.float32)
        return {'x': x, 'qw': w(ks[1]), 'qb': b(ks[2]), 'kw': w(ks[3]), 'kb': b(ks[4]), 'vw': w(ks[5]), 'vb': b(ks[6]), 'gw': w(ks[7]), 'gb': b(ks[8]), 'ow': w(ks[9]), 'ob': b(ks[10])}
    _L0_attn_in = _L0_attn_setup()

    def _L0_ffn_setup():
        import jax, jax.numpy as jnp
        import numpy as np
        D = 512
        M = 256
        E = 32
        K = 6
        G = 8
        KG = 4
        SH = 512
        SCALE = 2.5

        def _route(xf, Wr, br):
            T = xf.shape[0]
            s = jax.nn.sigmoid(xf @ Wr.T + br)
            sg = s.reshape(T, G, E // G)
            group_w = jax.lax.top_k(sg, 2)[0].sum(-1)
            top_g = jax.lax.top_k(group_w, KG)[1]
            gmask = jnp.zeros((T, G), bool).at[jnp.arange(T)[:, None], top_g].set(True)
            masked = jnp.where(gmask[:, :, None], sg, 0.0).reshape(T, E)
            idx = jax.lax.top_k(masked, K)[1]
            w = jnp.take_along_axis(s, idx, axis=1)
            w = w / (w.sum(-1, keepdims=True) + 1e-20)
            return (idx, w * SCALE)
        key = jax.random.key(seed)
        ks = jax.random.split(key, 7)
        w = 0.02
        return {'hidden_tensor': jax.random.normal(ks[0], (2, 512, D), dtype=jnp.float32), 'Wr': jax.random.normal(ks[1], (E, D), dtype=jnp.float32) * w, 'br': jax.random.normal(ks[2], (E,), dtype=jnp.float32) * w, 'W1': jax.random.normal(ks[3], (E, M, D), dtype=jnp.float32) * w, 'W2': jax.random.normal(ks[4], (E, D, M), dtype=jnp.float32) * w, 'Ws1': jax.random.normal(ks[5], (SH, D), dtype=jnp.float32) * w, 'Ws2': jax.random.normal(ks[6], (D, SH), dtype=jnp.float32) * w}
    _L0_ffn_in = _L0_ffn_setup()

    def _L1_attn_setup():
        import jax, jax.numpy as jnp
        import numpy as np
        import math
        D = 512
        H = 32
        HKV = 8
        HD = D // H
        ROPE_BASE = 10000.0

        def _rope_cache(T, hd, base=ROPE_BASE):
            theta = 1.0 / base ** (jnp.arange(0, hd, 2, dtype=jnp.float32) / hd)
            t = jnp.arange(T, dtype=jnp.float32)
            freqs = t[:, None] * theta[None, :]
            return (jnp.cos(freqs), jnp.sin(freqs))

        def _apply_rope(x, cos, sin):
            B, Hh, T, hd = x.shape
            x_ = x.reshape(B, Hh, T, hd // 2, 2)
            x1, x2 = (x_[..., 0], x_[..., 1])
            c = cos[None, None, :, :]
            s = sin[None, None, :, :]
            rx1 = x1 * c - x2 * s
            rx2 = x1 * s + x2 * c
            return jnp.stack([rx1, rx2], axis=-1).reshape(B, Hh, T, hd)
        key = jax.random.key(seed)
        ks = jax.random.split(key, 5)
        B, T = (1, 512)
        sc = 0.02
        return {'x': jax.random.normal(ks[0], (B, T, D), dtype=jnp.float32), 'wq': jax.random.normal(ks[1], (D, D), dtype=jnp.float32) * sc, 'wk': jax.random.normal(ks[2], (HKV * HD, D), dtype=jnp.float32) * sc, 'wv': jax.random.normal(ks[3], (HKV * HD, D), dtype=jnp.float32) * sc, 'wo': jax.random.normal(ks[4], (D, D), dtype=jnp.float32) * sc}
    _L1_attn_in = _L1_attn_setup()

    def _L1_ffn_setup():
        import jax, jax.numpy as jnp
        import numpy as np
        D_MODEL = 512
        D_FF = 2048

        def absmean_quant(w):
            scale = jnp.mean(jnp.abs(w))
            mask = (jnp.abs(w) >= scale * 0.7).astype(w.dtype)
            return jnp.sign(w) * mask
        key = jax.random.key(seed)
        k_x, k_w1, k_w2 = jax.random.split(key, 3)
        x = jax.random.normal(k_x, (4, 1024, D_MODEL), dtype=jnp.float32)
        w1 = jax.random.normal(k_w1, (D_FF, D_MODEL), dtype=jnp.float32)
        b1 = jnp.zeros((D_FF,), dtype=jnp.float32)
        w2 = jax.random.normal(k_w2, (D_MODEL, D_FF), dtype=jnp.float32)
        b2 = jnp.zeros((D_MODEL,), dtype=jnp.float32)
        return {'x': x, 'w1': w1, 'b1': b1, 'w2': w2, 'b2': b2}
    _L1_ffn_in = _L1_ffn_setup()
    _d = {'L0_attn_x': _L0_attn_in['x'], 'L0_attn_qw': _L0_attn_in['qw'], 'L0_attn_qb': _L0_attn_in['qb'], 'L0_attn_kw': _L0_attn_in['kw'], 'L0_attn_kb': _L0_attn_in['kb'], 'L0_attn_vw': _L0_attn_in['vw'], 'L0_attn_vb': _L0_attn_in['vb'], 'L0_attn_gw': _L0_attn_in['gw'], 'L0_attn_gb': _L0_attn_in['gb'], 'L0_attn_ow': _L0_attn_in['ow'], 'L0_attn_ob': _L0_attn_in['ob'], 'L0_ffn_Wr': _L0_ffn_in['Wr'], 'L0_ffn_br': _L0_ffn_in['br'], 'L0_ffn_W1': _L0_ffn_in['W1'], 'L0_ffn_W2': _L0_ffn_in['W2'], 'L0_ffn_Ws1': _L0_ffn_in['Ws1'], 'L0_ffn_Ws2': _L0_ffn_in['Ws2'], 'L1_attn_wq': _L1_attn_in['wq'], 'L1_attn_wk': _L1_attn_in['wk'], 'L1_attn_wv': _L1_attn_in['wv'], 'L1_attn_wo': _L1_attn_in['wo'], 'L1_ffn_w1': _L1_ffn_in['w1'], 'L1_ffn_b1': _L1_ffn_in['b1'], 'L1_ffn_w2': _L1_ffn_in['w2'], 'L1_ffn_b2': _L1_ffn_in['b2']}
    _x0 = _d['L0_attn_x']
    _d['L0_attn_x'] = jax.random.normal(jax.random.fold_in(jax.random.key(seed), 1), (2, 1024, 512), dtype=_x0.dtype)
    del _x0
    return _d

def reference(L0_attn_x, L0_attn_qw, L0_attn_qb, L0_attn_kw, L0_attn_kb, L0_attn_vw, L0_attn_vb, L0_attn_gw, L0_attn_gb, L0_attn_ow, L0_attn_ob, L0_ffn_Wr, L0_ffn_br, L0_ffn_W1, L0_ffn_W2, L0_ffn_Ws1, L0_ffn_Ws2, L1_attn_wq, L1_attn_wk, L1_attn_wv, L1_attn_wo, L1_ffn_w1, L1_ffn_b1, L1_ffn_w2, L1_ffn_b2):

    def _L0_attn_ref(x, qw, qb, kw, kb, vw, vb, gw, gb, ow, ob):
        import jax, jax.numpy as jnp
        import numpy as np
        D_MODEL = 512
        H = 16
        DK = D_MODEL // H
        CHUNK = 64
        B = 2
        T = 1024

        def apply_rope(x):
            d = x.shape[-1]
            t = x.shape[2]
            half = d // 2
            inv_freq = 1.0 / 10000.0 ** (jnp.arange(half, dtype=x.dtype) / half)
            ang = jnp.arange(t, dtype=x.dtype)[:, None] * inv_freq[None, :]
            sin = jnp.sin(ang)[None, None]
            cos = jnp.cos(ang)[None, None]
            x1, x2 = (x[..., :half], x[..., half:])
            return jnp.concatenate([x1 * cos - x2 * sin, x1 * sin + x2 * cos], axis=-1)
        b_, t_, c_ = x.shape
        split = lambda y: y.reshape(b_, t_, H, DK).transpose(0, 2, 1, 3)
        q = split(x @ qw + qb)
        k = split(x @ kw + kb)
        v = split(x @ vw + vb)
        g = jax.nn.sigmoid(split(x @ gw + gb))
        q = jax.nn.elu(apply_rope(q)) + 1.0
        k = jax.nn.elu(apply_rope(k)) + 1.0
        nc = t_ // CHUNK
        qc = q.reshape(b_, H, nc, CHUNK, DK)
        kc = k.reshape(b_, H, nc, CHUNK, DK)
        vc = v.reshape(b_, H, nc, CHUNK, DK)
        gc = g.reshape(b_, H, nc, CHUNK, DK)
        kv = jnp.einsum('bhncd,bhnce->bhnde', kc, vc)
        scum = jnp.cumsum(kv, axis=2)
        zcum = jnp.cumsum(kc.sum(axis=3), axis=2)
        num = jnp.einsum('bhncd,bhnde->bhnce', qc, scum)
        den = jnp.einsum('bhncd,bhnd->bhnc', qc, zcum)[..., None] + 1e-06
        out = gc * (num / den)
        out = out.reshape(b_, H, t_, DK).transpose(0, 2, 1, 3).reshape(b_, t_, c_)
        return out @ ow + ob

    def _L0_ffn_ref(hidden_tensor, Wr, br, W1, W2, Ws1, Ws2):
        import jax, jax.numpy as jnp
        import numpy as np
        D = 512
        M = 256
        E = 32
        K = 6
        G = 8
        KG = 4
        SH = 512
        SCALE = 2.5

        def _route(xf, Wr, br):
            T = xf.shape[0]
            s = jax.nn.sigmoid(xf @ Wr.T + br)
            sg = s.reshape(T, G, E // G)
            group_w = jax.lax.top_k(sg, 2)[0].sum(-1)
            top_g = jax.lax.top_k(group_w, KG)[1]
            gmask = jnp.zeros((T, G), bool).at[jnp.arange(T)[:, None], top_g].set(True)
            masked = jnp.where(gmask[:, :, None], sg, 0.0).reshape(T, E)
            idx = jax.lax.top_k(masked, K)[1]
            w = jnp.take_along_axis(s, idx, axis=1)
            w = w / (w.sum(-1, keepdims=True) + 1e-20)
            return (idx, w * SCALE)
        B, Tlen, C = hidden_tensor.shape
        xf = hidden_tensor.reshape(-1, C).astype(jnp.float32)
        T = xf.shape[0]
        idx, w = _route(xf, Wr, br)
        gate = jnp.zeros((T, E), w.dtype).at[jnp.arange(T)[:, None], idx].add(w)

        def step(acc, ew):
            w1, w2, g = ew
            h = jnp.square(jax.nn.relu(xf @ w1.T)) @ w2.T
            return (acc + g[:, None] * h, None)
        acc, _ = jax.lax.scan(step, jnp.zeros_like(xf), (W1, W2, gate.T))
        moe_out = acc.reshape(B, Tlen, C).astype(hidden_tensor.dtype)
        shared = jnp.square(jax.nn.relu(hidden_tensor @ Ws1.T)) @ Ws2.T
        return shared + moe_out

    def _L1_attn_ref(x, wq, wk, wv, wo):
        import jax, jax.numpy as jnp
        import numpy as np
        import math
        D = 512
        H = 32
        HKV = 8
        HD = D // H
        ROPE_BASE = 10000.0

        def _rope_cache(T, hd, base=ROPE_BASE):
            theta = 1.0 / base ** (jnp.arange(0, hd, 2, dtype=jnp.float32) / hd)
            t = jnp.arange(T, dtype=jnp.float32)
            freqs = t[:, None] * theta[None, :]
            return (jnp.cos(freqs), jnp.sin(freqs))

        def _apply_rope(x, cos, sin):
            B, Hh, T, hd = x.shape
            x_ = x.reshape(B, Hh, T, hd // 2, 2)
            x1, x2 = (x_[..., 0], x_[..., 1])
            c = cos[None, None, :, :]
            s = sin[None, None, :, :]
            rx1 = x1 * c - x2 * s
            rx2 = x1 * s + x2 * c
            return jnp.stack([rx1, rx2], axis=-1).reshape(B, Hh, T, hd)
        B, T, _ = x.shape
        q = (x @ wq.T).reshape(B, T, H, HD).transpose(0, 2, 1, 3)
        k = (x @ wk.T).reshape(B, T, HKV, HD).transpose(0, 2, 1, 3)
        v = (x @ wv.T).reshape(B, T, HKV, HD).transpose(0, 2, 1, 3)
        cos, sin = _rope_cache(T, HD)
        q = _apply_rope(q, cos, sin)
        k = _apply_rope(k, cos, sin)
        rep = H // HKV
        k = jnp.repeat(k, rep, axis=1)
        v = jnp.repeat(v, rep, axis=1)
        scores = jnp.einsum('bhtd,bhsd->bhts', q, k) / math.sqrt(HD)
        mask = jnp.triu(jnp.full((T, T), -jnp.inf, dtype=scores.dtype), k=1)
        scores = scores + mask[None, None, :, :]
        attn = jax.nn.softmax(scores, axis=-1)
        y = jnp.einsum('bhts,bhsd->bhtd', attn, v)
        y = y.transpose(0, 2, 1, 3).reshape(B, T, D)
        return y @ wo.T

    def _L1_ffn_ref(x, w1, b1, w2, b2):
        import jax, jax.numpy as jnp
        import numpy as np
        D_MODEL = 512
        D_FF = 2048

        def absmean_quant(w):
            scale = jnp.mean(jnp.abs(w))
            mask = (jnp.abs(w) >= scale * 0.7).astype(w.dtype)
            return jnp.sign(w) * mask
        w1_q = absmean_quant(w1)
        w2_q = absmean_quant(w2)
        h = jnp.einsum('bsd,fd->bsf', x, w1_q) + b1
        h = jax.nn.gelu(h, approximate=False)
        out = jnp.einsum('bsf,df->bsd', h, w2_q) + b2
        return out
    x = L0_attn_x
    xn = _layernorm(x, axis=-1)
    s = _L0_attn_ref(xn, L0_attn_qw, L0_attn_qb, L0_attn_kw, L0_attn_kb, L0_attn_vw, L0_attn_vb, L0_attn_gw, L0_attn_gb, L0_attn_ow, L0_attn_ob)
    g = _silu(_L0_ffn_ref(xn, L0_ffn_Wr, L0_ffn_br, L0_ffn_W1, L0_ffn_W2, L0_ffn_Ws1, L0_ffn_Ws2))
    x = x + s * g
    xn = _layernorm(x, axis=-1)
    s = _L1_attn_ref(xn, L1_attn_wq, L1_attn_wk, L1_attn_wv, L1_attn_wo)
    g = _silu(_L1_ffn_ref(xn, L1_ffn_w1, L1_ffn_b1, L1_ffn_w2, L1_ffn_b2))
    x = x + s * g
    return x

_drawn_inputs = setup_inputs


def setup_inputs(seed=0):
    import zlib

    import numpy as np

    out = dict(_drawn_inputs(seed))
    spreads = {'L1_ffn_b1': (0.0, 0.8), 'L1_ffn_b2': (0.0, 2.0)}
    factors = {'L0_attn_qw': 8.0,
     'L0_attn_qb': 42.72,
     'L0_attn_kw': 8.0,
     'L0_attn_kb': 42.407,
     'L0_attn_vw': 8.0,
     'L0_attn_vb': 8.0,
     'L0_attn_gw': 8.0,
     'L0_attn_gb': 8.0,
     'L0_attn_ow': 8.0,
     'L0_attn_ob': 8.0,
     'L0_ffn_Wr': 8.0,
     'L0_ffn_br': 8.0,
     'L0_ffn_W1': 8.0,
     'L0_ffn_W2': 8.0,
     'L0_ffn_Ws1': 8.0,
     'L0_ffn_Ws2': 8.0}
    for name, (base, spread) in spreads.items():
        noise = np.random.default_rng([zlib.crc32(name.encode()), seed]).standard_normal(out[name].shape)
        drawn = base * np.exp(spread * noise) if base else spread * noise
        out[name] = jnp.asarray(drawn.astype(out[name].dtype))
    for name, factor in factors.items():
        out[name] = (out[name] * factor).astype(out[name].dtype)
    return out
```

```python
from contextlib import ExitStack

import numpy as np

import concourse.bass as bass
from concourse import mybir

F32 = mybir.dt.float32
F16 = mybir.dt.float16
ALU = mybir.AluOpType
ACT = mybir.ActivationFunctionType
AX = mybir.AxisListType

P = 128
B, T, D = 2, 1024, 512
N = B * T
DC = D // P
TT = 512
NT = N // TT
NJ = N // P
EPS = 1e-5

E, M = 32, 256
G, KG, K = 8, 4, 6
SHARED = 2
EA = E + SHARED
EG = 2
NG = EA // EG
MC = M // P
WE = DC * M + MC * D
LO = 64

SCALE_ROUTE = 2.5
XS = 16.0
WS = 64.0
GS = 64.0
HS = 1.0 / 16.0


class Shared:
    pass


def split_product(pe, out, w_hi, w_lo, x_hi, x_lo, start, stop, **kw):
    pe.matmul(out, w_hi, x_hi, start=start, stop=False, **kw)
    pe.matmul(out, w_hi, x_lo, start=False, stop=False, **kw)
    return pe.matmul(out, w_lo, x_hi, start=False, stop=stop, **kw)


def layer_norm(nc, m, tag):
    ctx = ExitStack()
    with ctx:
        xc = ctx.enter_context(nc.sbuf_tensor(f"{tag}_centred", [P, 2, DC, TT], F32))
        sq = ctx.enter_context(nc.sbuf_tensor(f"{tag}_squares", [P, 2, DC, TT], F32))
        var = ctx.enter_context(nc.sbuf_tensor(f"{tag}_var", [P, 2, TT], F32))
        root = ctx.enter_context(nc.sbuf_tensor(f"{tag}_root", [P, 2, TT], F32))
        tmp = ctx.enter_context(nc.sbuf_tensor(f"{tag}_tmp", [P, 2, TT], F32))
        rstd = ctx.enter_context(nc.sbuf_tensor(f"{tag}_rstd", [P, 2, TT], F32))
        mean_done = m.sem(f"{tag}_mean_done")
        centred = m.sem(f"{tag}_centred_done")
        squared = m.sem(f"{tag}_squared")
        var_done = m.sem(f"{tag}_var_done")
        eps_added = m.sem(f"{tag}_eps_added")
        root_done = m.sem(f"{tag}_root_done")
        newton = m.sem(f"{tag}_newton")
        normed = m.sem(f"{tag}_normed")
        hi_done = m.sem(f"{tag}_hi_done")
        lo_done = m.sem(f"{tag}_lo_done")
        block = ctx.enter_context(nc.Block())

        @block.tensor
        def _(pe):
            def mean(t):
                if t >= 2:
                    pe.wait_ge(centred, t - 1)
                for c in range(DC):
                    mm = pe.matmul(m.bank[:, t % 2, :], m.mean_ones[:, :],
                                   m.x[:, c, t * TT:(t + 1) * TT], start=(c == 0), stop=(c == DC - 1))
                mm.then_inc(mean_done, 1)

            def variance(t):
                pe.wait_ge(squared, t + 1)
                if t >= 2:
                    pe.wait_ge(eps_added, t - 1)
                for c in range(DC):
                    mm = pe.matmul(m.bank[:, 2 + t % 2, :], m.mean_ones[:, :], sq[:, t % 2, c, :],
                                   start=(c == 0), stop=(c == DC - 1))
                mm.then_inc(var_done, 1)

            if tag == "ln0":
                pe.wait_ge(m.x_loaded, 16)
                pe.wait_ge(m.const_loaded, m.const_count)
            mean(0)
            for t in range(NT):
                if t + 1 < NT:
                    mean(t + 1)
                variance(t)

        @block.vector
        def _(dve):
            if tag == "ln0":
                dve.wait_ge(m.x_loaded, 16)
            def centre(t):
                dve.wait_ge(mean_done, t + 1)
                if t >= 2:
                    dve.wait_ge(lo_done, t - 1)
                mean = m.bank[:, t % 2, :].unsqueeze(1).broadcast_to([P, DC, TT])
                dve.tensor_tensor(xc[:, t % 2], m.x[:, :, t * TT:(t + 1) * TT], mean,
                                  ALU.subtract).then_inc(centred, 1)

            def scale(t):
                b = t % 2
                dve.wait_ge(var_done, t + 1)
                dve.tensor_scalar(var[:, b], m.bank[:, 2 + b, :], EPS, None, ALU.add).then_inc(eps_added, 1)
                dve.wait_ge(root_done, t + 1)
                dve.reciprocal(root[:, b], root[:, b]).then_inc(newton, 1)
                dve.wait_ge(newton, 4 * t + 1)
                dve.tensor_tensor(tmp[:, b], root[:, b], root[:, b], ALU.mult).then_inc(newton, 1)
                dve.wait_ge(newton, 4 * t + 2)
                dve.tensor_tensor(tmp[:, b], tmp[:, b], var[:, b], ALU.mult).then_inc(newton, 1)
                dve.wait_ge(newton, 4 * t + 3)
                dve.tensor_scalar(tmp[:, b], tmp[:, b], -0.5 * XS, 1.5 * XS, ALU.mult, ALU.add).then_inc(newton, 1)
                dve.wait_ge(newton, 4 * t + 4)
                dve.tensor_tensor(rstd[:, b], tmp[:, b], root[:, b], ALU.mult).then_inc(normed, 1)
                dve.wait_ge(normed, 2 * t + 1)
                dve.wait_ge(squared, t + 1)
                dve.tensor_tensor(xc[:, b], xc[:, b], rstd[:, b].unsqueeze(1).broadcast_to([P, DC, TT]),
                                  ALU.mult).then_inc(normed, 1)

            centre(0)
            for t in range(NT):
                if t + 1 < NT:
                    centre(t + 1)
                scale(t)

        @block.scalar
        def _(act):
            def square(t):
                act.wait_ge(centred, t + 1)
                if t >= 2:
                    act.wait_ge(var_done, t - 1)
                act.activation(sq[:, t % 2], xc[:, t % 2], ACT.Square).then_inc(squared, 1)

            square(0)
            for t in range(NT):
                if t + 1 < NT:
                    square(t + 1)
                act.wait_ge(eps_added, t + 1)
                if t >= 2:
                    act.wait_ge(normed, 2 * (t - 2) + 1)
                act.activation(root[:, t % 2], var[:, t % 2], ACT.Sqrt).then_inc(root_done, 1)
                act.wait_ge(normed, 2 * t + 2)
                act.activation(m.xh[:, :, t * TT:(t + 1) * TT], xc[:, t % 2], ACT.Copy).then_inc(hi_done, 1)

        @block.gpsimd
        def _(pool):
            for t in range(NT):
                pool.wait_ge(hi_done, t + 1)
                tile = m.xh[:, :, t * TT:(t + 1) * TT]
                pool.tensor_tensor(m.xl[:, :, t * TT:(t + 1) * TT], xc[:, t % 2], tile,
                                   ALU.subtract).then_inc(lo_done, 1)


def router(nc, m):
    ctx = ExitStack()
    with ctx:
        sb = lambda name, shape, dt=F32: ctx.enter_context(nc.sbuf_tensor("rt_" + name, shape, dt))
        wr = sb("wr", [P, DC, E])
        wr_hi = sb("wr_hi", [P, DC, E], F16)
        wr_lo = sb("wr_lo", [P, DC, E], F16)
        br = sb("br", [P, E])
        logit = sb("logit", [P, NJ, E])
        s = sb("s", [P, NJ, E])
        pair = sb("pair", [P, 4, NJ, G])
        gw = sb("gw", [P, NJ, G + 4])
        top = sb("top", [P, NJ, 8])
        kept = sb("kept", [P, NJ, G])
        mx = sb("mx", [P, NJ, E + 2])
        gate = sb("gate", [P, NJ, EA])
        total = sb("total", [P, NJ])
        loaded = m.sem("rt_loaded")
        split = m.sem("rt_split")
        logits_done = m.sem("rt_logits_done")
        step = m.sem("rt_step")
        sig = m.sem("rt_sig")
        gate_done = m.sem("rt_gate_done")
        turned = m.sem("rt_turned")
        gate_hi = m.sem("rt_gate_hi")
        gate_zero = m.sem("rt_gate_zero")
        block = ctx.enter_context(nc.Block())

        @block.sync
        def _(sp):
            sp.dma_start(wr[:, :, :], m.d["WrT"].rearrange("(c p) e -> p c e", p=P)).then_inc(loaded, 16)
            sp.dma_start(br[:, :], m.d["br"]).then_inc(loaded, 16)

        @block.gpsimd
        def _(pool):
            pool.memset(m.gates[:, :], 0.0).then_inc(gate_zero, 1)
            pool.memset(m.acc[:, :, :], 0.0)

        @block.scalar
        def _(act):
            act.wait_ge(loaded, 32)
            act.activation(wr_hi[:, :, :], wr[:, :, :], ACT.Copy, scale=WS).then_inc(split, 1)
            act.wait_ge(step, 1)
            act.activation(s[:, :, :], logit[:, :, :], ACT.Sigmoid).then_inc(sig, 1)
            act.wait_ge(gate_zero, 1)
            for t in range(NT):
                act.wait_ge(turned, 4 * (t + 1))
                act.activation(m.gates[0:EA, t * TT:(t + 1) * TT], m.bank[0:EA, 1 + t, :],
                               ACT.Copy).then_inc(gate_hi, 1)

        @block.tensor
        def _(pe):
            pe.wait_ge(split, 2)
            for j in range(NJ):
                for c in range(DC):
                    xh, xl = (v[:, c, j * P:(j + 1) * P] for v in (m.xh, m.xl))
                    mm = split_product(pe, m.bank[:, 0, j * E:(j + 1) * E], xh, xl, wr_hi[:, c, :],
                                       wr_lo[:, c, :], c == 0, c == DC - 1)
            mm.then_inc(logits_done, 1)
            pe.wait_ge(gate_done, 1)
            for j in range(NJ):
                pe.transpose(m.bank[0:EA, 1 + j // 4, (j % 4) * P:(j % 4 + 1) * P], gate[:, j, :],
                             m.ident[:, :]).then_inc(turned, 1)

        @block.vector
        def _(dve):
            n = [0]

            def then(ins):
                n[0] += 1
                ins.then_inc(step, 1)
                dve.wait_ge(step, n[0])

            dve.wait_ge(loaded, 32)
            dve.wait_ge(split, 1)
            dve.scalar_tensor_tensor(wr_lo[:, :, :], wr[:, :, :], WS, wr_hi[:, :, :], ALU.mult,
                                     ALU.subtract).then_inc(split, 1)
            for i in range(4):
                dve.memset(gw[:, :, G + i], -2.0 - i)
            for i in range(2):
                dve.memset(mx[:, :, E + i], -2.0 - i)
            dve.memset(gate[:, :, E:EA], GS)
            dve.wait_ge(logits_done, 1)
            then(dve.scalar_tensor_tensor(
                logit[:, :, :], m.bank[:, 0, :].rearrange("p (j e) -> p j e", e=E), 1.0 / (XS * WS),
                br[:, :].unsqueeze(1).broadcast_to([P, NJ, E]), ALU.mult, ALU.add))
            dve.wait_ge(sig, 1)
            q = s[:, :, :].rearrange("p j (g i) -> p j g i", i=4)
            dve.tensor_tensor(pair[:, 0], q[:, :, :, 0], q[:, :, :, 1], ALU.add)
            dve.tensor_tensor(pair[:, 1], q[:, :, :, 2], q[:, :, :, 3], ALU.add)
            dve.tensor_tensor(pair[:, 2], q[:, :, :, 0], q[:, :, :, 1], ALU.max)
            then(dve.tensor_tensor(pair[:, 3], q[:, :, :, 2], q[:, :, :, 3], ALU.max))
            then(dve.tensor_tensor(pair[:, 0], pair[:, 0], pair[:, 1], ALU.max))
            then(dve.tensor_tensor(pair[:, 2], pair[:, 2], pair[:, 3], ALU.add))
            then(dve.tensor_tensor(gw[:, :, 0:G], pair[:, 0], pair[:, 2], ALU.max))
            for j in range(NJ):
                last = dve.max(top[:, j, :], gw[:, j, :])
            then(last)
            for i in range(4):
                last = dve.memset(top[:, :, KG + i], -2.0 - i)
            then(last)
            for j in range(NJ):
                last = dve.match_replace(gw[:, j, :], top[:, j, :], gw[:, j, :], -9.0)
            then(last)
            then(dve.tensor_scalar(kept[:, :, :], gw[:, :, 0:G], -9.0, None, ALU.is_equal))
            then(dve.tensor_tensor(mx[:, :, 0:E].rearrange("p j (g i) -> p j g i", i=4), q,
                                   kept[:, :, :].unsqueeze(3).broadcast_to([P, NJ, G, 4]), ALU.mult))
            for j in range(NJ):
                last = dve.max(top[:, j, :], mx[:, j, :])
            then(last)
            for i in range(2):
                last = dve.memset(top[:, :, K + i], -2.0 - i)
            then(last)
            for j in range(NJ):
                last = dve.match_replace(mx[:, j, :], top[:, j, :], mx[:, j, :], -9.0)
            then(last)
            then(dve.tensor_scalar(mx[:, :, 0:E], mx[:, :, 0:E], -9.0, None, ALU.is_equal))
            then(dve.tensor_tensor(s[:, :, :], s[:, :, :], mx[:, :, 0:E], ALU.mult))
            then(dve.tensor_reduce(total[:, :], s[:, :, :], AX.X, ALU.add))
            then(dve.tensor_scalar(total[:, :], total[:, :], 1e-20, None, ALU.add))
            then(dve.reciprocal(total[:, :], total[:, :]))
            then(dve.tensor_scalar(total[:, :], total[:, :], SCALE_ROUTE * GS, None, ALU.mult))
            dve.tensor_tensor(gate[:, :, 0:E], s[:, :, :],
                              total[:, :].unsqueeze(2).broadcast_to([P, NJ, E]), ALU.mult).then_inc(gate_done, 1)
            for t in range(NT):
                dve.wait_ge(gate_hi, t + 1)
                dve.tensor_tensor(m.gates[LO:LO + EA, t * TT:(t + 1) * TT], m.bank[0:EA, 1 + t, :],
                                  m.gates[0:EA, t * TT:(t + 1) * TT], ALU.subtract)


def experts(nc, m):
    UNITS = EG * MC
    STEPS = NG * NT
    PIECE = EG * WE // NT
    ctx = ExitStack()
    with ctx:
        sb = lambda name, shape, dt=F32: ctx.enter_context(nc.sbuf_tensor("ex_" + name, shape, dt))
        stage = sb("stage", [P, 2, EG * WE])
        wh = sb("wh", [P, 2, EG * WE], F16)
        wl = sb("wl", [P, 2, EG * WE], F16)
        r = sb("relu", [P, 2, TT])
        g = sb("gate", [P, 2, TT])
        hg = sb("gated", [P, 2, TT])
        hh = sb("hidden_hi", [P, UNITS, TT], F16)
        hl = sb("hidden_lo", [P, UNITS, TT], F16)
        staged = m.sem("ex_staged")
        split_hi = m.sem("ex_split_hi")
        split_lo = m.sem("ex_split_lo")
        gate_bc = m.sem("ex_gate_bc")
        gate_sb = m.sem("ex_gate_sb")
        up_done = m.sem("ex_up_done")
        relu_done = m.sem("ex_relu_done")
        gate_r = m.sem("ex_gate_r")
        gated = m.sem("ex_gated")
        hi_done = m.sem("ex_hi_done")
        lo_done = m.sem("ex_lo_done")
        hl_free = m.sem("ex_hl_free")
        acc_free = m.sem("ex_acc_free")
        H, GB, A = 0, 2, 4

        block = ctx.enter_context(nc.Block())

        @block.sync
        def _(sp):
            for p in range(2):
                sp.dma_start(stage[:, p, :], m.d["WE"][p]).then_inc(staged, 16)
                sp.wait_ge(staged, 16 * p + 16)
            with sp.Fori(2, NG) as p:
                sp.wait_ge(staged, 16 * p)
                sp.wait_ge(split_lo, NT * p - NT)
                sp.wait_ge(split_hi, NT * p - NT)
                sp.dma_start(stage[:, bass.ds(p % 2, 1), :],
                             m.d["WE"][bass.ds(p, 1)].rearrange("a p w -> p a w")).then_inc(staged, 16)
            sp.wait_ge(staged, 16 * NG)

        def piece(buf, n):
            return buf[:, :, :].rearrange("p a w -> p (a w)")[:, bass.ds((n // NT + 1) % 2 * (EG * WE) + n % NT * PIECE, PIECE)]

        def piece0(buf, i):
            return buf[:, 0, i * PIECE:(i + 1) * PIECE]

        @block.scalar
        def _(act):
            act.wait_ge(staged, 16)
            for i in range(NT):
                act.activation(piece0(wh, i), piece0(stage, i), ACT.Copy, scale=WS).then_inc(split_hi, 1)

            def unit(n, u):
                k = n * UNITS + u
                if u % MC == 0:
                    e = u // MC
                    act.wait_ge(gate_bc, n * EG + e + 1)
                    act.activation(g[:, e, :], m.bank[:, GB + e, :], ACT.Copy, scale=HS / GS).then_inc(gate_sb, 1)
                act.wait_ge(up_done, k + 1)
                act.activation(r[:, u % 2, :], m.bank[:, H + u % 2, :], ACT.Relu,
                               scale=1.0 / (XS * WS)).then_inc(relu_done, 1)
                act.wait_ge(hl_free, k + 1)
                act.wait_ge(gated, k + 1)
                act.activation(hh[:, u, :], hg[:, u % 2, :], ACT.Copy).then_inc(hi_done, 1)

            with act.Fori(0, STEPS - NT) as n:
                for u in range(UNITS):
                    unit(n, u)
                act.wait_ge(staged, n // NT * 16 + 32)
                act.activation(piece(wh, n), piece(stage, n), ACT.Copy, scale=WS).then_inc(split_hi, 1)
            with act.Fori(STEPS - NT, STEPS) as n:
                for u in range(UNITS):
                    unit(n, u)

        @block.vector
        def _(dve):
            dve.sem_inc(acc_free, DC)
            for i in range(NT):
                dve.wait_ge(split_hi, i + 1)
                dve.scalar_tensor_tensor(piece0(wl, i), piece0(stage, i), WS, piece0(wh, i), ALU.mult,
                                         ALU.subtract).then_inc(split_lo, 1)

            def unit(n, u):
                k = n * UNITS + u
                dve.wait_ge(relu_done, k + 1)
                dve.wait_ge(gate_sb, n * EG + u // MC + 1)
                dve.tensor_tensor(hg[:, u % 2, :], r[:, u % 2, :], g[:, u // MC, :], ALU.mult).then_inc(gate_r, 1)
                dve.wait_ge(gate_r, k + 1)
                dve.tensor_tensor(hg[:, u % 2, :], hg[:, u % 2, :], r[:, u % 2, :], ALU.mult).then_inc(gated, 1)
                dve.wait_ge(hi_done, k + 1)
                dve.tensor_tensor(hl[:, u, :], hg[:, u % 2, :], hh[:, u, :], ALU.subtract).then_inc(lo_done, 1)

            def split(n):
                dve.wait_ge(split_hi, n + NT + 1)
                dve.scalar_tensor_tensor(piece(wl, n), piece(stage, n), WS, piece(wh, n), ALU.mult,
                                         ALU.subtract).then_inc(split_lo, 1)

            def add_sums(n, tile):
                dve.wait_ge(hl_free, n * UNITS + 2 * UNITS)
                for c in range(DC):
                    acc = m.acc[:, c, bass.ds(tile * TT, TT)]
                    dve.scalar_tensor_tensor(acc, m.bank[:, A + c, :], 1.0 / (WS * HS), acc, ALU.mult,
                                             ALU.add).then_inc(acc_free, 1)

            unit(0, 0)
            unit(0, 1)
            with dve.Fori(0, STEPS - NT) as n:
                unit(n, 2)
                unit(n, 3)
                split(n)
                unit(n + 1, 0)
                unit(n + 1, 1)
                add_sums(n, n % NT)
            with dve.Fori(STEPS - NT, STEPS - 1) as n:
                unit(n, 2)
                unit(n, 3)
                unit(n + 1, 0)
                unit(n + 1, 1)
                add_sums(n, n % NT)
            unit(STEPS - 1, 2)
            unit(STEPS - 1, 3)
            add_sums(STEPS - 1, NT - 1)

        @block.tensor
        def _(pe):
            pe.sem_inc(hl_free, UNITS)

            def weights(buf, n, at, width):
                if isinstance(n, int):
                    return buf[:, n // NT % 2, at:at + width]
                return buf[:, :, :].rearrange("p a w -> p (a w)")[:, bass.ds(n // NT % 2 * (EG * WE) + at, width)]

            def up(n, u, first=False):
                e, c = u // MC, u % MC
                if not first:
                    pe.wait_ge(relu_done, n * UNITS + u - 1)
                if u == 0:
                    pe.wait_ge(split_lo, n // NT * NT + NT)
                tile = n % NT
                tok = bass.ds(tile * TT, TT)
                if c == 0:
                    sel = m.sel[:, bass.ds((n // NT * EG + e) * P, P)]
                    pe.matmul(m.bank[:, GB + e, :], sel, m.gates[:, tok], start=True, stop=True).then_inc(gate_bc, 1)
                for k in range(DC):
                    at = e * WE + k * M + c * P
                    mm = split_product(pe, m.bank[:, H + u % 2, :], weights(wh, n, at, P), weights(wl, n, at, P),
                                       m.xh[:, k, tok], m.xl[:, k, tok], k == 0, k == DC - 1)
                mm.then_inc(up_done, 1)

            def down(n, u):
                e, c = u // MC, u % MC
                pe.wait_ge(lo_done, n * UNITS + u + 1)
                for d in range(DC):
                    if u == 0:
                        pe.wait_ge(acc_free, n * DC + d + 1)
                    at = e * WE + DC * M + c * D + d * P
                    mm = split_product(pe, m.bank[:, A + d, :], weights(wh, n, at, P), weights(wl, n, at, P),
                                       hh[:, u, :], hl[:, u, :], u == 0, u == UNITS - 1)
                mm.then_inc(hl_free, 1)

            up(0, 0, first=True)
            up(0, 1, first=True)
            with pe.Fori(0, STEPS - 1) as n:
                up(n, 2)
                down(n, 0)
                up(n, 3)
                down(n, 1)
                up(n + 1, 0)
                down(n, 2)
                up(n + 1, 1)
                down(n, 3)
            n = STEPS - 1
            up(n, 2)
            down(n, 0)
            up(n, 3)
            down(n, 1)
            down(n, 2)
            down(n, 3)

H0, DK, CHUNK = 16, 32, 64
HALF = DK // 2
HG = P // DK
NB = T // P
TB = T // TT
AS = 4.0


def linear_attention(nc, m):
    ctx = ExitStack()
    with ctx:
        sb = lambda name, shape, dt=F32: ctx.enter_context(nc.sbuf_tensor("la_" + name, shape, dt))
        names = ["q", "k", "v", "g", "o"]
        wstage = sb("wstage", [P, DC, D])
        w_hi = sb("w_hi", [P, 5, DC, D], F16)
        w_lo = sb("w_lo", [P, 5, DC, D], F16)
        rows = sb("rows", [P, 3, D])
        cols = sb("cols", [P, 2, DC])
        cos = sb("cos", [P, NB, HALF])
        sin = sb("sin", [P, NB, 2, HALF])
        mask = sb("mask", [P, P])
        ones = sb("ones", [P, DK])
        a = sb("a", [P, 2, D])
        t1 = sb("t1", [P, 2, D])
        t2 = sb("t2", [P, 2, D])
        f = sb("f", [P, 2, 2, D])
        v = sb("v", [P, 2, D])
        qT = sb("qT", [P, DC, P])
        S = sb("S", [P, 2, 2, DC, P])
        ao = sb("ao", [P, 2, DC, P])
        aoh = sb("aoh", [P, DC, TT], F16)
        aol = sb("aol", [P, DC, TT], F16)
        gT = sb("gT", [P, DC, TT])
        sig = t2
        s = t1

        loaded, w_loaded = m.sem("la_loaded"), m.sem("la_w_loaded")
        whi, wlo = m.sem("la_whi"), m.sem("la_wlo")
        ones_set = m.sem("la_ones")
        g_mm, g_sig = m.sem("la_g_mm"), m.sem("la_g_sig")
        proj_qk, proj_v = m.sem("la_proj_qk"), m.sem("la_proj_v")
        qk_biased, v_biased = m.sem("la_qk_biased"), m.sem("la_v_biased")
        cos_done, sin_done, turned = m.sem("la_cos_done"), m.sem("la_sin_done"), m.sem("la_turned")
        min_done, exp_done, mapped = m.sem("la_min_done"), m.sem("la_exp_done"), m.sem("la_mapped")
        qT_mm, qT_sb = m.sem("la_qT_mm"), m.sem("la_qT_sb")
        kv_done, state_set, num_done = m.sem("la_kv_done"), m.sem("la_state_set"), m.sem("la_num_done")
        den_eps, den_inv, divided, gated = (m.sem("la_" + n) for n in ("den_eps", "den_inv", "divided", "gated"))
        ao_hi, ao_lo = m.sem("la_ao_hi"), m.sem("la_ao_lo")
        gact_sig, gact_done = m.sem("la_gact_sig"), m.sem("la_gact_done")
        o_mm, o_biased, o_gated, x_added = (m.sem("la_" + n) for n in ("o_mm", "o_biased", "o_gated", "x_added"))
        Q, V, NUM, DEN, QT, KV, Z = 0, 2, 3, 4, 5, 6, 7
        LOADS = 3 + 1 + 1 + 2 + 1
        block = ctx.enter_context(nc.Block())

        @block.sync
        def _(sp):
            for i, w in enumerate((m.d["q0"], m.d["k0"], m.d["v0"], m.d["g0"], m.d["o0"])):
                if i:
                    sp.wait_ge(whi, i)
                    sp.wait_ge(wlo, i)
                sp.dma_start(wstage[:, :, :], w.rearrange("(c p) n -> p c n", p=P)).then_inc(w_loaded, 16)
                if i == 0:
                    for j, bias in enumerate((m.d["qb"], m.d["kb"], m.d["vb"])):
                        sp.dma_start(rows[:, j, :], bias.partition_broadcast(P)).then_inc(loaded, 16)
                    sp.dma_start(cols[:, 0, :], m.d["gbT"]).then_inc(loaded, 16)
                    sp.dma_start(cols[:, 1, :], m.d["obT"]).then_inc(loaded, 16)
                    sp.dma_start(cos[:, :, :], m.d["cos0"]).then_inc(loaded, 16)
                    sp.dma_start(sin[:, :, :, :], m.d["sin0"]).then_inc(loaded, 16)
                    sp.dma_start(mask[:, :], m.d["block_mask"]).then_inc(loaded, 16)
                sp.wait_ge(w_loaded, 16 * i + 16)

        @block.gpsimd
        def _(pool):
            pool.memset(ones[:, :], 1.0).then_inc(ones_set, 1)
            pool.wait_ge(loaded, 16 * LOADS)
            with pool.Fori(0, B) as b:
                def sines(j):
                    pool.wait_ge(qk_biased, b * NB + j + 1)
                    heads = a[:, :, :].rearrange("p a (h r i) -> p (a h) r i", r=2, i=HALF)
                    out = t2[:, :, :].rearrange("p a (h r i) -> p (a h) r i", r=2, i=HALF)
                    for r in range(2):
                        sn = sin[:, j, r, :].unsqueeze(1).broadcast_to([P, 2 * H0, HALF])
                        ins = pool.tensor_tensor(out[:, :, r, :], heads[:, :, 1 - r, :], sn, ALU.mult)
                    ins.then_inc(sin_done, 1)

                def low(j):
                    pool.wait_ge(ao_hi, b * NB + j + 1)
                    at = (j % (NB // TB)) * P
                    pool.tensor_tensor(aol[:, :, at:at + P], ao[:, j % 2], aoh[:, :, at:at + P],
                                       ALU.subtract).then_inc(ao_lo, 1)

                for j in range(NB):
                    if j % (NB // TB) == 0:
                        i = b * TB + j // (NB // TB)
                        for c in range(DC):
                            pool.wait_ge(gact_sig, i * DC + c + 1)
                            acc = m.acc[:, c, bass.ds(i * TT, TT)]
                            pool.tensor_tensor(acc, acc, sig[:, c % 2, :], ALU.mult).then_inc(gact_done, 1)
                        pool.wait_ge(gact_done, i * DC + DC)
                    sines(j)
                    if j % (NB // TB):
                        low(j - 1)
                    if j % (NB // TB) == NB // TB - 1:
                        low(j)

        @block.scalar
        def _(act):
            for i in range(5):
                act.wait_ge(w_loaded, 16 * i + 16)
                act.activation(w_hi[:, i], wstage[:, :, :], ACT.Copy, scale=WS).then_inc(whi, 1)
            act.wait_ge(loaded, 16 * LOADS)
            with act.Fori(0, B) as b:
                def exps(j):
                    act.wait_ge(min_done, b * NB + j + 1)
                    act.activation(t2[:, :, :], t1[:, :, :], ACT.Exp).then_inc(exp_done, 1)

                def high(j):
                    act.wait_ge(gated, b * NB + j + 1)
                    at = (j % (NB // TB)) * P
                    act.activation(aoh[:, :, at:at + P], ao[:, j % 2], ACT.Copy).then_inc(ao_hi, 1)

                for j in range(NB):
                    if j % (NB // TB) == 0:
                        i = b * TB + j // (NB // TB)
                        for c in range(DC):
                            if c >= 2:
                                act.wait_ge(gact_done, i * DC + c - 1)
                            act.activation(sig[:, c % 2, :], m.acc[:, c, bass.ds(i * TT, TT)],
                                           ACT.Sigmoid).then_inc(gact_sig, 1)
                        for c in range(DC):
                            act.wait_ge(g_mm, i * DC + c + 1)
                            act.activation(gT[:, c, :], m.bank[:, c % 2, :], ACT.Sigmoid, bias=cols[:, 0, c:c + 1],
                                           scale=1.0 / (XS * WS)).then_inc(g_sig, 1)
                        exps(j)
                    act.wait_ge(qT_mm, b * NB + j + 1)
                    act.activation(qT[:, :, :], m.bank[:, QT, :].rearrange("p (c t) -> p c t", c=DC),
                                   ACT.Copy).then_inc(qT_sb, 1)
                    if j + 1 < NB and (j + 1) % (NB // TB):
                        exps(j + 1)
                    high(j)
                    if j % (NB // TB) == NB // TB - 1:
                        i = b * TB + j // (NB // TB)
                        for c in range(DC):
                            act.wait_ge(o_mm, i * DC + c + 1)
                            if c >= 2:
                                act.wait_ge(x_added, i * DC + c - 1)
                            act.activation(s[:, c % 2, :], m.bank[:, c % 2, :], ACT.Identity, bias=cols[:, 1, c:c + 1],
                                           scale=1.0 / (AS * WS)).then_inc(o_biased, 1)

        @block.vector
        def _(dve):
            for i in range(5):
                dve.wait_ge(whi, i + 1)
                dve.scalar_tensor_tensor(w_lo[:, i], wstage[:, :, :], WS, w_hi[:, i], ALU.mult,
                                         ALU.subtract).then_inc(wlo, 1)
            dve.wait_ge(loaded, 16 * LOADS)
            with dve.Fori(0, B) as b:
                at = lambda j: b * NB + j + 1

                def front1(j):
                    dve.wait_ge(proj_qk, at(j))
                    if j:
                        dve.wait_ge(mapped, at(j - 1))
                    dve.scalar_tensor_tensor(a[:, :, :], m.bank[:, Q:Q + 2, :], 1.0 / (XS * WS), rows[:, 0:2, :],
                                             ALU.mult, ALU.add).then_inc(qk_biased, 1)
                    dve.wait_ge(proj_v, at(j))
                    dve.scalar_tensor_tensor(v[:, j % 2, :], m.bank[:, V, :], 1.0 / (XS * WS), rows[:, 2, :],
                                             ALU.mult, ALU.add).then_inc(v_biased, 1)
                    dve.wait_ge(qk_biased, at(j))
                    cs = cos[:, j, :].unsqueeze(1).broadcast_to([P, 4 * H0, HALF])
                    dve.tensor_tensor(t1[:, :, :].rearrange("p a (h i) -> p (a h) i", i=HALF),
                                      a[:, :, :].rearrange("p a (h i) -> p (a h) i", i=HALF), cs,
                                      ALU.mult).then_inc(cos_done, 1)

                def front2(j):
                    dve.wait_ge(cos_done, at(j))
                    dve.wait_ge(sin_done, at(j))
                    dve.tensor_tensor(a[:, :, :], t1[:, :, :], t2[:, :, :], ALU.add).then_inc(turned, 1)
                    dve.wait_ge(turned, at(j))
                    dve.tensor_scalar(t1[:, :, :], a[:, :, :], 0.0, None, ALU.min).then_inc(min_done, 1)

                def front3(j):
                    dve.wait_ge(exp_done, at(j))
                    dve.scalar_tensor_tensor(f[:, j % 2], a[:, :, :], 0.0, t2[:, :, :], ALU.max,
                                             ALU.add).then_inc(mapped, 1)

                def state(j, h):
                    n = 2 * j + h
                    dve.wait_ge(kv_done, b * 2 * NB + n + 1)
                    mk = mask[:, :].unsqueeze(1).broadcast_to([P, DC, P])
                    dve.tensor_tensor(S[:, h, 0], m.bank[:, KV, :].rearrange("p (c e) -> p c e", c=DC), mk, ALU.mult)
                    for c in range(DC):
                        z = m.bank[:, Z, c * DK:(c + 1) * DK].unsqueeze(1).broadcast_to([P, HG, DK])
                        ins = dve.tensor_tensor(S[:, h, 1, c].rearrange("p (h e) -> p h e", e=DK), z,
                                                mask[:, :].rearrange("p (h e) -> p h e", e=DK), ALU.mult)
                    ins.then_inc(state_set, 1)

                def out1(j):
                    dve.wait_ge(num_done, b * 2 * NB + 2 * j + 2)
                    dve.tensor_scalar(ao[:, j % 2], m.bank[:, DEN, :].rearrange("p (c t) -> p c t", c=DC), 1e-6, None,
                                      ALU.add).then_inc(den_eps, 1)
                    dve.wait_ge(den_eps, at(j))
                    dve.reciprocal(ao[:, j % 2], ao[:, j % 2]).then_inc(den_inv, 1)

                def out2(j):
                    dve.wait_ge(den_inv, at(j))
                    dve.scalar_tensor_tensor(ao[:, j % 2], m.bank[:, NUM, :].rearrange("p (c t) -> p c t", c=DC), AS,
                                             ao[:, j % 2], ALU.mult, ALU.mult).then_inc(divided, 1)
                    dve.wait_ge(divided, at(j))
                    i = (j % (NB // TB)) * P
                    dve.tensor_tensor(ao[:, j % 2], ao[:, j % 2], gT[:, :, i:i + P], ALU.mult).then_inc(gated, 1)

                for t in range(TB):
                    j0 = t * (NB // TB)
                    front1(j0)
                    front2(j0)
                    front3(j0)
                    for j in range(j0, j0 + NB // TB):
                        state(j, 0)
                        state(j, 1)
                        more = j + 1 < j0 + NB // TB
                        if more:
                            front1(j + 1)
                        out1(j)
                        if more:
                            front2(j + 1)
                        out2(j)
                        if more:
                            front3(j + 1)
                    i = b * TB + t
                    for c in range(DC):
                        dve.wait_ge(o_biased, i * DC + c + 1)
                        dve.tensor_tensor(s[:, c % 2, :], s[:, c % 2, :], m.acc[:, c, bass.ds(i * TT, TT)], ALU.mult).then_inc(o_gated, 1)
                        dve.wait_ge(o_gated, i * DC + c + 1)
                        xs = m.x[:, c, bass.ds(i * TT, TT)]
                        dve.tensor_tensor(xs, xs, s[:, c % 2, :], ALU.add).then_inc(x_added, 1)
                    dve.wait_ge(x_added, i * DC + DC)

        @block.tensor
        def _(pe):
            pe.wait_ge(ones_set, 1)
            pe.wait_ge(wlo, 5)
            with pe.Fori(0, B) as b:
                at = lambda j: b * NB + j + 1

                def project(j):
                    tok = bass.ds((b * NB + j) * P, P)
                    for w in range(3):
                        if w == 0 and j % (NB // TB):
                            pe.wait_ge(qk_biased, at(j - 1))
                        if w == 2 and j % (NB // TB):
                            pe.wait_ge(v_biased, at(j - 1))
                        for c in range(DC):
                            mm = split_product(pe, m.bank[:, Q + w, :], m.xh[:, c, tok], m.xl[:, c, tok],
                                               w_hi[:, w, c, :], w_lo[:, w, c, :], c == 0, c == DC - 1)
                        if w:
                            mm.then_inc(proj_qk if w == 1 else proj_v, 1)

                for t in range(TB):
                    j0 = t * (NB // TB)
                    i = b * TB + t
                    tok = bass.ds(i * TT, TT)
                    for c in range(DC):
                        if c >= 2:
                            pe.wait_ge(g_sig, i * DC + c - 1)
                        for k in range(DC):
                            mm = split_product(pe, m.bank[:, c % 2, :], w_hi[:, 3, k, c * P:(c + 1) * P],
                                               w_lo[:, 3, k, c * P:(c + 1) * P], m.xh[:, k, tok], m.xl[:, k, tok],
                                               k == 0, k == DC - 1)
                        mm.then_inc(g_mm, 1)
                    pe.wait_ge(g_sig, i * DC + DC)
                    project(j0)
                    for j in range(j0, j0 + NB // TB):
                        if j + 1 < j0 + NB // TB:
                            project(j + 1)
                        pe.wait_ge(mapped, at(j))
                        if j:
                            pe.wait_ge(qT_sb, at(j - 1))
                        for c in range(DC):
                            mm = pe.transpose(m.bank[:, QT, c * P:(c + 1) * P], f[:, j % 2, 0, c * P:(c + 1) * P],
                                              m.ident[:, :])
                        mm.then_inc(qT_mm, 1)

                        def outer(h):
                            n = 2 * j + h
                            if n:
                                pe.wait_ge(state_set, b * 2 * NB + n)
                            lo, hi = h * CHUNK, (h + 1) * CHUNK
                            for c in range(DC):
                                kk = f[lo:hi, j % 2, 1, c * P:(c + 1) * P]
                                pe.matmul(m.bank[:, KV, c * P:(c + 1) * P], kk, v[lo:hi, j % 2, c * P:(c + 1) * P],
                                          start=(n == 0 and c == 0), stop=True, skip_group_check=True)
                                mm = pe.matmul(m.bank[:, Z, c * DK:(c + 1) * DK], kk, ones[lo:hi, :],
                                               start=(n == 0 and c == 0), stop=True, skip_group_check=True)
                            mm.then_inc(kv_done, 1)

                        def outputs(h):
                            pe.wait_ge(state_set, b * 2 * NB + 2 * j + h + 1)
                            for c in range(DC):
                                q = qT[:, c, h * CHUNK:(h + 1) * CHUNK]
                                for z, bank in ((0, NUM), (1, DEN)):
                                    o = c * P + h * CHUNK
                                    mm = pe.matmul(m.bank[:, bank, o:o + CHUNK], S[:, h, z, c, :], q, start=True,
                                                   stop=True)
                            mm.then_inc(num_done, 1)

                        pe.wait_ge(v_biased, at(j))
                        outer(0)
                        pe.wait_ge(qT_sb, at(j))
                        outer(1)
                        if j:
                            pe.wait_ge(divided, at(j - 1))
                        outputs(0)
                        outputs(1)
                    pe.wait_ge(ao_lo, at(j0 + NB // TB - 1))
                    for c in range(DC):
                        if c >= 2:
                            pe.wait_ge(o_biased, i * DC + c - 1)
                        for k in range(DC):
                            mm = split_product(pe, m.bank[:, c % 2, :], w_hi[:, 4, k, c * P:(c + 1) * P],
                                               w_lo[:, 4, k, c * P:(c + 1) * P], aoh[:, k, :], aol[:, k, :],
                                               k == 0, k == DC - 1)
                        mm.then_inc(o_mm, 1)
                    pe.wait_ge(o_biased, i * DC + DC)

F = 2048
FC = F // P
TERNARY = 0.7
H1, HKV, HD = 32, 8, 16
REP = H1 // HKV
HH = HD // 2
QS = 16.0
YS = 16.0
STACK = 3 * HD
FAR = 60000.0


def ternary_ffn(nc, m):
    ctx = ExitStack()
    with ctx:
        sb = lambda name, shape, dt=F32: ctx.enter_context(nc.sbuf_tensor("tf_" + name, shape, dt))
        W = DC * F
        stage = sb("stage", [P, W])
        w1 = sb("w1", [P, DC, F], F16)
        w2 = sb("w2", [P, FC, D], F16)
        b1 = sb("b1", [P, FC])
        b2 = sb("b2", [P, DC])
        part = sb("part", [P, W // P])
        whole = sb("whole", [P, 2])
        thr = sb("thr", [P, 2, 2])
        h = sb("h", [P, 2, TT])
        hh = sb("hh", [P, 4, TT], F16)
        hl = sb("hl", [P, 4, TT], F16)
        loaded, staged = m.sem("tf_loaded"), m.sem("tf_staged")
        summed, total = m.sem("tf_summed"), m.sem("tf_total")
        step, ternary = m.sem("tf_step"), m.sem("tf_ternary")
        up_done, gelu_done, hi_done, lo_done = (m.sem("tf_" + n) for n in ("up_done", "gelu_done", "hi_done", "lo_done"))
        down_done, sig_done, out_done = (m.sem("tf_" + n) for n in ("down_done", "sig_done", "out_done"))
        block = ctx.enter_context(nc.Block())

        @block.sync
        def _(sp):
            sp.dma_start(b1[:, :], m.d["b1T"]).then_inc(loaded, 16)
            sp.dma_start(b2[:, :], m.d["b2T"]).then_inc(loaded, 16)
            sp.dma_start(stage[:, :].rearrange("p (c f) -> p c f", f=F),
                         m.d["w1T"].rearrange("(c p) f -> p c f", p=P)).then_inc(staged, 16)
            sp.wait_ge(ternary, 1)
            sp.dma_start(stage[:, :].rearrange("p (c d) -> p c d", d=D),
                         m.d["w2T"].rearrange("(c p) d -> p c d", p=P)).then_inc(staged, 16)

        @block.scalar
        def _(act):
            act.wait_ge(loaded, 32)
            with act.Fori(0, NT) as t:
                for f in range(FC):
                    k = t * FC + f
                    act.wait_ge(up_done, k + 1)
                    if f >= 2:
                        act.wait_ge(lo_done, k - 1)
                    act.activation(h[:, f % 2, :], m.bank[:, f % 2, :], ACT.Gelu, bias=b1[:, f:f + 1],
                                   scale=1.0 / XS).then_inc(gelu_done, 1)
                    if f >= 4:
                        act.wait_ge(down_done, k - 3)
                    act.wait_ge(gelu_done, k + 1)
                    act.activation(hh[:, f % 4, :], h[:, f % 2, :], ACT.Copy).then_inc(hi_done, 1)
                act.wait_ge(down_done, t * FC + FC)
                act.wait_ge(lo_done, t * FC + FC)
                for d in range(DC):
                    if d >= 2:
                        act.wait_ge(out_done, t * DC + d - 1)
                    act.activation(h[:, d % 2, :], m.bank[:, 4 + d, :], ACT.Sigmoid,
                                   bias=b2[:, d:d + 1]).then_inc(sig_done, 1)
                act.wait_ge(out_done, t * DC + DC)

        @block.vector
        def _(dve):
            dve.wait_ge(loaded, 32)
            n = 0
            for i, q in enumerate((w1, w2)):
                dve.wait_ge(staged, 16 * i + 16)
                dve.tensor_reduce(part[:, :], stage[:, :].rearrange("p (a b) -> p a b", b=P), AX.X, ALU.add,
                                  apply_absolute_value=True).then_inc(step, 1)
                n += 1
                dve.wait_ge(step, n)
                dve.tensor_reduce(whole[:, i:i + 1], part[:, :], AX.X, ALU.add).then_inc(summed, 1)
                dve.wait_ge(total, i + 1)
                dve.tensor_scalar(thr[:, i, 0:1], m.bank[:, 0, 0:1], D / (F * D), TERNARY, ALU.mult,
                                  ALU.mult).then_inc(step, 1)
                n += 1
                dve.wait_ge(step, n)
                dve.tensor_scalar(thr[:, i, 1:2], thr[:, i, 0:1], -1.0, None, ALU.mult).then_inc(step, 1)
                n += 1
                dve.wait_ge(step, n)
                flat = q[:, :, :].rearrange("p a b -> p (a b)")
                dve.tensor_scalar(flat, stage[:, :], thr[:, i, 1:2], None, ALU.is_le).then_inc(step, 1)
                n += 1
                dve.wait_ge(step, n)
                dve.scalar_tensor_tensor(flat, stage[:, :], thr[:, i, 0:1], flat, ALU.is_ge,
                                         ALU.subtract).then_inc(ternary, 1)
            with dve.Fori(0, NT) as t:
                for f in range(FC):
                    k = t * FC + f
                    dve.wait_ge(hi_done, k + 1)
                    dve.tensor_tensor(hl[:, f % 4, :], h[:, f % 2, :], hh[:, f % 4, :], ALU.subtract).then_inc(lo_done, 1)
                for d in range(DC):
                    dve.wait_ge(sig_done, t * DC + d + 1)
                    dve.scalar_tensor_tensor(m.acc[:, d, bass.ds(t * TT, TT)], m.bank[:, 4 + d, :], b2[:, d:d + 1],
                                             h[:, d % 2, :], ALU.add, ALU.mult).then_inc(out_done, 1)

        @block.tensor
        def _(pe):
            for i in range(2):
                pe.wait_ge(summed, i + 1)
                pe.matmul(m.bank[:, 0, 0:1], m.mean_ones[:, :], whole[:, i:i + 1], start=True,
                          stop=True).then_inc(total, 1)
            pe.wait_ge(ternary, 2)
            with pe.Fori(0, NT) as t:
                def up(f):
                    k = t * FC + f
                    if f >= 2:
                        pe.wait_ge(gelu_done, k - 1)
                    tok = bass.ds(t * TT, TT)
                    for c in range(DC):
                        w = w1[:, c, f * P:(f + 1) * P]
                        pe.matmul(m.bank[:, f % 2, :], w, m.xh[:, c, tok], start=(c == 0), stop=False)
                        mm = pe.matmul(m.bank[:, f % 2, :], w, m.xl[:, c, tok], start=False, stop=(c == DC - 1))
                    mm.then_inc(up_done, 1)

                def down(f):
                    k = t * FC + f
                    pe.wait_ge(lo_done, k + 1)
                    for d in range(DC):
                        w = w2[:, f, d * P:(d + 1) * P]
                        pe.matmul(m.bank[:, 4 + d, :], w, hh[:, f % 4, :], start=(f == 0), stop=False)
                        mm = pe.matmul(m.bank[:, 4 + d, :], w, hl[:, f % 4, :], start=False, stop=(f == FC - 1))
                    mm.then_inc(down_done, 1)

                up(0)
                up(1)
                for f in range(FC):
                    if f + 2 < FC:
                        up(f + 2)
                    down(f)
                pe.wait_ge(out_done, t * DC + DC)


def project_qkv(nc, m):
    ctx = ExitStack()
    with ctx:
        sb = lambda name, shape, dt=F32: ctx.enter_context(nc.sbuf_tensor("pj_" + name, shape, dt))
        WN = D + 2 * HKV * HD
        stage = sb("stage", [P, DC, WN])
        w_hi = sb("w_hi", [P, DC, WN], F16)
        w_lo = sb("w_lo", [P, DC, WN], F16)
        cos = sb("cos", [P, T])
        sin = sb("sin", [P, T])
        t1 = sb("t1", [P, 2, 4, TT])
        ev = sb("ev", [P, 2, 2, TT])
        pr = sb("pr", [P, 2, 2, 2, TT], F16)
        v = sb("v", [P, 2, 4, P])
        loaded, whi, wlo = m.sem("pj_loaded"), m.sem("pj_whi"), m.sem("pj_wlo")
        proj, mults, turned, hi_done, lo_done = (m.sem("pj_" + n) for n in ("proj", "mults", "turned", "hi_done", "lo_done"))
        stored = [m.sem("pj_stored0"), m.sem("pj_stored1")]
        v_mm, v_sb, v_stored = m.sem("pj_v_mm"), m.sem("pj_v_sb"), m.sem("pj_v_stored")
        UN = NT * 3
        units = [(t, w) for t in range(NT) for w in range(3)]
        block = ctx.enter_context(nc.Block())

        @block.sync
        def _(sp):
            sp.dma_start(stage[:, :, :], m.d["wqkvT"].rearrange("(c p) n -> p c n", p=P)).then_inc(loaded, 16)
            sp.dma_start(cos[:, :], m.d["cos1"]).then_inc(loaded, 16)
            sp.dma_start(sin[:, :], m.d["sin1"]).then_inc(loaded, 16)
            for n, (t, w) in enumerate(units):
                sp.wait_ge(lo_done, n + 1)
                rows = P if w < 2 else P // 2
                dst = (m.q_dram[w] if w < 2 else m.k_dram)[:, :, :, t * TT:(t + 1) * TT]
                sp.dma_start(dst.rearrange("a b p n -> p a b n"), pr[0:rows, n % 2]).then_inc(stored[n % 2], 16)
                if w == 2:
                    sp.wait_ge(v_sb, t + 1)
                    sp.dma_start(m.v_dram[t * 4:(t + 1) * 4].rearrange("j p e -> p j e"), v[:, t % 2]).then_inc(v_stored, 16)
                    sp.wait_ge(v_stored, 16 * t + 16)
            for s in stored:
                sp.wait_ge(s, UN // 2 * 16)

        @block.scalar
        def _(act):
            act.wait_ge(loaded, 48)
            act.activation(w_hi[:, :, :], stage[:, :, :], ACT.Copy, scale=WS).then_inc(whi, 1)
            for n, (t, w) in enumerate(units):
                rows = P if w < 2 else P // 2
                act.wait_ge(turned, n + 1)
                if n >= 2:
                    act.wait_ge(stored[n % 2], n // 2 * 16)
                act.activation(pr[0:rows, n % 2, 0], ev[0:rows, n % 2], ACT.Copy).then_inc(hi_done, 1)
                if w == 2:
                    act.wait_ge(v_mm, t + 1)
                    if t >= 2:
                        act.wait_ge(v_stored, 16 * (t - 1))
                    act.activation(v[:, t % 2], m.bank[:, 6 + t % 2, :].rearrange("p (j e) -> p j e", e=P), ACT.Copy,
                                   scale=1.0 / (XS * WS)).then_inc(v_sb, 1)

        @block.vector
        def _(dve):
            dve.wait_ge(whi, 1)
            dve.scalar_tensor_tensor(w_lo[:, :, :], stage[:, :, :], WS, w_hi[:, :, :], ALU.mult,
                                     ALU.subtract).then_inc(wlo, 1)
            for n, (t, w) in enumerate(units):
                rows, b = P if w < 2 else P // 2, n % 2
                dve.wait_ge(proj, n + 1)
                cs = cos[0:rows, (t % TB) * TT:(t % TB + 1) * TT]
                sn = sin[0:rows, (t % TB) * TT:(t % TB + 1) * TT]
                ev_, od = (m.bank[0:rows, 2 * b + i, :] for i in range(2))
                for i, (x, y) in enumerate(((ev_, cs), (od, sn), (ev_, sn), (od, cs))):
                    ins = dve.tensor_tensor(t1[0:rows, b, i, :], x, y, ALU.mult)
                ins.then_inc(mults, 1)
                dve.wait_ge(mults, n + 1)
                if n >= 2:
                    dve.wait_ge(lo_done, n - 1)
                dve.tensor_tensor(ev[0:rows, b, 0, :], t1[0:rows, b, 0, :], t1[0:rows, b, 1, :], ALU.subtract)
                dve.tensor_tensor(ev[0:rows, b, 1, :], t1[0:rows, b, 2, :], t1[0:rows, b, 3, :],
                                  ALU.add).then_inc(turned, 1)

        @block.gpsimd
        def _(pool):
            for n, (t, w) in enumerate(units):
                rows, b = P if w < 2 else P // 2, n % 2
                pool.wait_ge(hi_done, n + 1)
                pool.tensor_tensor(pr[0:rows, b, 1], ev[0:rows, b], pr[0:rows, b, 0], ALU.subtract).then_inc(lo_done, 1)

        @block.tensor
        def _(pe):
            pe.wait_ge(wlo, 1)
            for n, (t, w) in enumerate(units):
                rows = P if w < 2 else P // 2
                if n >= 2:
                    pe.wait_ge(mults, n - 1)
                at = 2 * P * w
                for i in range(2):
                    for c in range(DC):
                        ws = slice(at + i * rows, at + (i + 1) * rows)
                        mm = split_product(pe, m.bank[0:rows, 2 * (n % 2) + i, :], w_hi[:, c, ws], w_lo[:, c, ws],
                                           m.xh[:, c, t * TT:(t + 1) * TT], m.xl[:, c, t * TT:(t + 1) * TT],
                                           c == 0, c == DC - 1)
                mm.then_inc(proj, 1)
                if w == 2:
                    if t >= 2:
                        pe.wait_ge(v_sb, t - 1)
                    for j in range(4):
                        tok = slice(t * TT + j * P, t * TT + (j + 1) * P)
                        for c in range(DC):
                            ws = slice(D + HKV * HD, WN)
                            mm = split_product(pe, m.bank[:, 6 + t % 2, j * P:(j + 1) * P], m.xh[:, c, tok], m.xl[:, c, tok],
                                               w_hi[:, c, ws], w_lo[:, c, ws], c == 0, c == DC - 1)
                    mm.then_inc(v_mm, 1)


def softmax_attention(nc, m):
    ctx = ExitStack()
    with ctx:
        sb = lambda name, shape, dt=F32: ctx.enter_context(nc.sbuf_tensor("sa_" + name, shape, dt))
        qs = sb("qs", [P, H1, T], F16)
        ks = sb("ks", [P, HKV, T], F16)
        va = sb("va", [P, NB, HKV, HD + 1])
        pexp = sb("pexp", [P, 3, T])
        mx = sb("mx", [P, NB, H1])
        mh = sb("mh", [H1, 2, T], F16)
        far = sb("far", [P, 3, P], F16)
        rec = sb("rec", [P, 2, NB])
        memsets, ones_set = m.sem("sa_memsets"), m.sem("sa_ones_set")
        loaded, mask_loaded = m.sem("sa_loaded"), m.sem("sa_mask_loaded")
        sc_done, max_done = m.sem("sa_sc_done"), m.sem("sa_max_done")
        turned, mhi, mlo = m.sem("sa_turned"), m.sem("sa_mhi"), m.sem("sa_mlo")
        m_stored, m_loaded = m.sem("sa_m_stored"), m.sem("sa_m_loaded")
        st_done, exp_done, pv_done = m.sem("sa_st_done"), m.sem("sa_exp_done"), m.sem("sa_pv_done")
        rec_done, y_done = m.sem("sa_rec_done"), m.sem("sa_y_done")
        QLOADS = 12 + 6 + NB
        U1 = HKV * REP * NB
        block = ctx.enter_context(nc.Block())

        @block.sync
        def _(sp):
            sp.dma_start(far[:, :, :], m.d["far"]).then_inc(mask_loaded, 16)
            sp.wait_ge(memsets, 4)
            sp.wait_ge(ones_set, 2)
            for b in range(B):
                if b:
                    sp.wait_ge(y_done, H1 * b)
                tok = slice(b * T, (b + 1) * T)
                for slot, (qp, kp) in enumerate(((0, 0), (1, 0), (0, 1))):
                    for i in range(2):
                        at = slot * HD + i * HH
                        for a in range(2):
                            sp.dma_start(qs[at:at + HH, a * 16:(a + 1) * 16, :],
                                         m.q_dram[a, qp, i, :, tok].rearrange("(h i) n -> i h n", i=HH)).then_inc(loaded, 16)
                        sp.dma_start(ks[at:at + HH, :, :],
                                     m.k_dram[kp, i, :, tok].rearrange("(h i) n -> i h n", i=HH)).then_inc(loaded, 16)
                for j in range(NB):
                    sp.dma_start(va[:, j, :, 0:HD], m.v_dram[b * NB + j].rearrange(
                        "p (h e) -> p h e", e=HD)).then_inc(loaded, 16)
                sp.wait_ge(mlo, 2 * b + 2)
                sp.dma_start(m.m_dram[b].rearrange("a h n -> h a n"), mh[:, :, :]).then_inc(m_stored, 16)
                sp.wait_ge(m_stored, 16 * b + 16)
                sp.dma_start(qs[STACK:STACK + 2, :, :], m.m_dram[b]).then_inc(m_loaded, 16)

        @block.gpsimd
        def _(pool):
            pool.memset(ks[32:64, :, :], QS).then_inc(memsets, 1)
            pool.memset(ks[64:128, :, :], 0.0).then_inc(memsets, 1)
            pool.memset(qs[64:128, 3 * H1 // 4:, :], 0.0).then_inc(ones_set, 1)
            pool.wait_ge(memsets, 2)
            pool.wait_ge(ones_set, 1)
            pool.memset(va[:, :, :, HD:HD + 1], 1.0).then_inc(ones_set, 1)

        def pair(i):
            return m.bank[:, 2 * i:2 * i + 2, :].rearrange("p a n -> p (a n)")

        def cuts(lo, hi):
            return [(lo, hi)] if hi <= TT or lo >= TT else [(lo, TT), (TT, hi)]

        @block.tensor
        def _(pe):
            pe.wait_ge(memsets, 4)
            pe.wait_ge(ones_set, 2)
            pe.wait_ge(mask_loaded, 16)
            with pe.Fori(0, B) as b:
                with pe.Fori(0, HKV) as g:
                    pe.wait_ge(loaded, b * QLOADS * 16 + QLOADS * 16)
                    for u in range(REP * NB):
                        i, r = u // REP, u % REP
                        if u >= 4:
                            pe.wait_ge(max_done, b * U1 + g * (REP * NB) + u - 3)
                        S = (i + 1) * P
                        q = qs[:, bass.ds(g * REP + r, 1), i * P:(i + 1) * P].squeeze(1)
                        out = pair(u % 4)
                        pe.matmul(out[:, S - P:S], far[:, 0, :], far[:, 1, :], start=True, stop=False)
                        k = ks[:, bass.ds(g, 1), S - P:S].squeeze(1)
                        mm = pe.matmul(out[:, S - P:S], q, k, start=False, stop=True)
                        for lo, hi in cuts(0, S - P) if i else ():
                            k = ks[:, bass.ds(g, 1), lo:hi].squeeze(1)
                            mm = pe.matmul(out[:, lo:hi], q, k, start=True, stop=True)
                        mm.then_inc(sc_done, 1)
                    pe.wait_ge(max_done, b * U1 + g * (REP * NB) + REP * NB)
                for i in range(NB):
                    mm = pe.transpose(m.bank[0:H1, i // 4, (i % 4) * P:(i % 4 + 1) * P], mx[:, i, :], m.ident[:, :])
                mm.then_inc(turned, 1)
                with pe.Fori(0, HKV) as g:
                    pe.wait_ge(mlo, 2 * b + 2)
                    pe.wait_ge(m_loaded, b * 16 + 16)
                    for r in range(REP):
                        hd = b * H1 + g * REP + r

                        def scores(i):
                            n = r * NB + i
                            if n >= 3:
                                pe.wait_ge(exp_done, (hd - r) * NB + n - 2)
                            out = pair(n % 3)
                            k = ks[:, bass.ds(g, 1), i * P:(i + 1) * P].squeeze(1)
                            lo, hi = i * P, (i + 1) * P
                            pe.matmul(out[:, lo:hi], far[:, 0, :], far[:, 2, :], start=True, stop=False)
                            q = qs[:, bass.ds(g * REP + r, 1), lo:hi].squeeze(1)
                            mm = pe.matmul(out[:, lo:hi], k, q, start=False, stop=True)
                            for lo, hi in cuts(hi, T) if hi < T else ():
                                q = qs[:, bass.ds(g * REP + r, 1), lo:hi].squeeze(1)
                                mm = pe.matmul(out[:, lo:hi], k, q, start=True, stop=True)
                            mm.then_inc(st_done, 1)

                        def values(i):
                            n = r * NB + i
                            pe.wait_ge(exp_done, (hd - r) * NB + n + 1)
                            if i == 0 and r >= 2:
                                pe.wait_ge(y_done, hd - 1)
                            vv = va[:, i, bass.ds(g, 1), :].squeeze(1)
                            for jt in range(i, NB):
                                o = jt * (HD + 1)
                                mm = pe.matmul(m.bank[:, 6 + r % 2, o:o + HD + 1], pexp[:, n % 3, jt * P:(jt + 1) * P],
                                               vv, start=(i == 0 and jt == 0), stop=True, skip_group_check=True)
                            mm.then_inc(pv_done, 1)

                        scores(0)
                        scores(1)
                        for i in range(NB):
                            if i + 2 < NB:
                                scores(i + 2)
                            values(i)
                    pe.wait_ge(y_done, b * H1 + g * REP + REP)

        @block.scalar
        def _(act):
            with act.Fori(0, B) as b:
                act.wait_ge(turned, b + 1)
                for i in range(2):
                    act.activation(mh[:, 0, i * TT:(i + 1) * TT], m.bank[0:H1, i, :], ACT.Copy,
                                   scale=-1.0 / QS).then_inc(mhi, 1)
                with act.Fori(0, HKV) as g:
                    for r in range(REP):
                        for i in range(NB):
                            n = r * NB + i
                            hd = b * H1 + g * REP
                            act.wait_ge(st_done, hd * NB + n + 1)
                            if n >= 3:
                                act.wait_ge(pv_done, hd * NB + n - 2)
                            act.activation(pexp[:, n % 3, i * P:T], pair(n % 3)[:, i * P:T], ACT.Exp,
                                           scale=1.0 / (QS * QS * HD ** 0.5)).then_inc(exp_done, 1)

        @block.vector
        def _(dve):
            dve.memset(qs[32:64, :, :].bitcast(mybir.dt.uint32), 0).then_inc(memsets, 1)
            dve.memset(qs[64:128, 0:3 * H1 // 4, :].bitcast(mybir.dt.uint32), 0).then_inc(memsets, 1)
            with dve.Fori(0, B) as b:
                with dve.Fori(0, HKV) as g:
                    for u in range(REP * NB):
                        i, r = u // REP, u % REP
                        dve.wait_ge(sc_done, b * U1 + g * (REP * NB) + u + 1)
                        dve.tensor_reduce(mx[:, i, bass.ds(g * REP + r, 1)], pair(u % 4)[:, 0:(i + 1) * P], AX.X,
                                          ALU.max).then_inc(max_done, 1)
                for i in range(2):
                    dve.wait_ge(mhi, 2 * b + i + 1)
                    dve.scalar_tensor_tensor(mh[:, 1, i * TT:(i + 1) * TT], m.bank[0:H1, i, :], -1.0 / QS,
                                             mh[:, 0, i * TT:(i + 1) * TT], ALU.mult, ALU.subtract).then_inc(mlo, 1)
                with dve.Fori(0, HKV) as g:
                    for r in range(REP):
                        hd = b * H1 + g * REP + r
                        dve.wait_ge(pv_done, hd * NB + NB)
                        o = m.bank[:, 6 + r % 2, 0:NB * (HD + 1)].rearrange("p (j e) -> p j e", e=HD + 1)
                        dve.reciprocal(rec[:, r % 2, :], o[:, :, HD]).then_inc(rec_done, 1)
                        dve.wait_ge(rec_done, hd + 1)
                        y = m.y[:, bass.ds(b * NB, NB), bass.ds((g * REP + r) * HD, HD)]
                        dve.tensor_tensor(y, o[:, :, 0:HD], rec[:, r % 2, :].unsqueeze(2).broadcast_to([P, NB, HD]),
                                          ALU.mult).then_inc(y_done, 1)


def project_out(nc, m):
    ctx = ExitStack()
    with ctx:
        sb = lambda name, shape, dt=F32: ctx.enter_context(nc.sbuf_tensor("po_" + name, shape, dt))
        stage = sb("stage", [P, DC, D])
        w_hi = sb("w_hi", [P, DC, D], F16)
        w_lo = sb("w_lo", [P, DC, D], F16)
        yh = sb("yh", [P, DC, TT], F16)
        yl = sb("yl", [P, DC, TT], F16)
        s = sb("s", [P, 2, TT])
        loaded, whi, wlo = m.sem("po_loaded"), m.sem("po_whi"), m.sem("po_wlo")
        turned, hi_done, lo_done = m.sem("po_turned"), m.sem("po_hi_done"), m.sem("po_lo_done")
        o_mm, scaled, added, stored = (m.sem("po_" + n) for n in ("o_mm", "scaled", "added", "stored"))
        block = ctx.enter_context(nc.Block())

        @block.sync
        def _(sp):
            sp.dma_start(stage[:, :, :], m.d["woT"].rearrange("(c p) n -> p c n", p=P)).then_inc(loaded, 16)
            for t in range(NT):
                sp.wait_ge(added, DC * (t + 1))
                tok = slice(t * TT, (t + 1) * TT)
                sp.dma_start(m.outT[:, tok].rearrange("(c p) n -> p c n", p=P), m.x[:, :, tok]).then_inc(stored, 16)
            sp.wait_ge(stored, NT * 16)

        @block.scalar
        def _(act):
            act.wait_ge(loaded, 16)
            act.activation(w_hi[:, :, :], stage[:, :, :], ACT.Copy, scale=WS).then_inc(whi, 1)
            for t in range(NT):
                for c in range(DC):
                    act.wait_ge(turned, t * DC + c + 1)
                    if t:
                        act.wait_ge(o_mm, t * DC)
                    act.activation(yh[:, c, :], m.bank[:, c, :], ACT.Copy, scale=YS).then_inc(hi_done, 1)

        @block.vector
        def _(dve):
            dve.wait_ge(whi, 1)
            dve.scalar_tensor_tensor(w_lo[:, :, :], stage[:, :, :], WS, w_hi[:, :, :], ALU.mult,
                                     ALU.subtract).then_inc(wlo, 1)
            for t in range(NT):
                for c in range(DC):
                    dve.wait_ge(hi_done, t * DC + c + 1)
                    dve.scalar_tensor_tensor(yl[:, c, :], m.bank[:, c, :], YS, yh[:, c, :], ALU.mult,
                                             ALU.subtract).then_inc(lo_done, 1)
                for c in range(DC):
                    n = t * DC + c
                    dve.wait_ge(o_mm, n + 1)
                    tok = slice(t * TT, (t + 1) * TT)
                    dve.scalar_tensor_tensor(s[:, c % 2, :], m.bank[:, 4 + c, :], 1.0 / (YS * WS), m.acc[:, c, tok],
                                             ALU.mult, ALU.mult).then_inc(scaled, 1)
                    dve.wait_ge(scaled, n + 1)
                    dve.tensor_tensor(m.x[:, c, tok], m.x[:, c, tok], s[:, c % 2, :], ALU.add).then_inc(added, 1)

        @block.tensor
        def _(pe):
            pe.wait_ge(wlo, 1)
            for t in range(NT):
                for c in range(DC):
                    if t:
                        pe.wait_ge(lo_done, DC * (t - 1) + c + 1)
                    for j in range(4):
                        mm = pe.transpose(m.bank[:, c, j * P:(j + 1) * P], m.y[:, t * 4 + j, c * P:(c + 1) * P],
                                          m.ident[:, :])
                    mm.then_inc(turned, 1)
                pe.wait_ge(lo_done, DC * (t + 1))
                for c in range(DC):
                    if t:
                        pe.wait_ge(scaled, DC * (t - 1) + c + 1)
                    for k in range(DC):
                        mm = split_product(pe, m.bank[:, 4 + c, :], w_hi[:, k, c * P:(c + 1) * P],
                                           w_lo[:, k, c * P:(c + 1) * P], yh[:, k, :], yl[:, k, :], k == 0, k == DC - 1)
                    mm.then_inc(o_mm, 1)


def program(nc, d, outT):
    m = Shared()
    m.d, m.outT = d, outT
    with ExitStack() as ctx:
        def sb(name, shape, dt=F32, on=ctx):
            return on.enter_context(nc.sbuf_tensor("m_" + name, shape, dt))

        m.sem = lambda name: ctx.enter_context(nc.semaphore(name))
        m.bank = ctx.enter_context(nc.psum_tensor("bank", [P, 8, TT], F32))
        m.q_dram = nc.dram_tensor("q_scratch", (2, 2, 2, P, N), F16, kind="Internal").ap()
        m.k_dram = nc.dram_tensor("k_scratch", (2, 2, HKV * HH, N), F16, kind="Internal").ap()
        m.v_dram = nc.dram_tensor("v_scratch", (NJ, P, HKV * HD), F32, kind="Internal").ap()
        m.m_dram = nc.dram_tensor("m_scratch", (B, 2, H1, T), F16, kind="Internal").ap()
        m.x = sb("x", [P, DC, N])
        m.acc = sb("acc", [P, DC, N])
        m.ident = sb("ident", [P, P])
        m.mean_ones = sb("mean_ones", [P, P])
        m.x_loaded = m.sem("x_loaded")
        m.const_loaded = m.sem("const_loaded")
        m.const_count = 3 * 16
        with ExitStack() as normed:
            m.xh = sb("xh", [P, DC, N], F16, normed)
            m.xl = sb("xl", [P, DC, N], F16, normed)
            with ExitStack() as routed:
                m.gates = sb("gates", [P, N], F16, routed)
                m.sel = sb("sel", [P, EA * P], F16, routed)
                with nc.Block() as block:
                    @block.sync
                    def _(sp):
                        sp.dma_start(m.x[:, :, :], d["xT"].rearrange("(c p) n -> p c n", p=P)).then_inc(m.x_loaded, 16)
                        sp.dma_start(m.ident[:, :], d["ident"]).then_inc(m.const_loaded, 16)
                        sp.dma_start(m.mean_ones[:, :], d["mean_ones"]).then_inc(m.const_loaded, 16)
                        sp.dma_start(m.sel[:, :], d["sel"]).then_inc(m.const_loaded, 16)
                layer_norm(nc, m, "ln0")
                router(nc, m)
                experts(nc, m)
            linear_attention(nc, m)
            layer_norm(nc, m, "ln1")
            ternary_ffn(nc, m)
            project_qkv(nc, m)
        m.y = sb("y", [P, NJ, D])
        softmax_attention(nc, m)
        project_out(nc, m)


def constants():
    f = np.float32
    c = {"ident": np.eye(P, dtype=f), "mean_ones": np.full((P, P), 1.0 / D, f)}
    sel = np.zeros((P, EA, P), np.float16)
    for e in range(EA):
        sel[e, e] = sel[LO + e, e] = 1
    c["sel"] = sel.reshape(P, EA * P)
    c["block_mask"] = np.kron(np.eye(HG, dtype=f), np.ones((DK, DK), f))
    t = np.arange(T, dtype=f)[:, None]
    inv = (f(1.0) / f(10000.0) ** (np.arange(HALF, dtype=f) / f(HALF))).astype(f)
    ang = (t * inv[None, :]).astype(f)
    cos, sin = np.cos(ang).astype(f), np.sin(ang).astype(f)
    c["cos0"] = cos.reshape(NB, P, HALF).transpose(1, 0, 2)
    c["sin0"] = np.stack([-sin, sin], 1).reshape(NB, P, 2, HALF).transpose(1, 0, 2, 3)
    inv = (f(1.0) / f(10000.0) ** (np.arange(0, HD, 2, dtype=f) / f(HD))).astype(f)
    ang = (t * inv[None, :]).astype(f)
    scale = f(QS / (XS * WS))
    c["cos1"] = np.tile((np.cos(ang).astype(f) * scale).T, (P // HH, 1))
    c["sin1"] = np.tile((np.sin(ang).astype(f) * scale).T, (P // HH, 1))
    far = np.zeros((P, 3, P), np.float16)
    far[:, 0] = np.eye(P) * FAR
    far[:, 1] = np.triu(np.full((P, P), -FAR), 1)
    far[:, 2] = np.tril(np.full((P, P), -FAR), -1)
    c["far"] = far
    return c


def layouts(i):
    t = {"xT": i["L0_attn_x"].reshape(N, D).T, "WrT": i["L0_ffn_Wr"].T,
         "br": np.broadcast_to(i["L0_ffn_br"], (P, E))}
    up = np.concatenate([i["L0_ffn_W1"], i["L0_ffn_Ws1"].reshape(SHARED, M, D)]).transpose(0, 2, 1)
    down = np.concatenate([i["L0_ffn_W2"].transpose(0, 2, 1), i["L0_ffn_Ws2"].T.reshape(SHARED, M, D)])
    up = up.reshape(NG, EG, DC, P, M).transpose(0, 3, 1, 2, 4).reshape(NG, P, EG, DC * M)
    down = down.reshape(NG, EG, MC, P, D).transpose(0, 3, 1, 2, 4).reshape(NG, P, EG, MC * D)
    t["WE"] = np.concatenate([up, down], 3).reshape(NG, P, EG * WE)
    for a in "qkvgo":
        t[a + "0"] = i[f"L0_attn_{a}w"]
    for a in "qkv":
        t[a + "b"] = i[f"L0_attn_{a}b"]
    for a in "go":
        t[a + "bT"] = i[f"L0_attn_{a}b"].reshape(DC, P).T
    t["w1T"], t["w2T"] = i["L1_ffn_w1"].T, i["L1_ffn_w2"].T
    t["b1T"], t["b2T"] = i["L1_ffn_b1"].reshape(FC, P).T, i["L1_ffn_b2"].reshape(DC, P).T
    q = i["L1_attn_wq"].reshape(2, 16, HH, 2, D).transpose(0, 3, 1, 2, 4).reshape(D, D)
    k = i["L1_attn_wk"].reshape(HKV, HH, 2, D).transpose(2, 0, 1, 3).reshape(HKV * HD, D)
    t["wqkvT"] = np.concatenate([q, k, i["L1_attn_wv"]]).T
    t["woT"] = i["L1_attn_wo"].T
    return t


def kernel(**inputs):
    import concourse.bacc as bacc
    from concourse.bass_utils import run_bass_kernel_spmd

    arrays = layouts({k: np.asarray(v) for k, v in inputs.items()}) | constants()
    arrays = {f"in_{k}": np.ascontiguousarray(v) for k, v in arrays.items()}
    nc = bacc.Bacc("TRN2", target_bir_lowering=False, num_devices=1)
    d = {
        k[3:]: nc.dram_tensor(k, v.shape, mybir.dt.from_np(v.dtype), kind="ExternalInput").ap()
        for k, v in arrays.items()}
    outT = nc.dram_tensor("outT", (D, N), F32, kind="ExternalOutput").ap()
    program(nc, d, outT)
    r = run_bass_kernel_spmd(nc, [arrays], core_ids=[0])
    return np.ascontiguousarray(r.results[0]["outT"].T).reshape(B, T, D)
```

```python
from contextlib import ExitStack

import numpy as np

import concourse.bass as bass
from concourse import mybir

F32 = mybir.dt.float32
F16 = mybir.dt.float16
ALU = mybir.AluOpType
ACT = mybir.ActivationFunctionType
AX = mybir.AxisListType

P = 128
B, T, D = 2, 1024, 512
N = B * T
DC = D // P
TT = 512
NT = N // TT
NJ = N // P
EPS = 1e-5

E, M = 32, 256
G, KG, K = 8, 4, 6
SHARED = 2
EA = E + SHARED
EG = 2
NG = EA // EG
MC = M // P
WE = DC * M + MC * D
LO = 64

SCALE_ROUTE = 2.5
XS = 16.0
WS = 64.0
GS = 64.0
HS = 1.0 / 16.0


class Shared:
    pass


def split_product(pe, out, w_hi, w_lo, x_hi, x_lo, start, stop, **kw):
    pe.matmul(out, w_hi, x_hi, start=start, stop=False, **kw)
    pe.matmul(out, w_hi, x_lo, start=False, stop=False, **kw)
    return pe.matmul(out, w_lo, x_hi, start=False, stop=stop, **kw)


def layer_norm(nc, m, tag):
    ctx = ExitStack()
    with ctx:
        xc = ctx.enter_context(nc.sbuf_tensor(f"{tag}_centred", [P, 2, DC, TT], F32))
        sq = ctx.enter_context(nc.sbuf_tensor(f"{tag}_squares", [P, 2, DC, TT], F32))
        var = ctx.enter_context(nc.sbuf_tensor(f"{tag}_var", [P, 2, TT], F32))
        root = ctx.enter_context(nc.sbuf_tensor(f"{tag}_root", [P, 2, TT], F32))
        tmp = ctx.enter_context(nc.sbuf_tensor(f"{tag}_tmp", [P, 2, TT], F32))
        rstd = ctx.enter_context(nc.sbuf_tensor(f"{tag}_rstd", [P, 2, TT], F32))
        mean_done = m.sem(f"{tag}_mean_done")
        centred = m.sem(f"{tag}_centred_done")
        squared = m.sem(f"{tag}_squared")
        var_done = m.sem(f"{tag}_var_done")
        eps_added = m.sem(f"{tag}_eps_added")
        root_done = m.sem(f"{tag}_root_done")
        newton = m.sem(f"{tag}_newton")
        normed = m.sem(f"{tag}_normed")
        hi_done = m.sem(f"{tag}_hi_done")
        lo_done = m.sem(f"{tag}_lo_done")
        block = ctx.enter_context(nc.Block())

        @block.tensor
        def _(pe):
            def mean(t):
                if t >= 2:
                    pe.wait_ge(centred, t - 1)
                for c in range(DC):
                    mm = pe.matmul(m.bank[:, t % 2, :], m.mean_ones[:, :],
                                   m.x[:, c, t * TT:(t + 1) * TT], start=(c == 0), stop=(c == DC - 1))
                mm.then_inc(mean_done, 1)

            def variance(t):
                pe.wait_ge(squared, t + 1)
                if t >= 2:
                    pe.wait_ge(eps_added, t - 1)
                for c in range(DC):
                    mm = pe.matmul(m.bank[:, 2 + t % 2, :], m.mean_ones[:, :], sq[:, t % 2, c, :],
                                   start=(c == 0), stop=(c == DC - 1))
                mm.then_inc(var_done, 1)

            if tag == "ln0":
                pe.wait_ge(m.x_loaded, 16)
                pe.wait_ge(m.const_loaded, m.const_count)
            mean(0)
            for t in range(NT):
                if t + 1 < NT:
                    mean(t + 1)
                variance(t)

        @block.vector
        def _(dve):
            if tag == "ln0":
                dve.wait_ge(m.x_loaded, 16)
            def centre(t):
                dve.wait_ge(mean_done, t + 1)
                if t >= 2:
                    dve.wait_ge(lo_done, t - 1)
                mean = m.bank[:, t % 2, :].unsqueeze(1).broadcast_to([P, DC, TT])
                dve.tensor_tensor(xc[:, t % 2], m.x[:, :, t * TT:(t + 1) * TT], mean,
                                  ALU.subtract).then_inc(centred, 1)

            def scale(t):
                b = t % 2
                dve.wait_ge(var_done, t + 1)
                dve.tensor_scalar(var[:, b], m.bank[:, 2 + b, :], EPS, None, ALU.add).then_inc(eps_added, 1)
                dve.wait_ge(root_done, t + 1)
                dve.reciprocal(root[:, b], root[:, b]).then_inc(newton, 1)
                dve.wait_ge(newton, 4 * t + 1)
                dve.tensor_tensor(tmp[:, b], root[:, b], root[:, b], ALU.mult).then_inc(newton, 1)
                dve.wait_ge(newton, 4 * t + 2)
                dve.tensor_tensor(tmp[:, b], tmp[:, b], var[:, b], ALU.mult).then_inc(newton, 1)
                dve.wait_ge(newton, 4 * t + 3)
                dve.tensor_scalar(tmp[:, b], tmp[:, b], -0.5 * XS, 1.5 * XS, ALU.mult, ALU.add).then_inc(newton, 1)
                dve.wait_ge(newton, 4 * t + 4)
                dve.tensor_tensor(rstd[:, b], tmp[:, b], root[:, b], ALU.mult).then_inc(normed, 1)
                dve.wait_ge(normed, 2 * t + 1)
                dve.wait_ge(squared, t + 1)
                dve.tensor_tensor(xc[:, b], xc[:, b], rstd[:, b].unsqueeze(1).broadcast_to([P, DC, TT]),
                                  ALU.mult).then_inc(normed, 1)

            centre(0)
            for t in range(NT):
                if t + 1 < NT:
                    centre(t + 1)
                scale(t)

        @block.scalar
        def _(act):
            def square(t):
                act.wait_ge(centred, t + 1)
                if t >= 2:
                    act.wait_ge(var_done, t - 1)
                act.activation(sq[:, t % 2], xc[:, t % 2], ACT.Square).then_inc(squared, 1)

            square(0)
            for t in range(NT):
                if t + 1 < NT:
                    square(t + 1)
                act.wait_ge(eps_added, t + 1)
                if t >= 2:
                    act.wait_ge(normed, 2 * (t - 2) + 1)
                act.activation(root[:, t % 2], var[:, t % 2], ACT.Sqrt).then_inc(root_done, 1)
                act.wait_ge(normed, 2 * t + 2)
                act.activation(m.xh[:, :, t * TT:(t + 1) * TT], xc[:, t % 2], ACT.Copy).then_inc(hi_done, 1)

        @block.gpsimd
        def _(pool):
            for t in range(NT):
                pool.wait_ge(hi_done, t + 1)
                tile = m.xh[:, :, t * TT:(t + 1) * TT]
                pool.tensor_tensor(m.xl[:, :, t * TT:(t + 1) * TT], xc[:, t % 2], tile,
                                   ALU.subtract).then_inc(lo_done, 1)


def router(nc, m):
    ctx = ExitStack()
    with ctx:
        sb = lambda name, shape, dt=F32: ctx.enter_context(nc.sbuf_tensor("rt_" + name, shape, dt))
        wr = sb("wr", [P, DC, E])
        wr_hi = sb("wr_hi", [P, DC, E], F16)
        wr_lo = sb("wr_lo", [P, DC, E], F16)
        br = sb("br", [P, E])
        logit = sb("logit", [P, NJ, E])
        s = sb("s", [P, NJ, E])
        pair = sb("pair", [P, 4, NJ, G])
        gw = sb("gw", [P, NJ, G + 4])
        top = sb("top", [P, NJ, 8])
        kept = sb("kept", [P, NJ, G])
        mx = sb("mx", [P, NJ, E + 2])
        gate = sb("gate", [P, NJ, EA])
        total = sb("total", [P, NJ])
        loaded = m.sem("rt_loaded")
        split = m.sem("rt_split")
        logits_done = m.sem("rt_logits_done")
        step = m.sem("rt_step")
        sig = m.sem("rt_sig")
        gate_done = m.sem("rt_gate_done")
        turned = m.sem("rt_turned")
        gate_hi = m.sem("rt_gate_hi")
        gate_zero = m.sem("rt_gate_zero")
        block = ctx.enter_context(nc.Block())

        @block.sync
        def _(sp):
            sp.dma_start(wr[:, :, :], m.d["WrT"].rearrange("(c p) e -> p c e", p=P)).then_inc(loaded, 16)
            sp.dma_start(br[:, :], m.d["br"]).then_inc(loaded, 16)

        @block.gpsimd
        def _(pool):
            pool.memset(m.gates[:, :], 0.0).then_inc(gate_zero, 1)
            pool.memset(m.acc[:, :, :], 0.0)

        @block.scalar
        def _(act):
            act.wait_ge(loaded, 32)
            act.activation(wr_hi[:, :, :], wr[:, :, :], ACT.Copy, scale=WS).then_inc(split, 1)
            act.wait_ge(step, 1)
            act.activation(s[:, :, :], logit[:, :, :], ACT.Sigmoid).then_inc(sig, 1)
            act.wait_ge(gate_zero, 1)
            for t in range(NT):
                act.wait_ge(turned, 4 * (t + 1))
                act.activation(m.gates[0:EA, t * TT:(t + 1) * TT], m.bank[0:EA, 1 + t, :],
                               ACT.Copy).then_inc(gate_hi, 1)

        @block.tensor
        def _(pe):
            pe.wait_ge(split, 2)
            for j in range(NJ):
                for c in range(DC):
                    xh, xl = (v[:, c, j * P:(j + 1) * P] for v in (m.xh, m.xl))
                    mm = split_product(pe, m.bank[:, 0, j * E:(j + 1) * E], xh, xl, wr_hi[:, c, :],
                                       wr_lo[:, c, :], c == 0, c == DC - 1)
            mm.then_inc(logits_done, 1)
            pe.wait_ge(gate_done, 1)
            for j in range(NJ):
                pe.transpose(m.bank[0:EA, 1 + j // 4, (j % 4) * P:(j % 4 + 1) * P], gate[:, j, :],
                             m.ident[:, :]).then_inc(turned, 1)

        @block.vector
        def _(dve):
            n = [0]

            def then(ins):
                n[0] += 1
                ins.then_inc(step, 1)
                dve.wait_ge(step, n[0])

            dve.wait_ge(loaded, 32)
            dve.wait_ge(split, 1)
            dve.scalar_tensor_tensor(wr_lo[:, :, :], wr[:, :, :], WS, wr_hi[:, :, :], ALU.mult,
                                     ALU.subtract).then_inc(split, 1)
            for i in range(4):
                dve.memset(gw[:, :, G + i], -2.0 - i)
            for i in range(2):
                dve.memset(mx[:, :, E + i], -2.0 - i)
            dve.memset(gate[:, :, E:EA], GS)
            dve.wait_ge(logits_done, 1)
            then(dve.scalar_tensor_tensor(
                logit[:, :, :], m.bank[:, 0, :].rearrange("p (j e) -> p j e", e=E), 1.0 / (XS * WS),
                br[:, :].unsqueeze(1).broadcast_to([P, NJ, E]), ALU.mult, ALU.add))
            dve.wait_ge(sig, 1)
            q = s[:, :, :].rearrange("p j (g i) -> p j g i", i=4)
            dve.tensor_tensor(pair[:, 0], q[:, :, :, 0], q[:, :, :, 1], ALU.add)
            dve.tensor_tensor(pair[:, 1], q[:, :, :, 2], q[:, :, :, 3], ALU.add)
            dve.tensor_tensor(pair[:, 2], q[:, :, :, 0], q[:, :, :, 1], ALU.max)
            then(dve.tensor_tensor(pair[:, 3], q[:, :, :, 2], q[:, :, :, 3], ALU.max))
            then(dve.tensor_tensor(pair[:, 0], pair[:, 0], pair[:, 1], ALU.max))
            then(dve.tensor_tensor(pair[:, 2], pair[:, 2], pair[:, 3], ALU.add))
            then(dve.tensor_tensor(gw[:, :, 0:G], pair[:, 0], pair[:, 2], ALU.max))
            for j in range(NJ):
                last = dve.max(top[:, j, :], gw[:, j, :])
            then(last)
            for i in range(4):
                last = dve.memset(top[:, :, KG + i], -2.0 - i)
            then(last)
            for j in range(NJ):
                last = dve.match_replace(gw[:, j, :], top[:, j, :], gw[:, j, :], -9.0)
            then(last)
            then(dve.tensor_scalar(kept[:, :, :], gw[:, :, 0:G], -9.0, None, ALU.is_equal))
            then(dve.tensor_tensor(mx[:, :, 0:E].rearrange("p j (g i) -> p j g i", i=4), q,
                                   kept[:, :, :].unsqueeze(3).broadcast_to([P, NJ, G, 4]), ALU.mult))
            for j in range(NJ):
                last = dve.max(top[:, j, :], mx[:, j, :])
            then(last)
            for i in range(2):
                last = dve.memset(top[:, :, K + i], -2.0 - i)
            then(last)
            for j in range(NJ):
                last = dve.match_replace(mx[:, j, :], top[:, j, :], mx[:, j, :], -9.0)
            then(last)
            then(dve.tensor_scalar(mx[:, :, 0:E], mx[:, :, 0:E], -9.0, None, ALU.is_equal))
            then(dve.tensor_tensor(s[:, :, :], s[:, :, :], mx[:, :, 0:E], ALU.mult))
            then(dve.tensor_reduce(total[:, :], s[:, :, :], AX.X, ALU.add))
            then(dve.tensor_scalar(total[:, :], total[:, :], 1e-20, None, ALU.add))
            then(dve.reciprocal(total[:, :], total[:, :]))
            then(dve.tensor_scalar(total[:, :], total[:, :], SCALE_ROUTE * GS, None, ALU.mult))
            dve.tensor_tensor(gate[:, :, 0:E], s[:, :, :],
                              total[:, :].unsqueeze(2).broadcast_to([P, NJ, E]), ALU.mult).then_inc(gate_done, 1)
            for t in range(NT):
                dve.wait_ge(gate_hi, t + 1)
                dve.tensor_tensor(m.gates[LO:LO + EA, t * TT:(t + 1) * TT], m.bank[0:EA, 1 + t, :],
                                  m.gates[0:EA, t * TT:(t + 1) * TT], ALU.subtract)


def experts(nc, m):
    UNITS = EG * MC
    STEPS = NG * NT
    PIECE = EG * WE // NT
    ctx = ExitStack()
    with ctx:
        sb = lambda name, shape, dt=F32: ctx.enter_context(nc.sbuf_tensor("ex_" + name, shape, dt))
        stage = sb("stage", [P, 2, EG * WE])
        wh = sb("wh", [P, 2, EG * WE], F16)
        wl = sb("wl", [P, 2, EG * WE], F16)
        r = sb("relu", [P, 2, TT])
        g = sb("gate", [P, 2, TT])
        hg = sb("gated", [P, 2, TT])
        hh = sb("hidden_hi", [P, UNITS, TT], F16)
        hl = sb("hidden_lo", [P, UNITS, TT], F16)
        staged = m.sem("ex_staged")
        split_hi = m.sem("ex_split_hi")
        split_lo = m.sem("ex_split_lo")
        gate_bc = m.sem("ex_gate_bc")
        gate_sb = m.sem("ex_gate_sb")
        up_done = m.sem("ex_up_done")
        relu_done = m.sem("ex_relu_done")
        gate_r = m.sem("ex_gate_r")
        gated = m.sem("ex_gated")
        hi_done = m.sem("ex_hi_done")
        lo_done = m.sem("ex_lo_done")
        hl_free = m.sem("ex_hl_free")
        acc_free = m.sem("ex_acc_free")
        H, GB, A = 0, 2, 4

        block = ctx.enter_context(nc.Block())

        @block.sync
        def _(sp):
            for p in range(2):
                sp.dma_start(stage[:, p, :], m.d["WE"][p]).then_inc(staged, 16)
                sp.wait_ge(staged, 16 * p + 16)
            with sp.Fori(2, NG) as p:
                sp.wait_ge(staged, 16 * p)
                sp.wait_ge(split_lo, NT * p - NT)
                sp.wait_ge(split_hi, NT * p - NT)
                sp.dma_start(stage[:, bass.ds(p % 2, 1), :],
                             m.d["WE"][bass.ds(p, 1)].rearrange("a p w -> p a w")).then_inc(staged, 16)
            sp.wait_ge(staged, 16 * NG)

        def piece(buf, n):
            return buf[:, :, :].rearrange("p a w -> p (a w)")[:, bass.ds((n // NT + 1) % 2 * (EG * WE) + n % NT * PIECE, PIECE)]

        def piece0(buf, i):
            return buf[:, 0, i * PIECE:(i + 1) * PIECE]

        @block.scalar
        def _(act):
            act.wait_ge(staged, 16)
            for i in range(NT):
                act.activation(piece0(wh, i), piece0(stage, i), ACT.Copy, scale=WS).then_inc(split_hi, 1)

            def unit(n, u):
                k = n * UNITS + u
                if u % MC == 0:
                    e = u // MC
                    act.wait_ge(gate_bc, n * EG + e + 1)
                    act.activation(g[:, e, :], m.bank[:, GB + e, :], ACT.Copy, scale=HS / GS).then_inc(gate_sb, 1)
                act.wait_ge(up_done, k + 1)
                act.activation(r[:, u % 2, :], m.bank[:, H + u % 2, :], ACT.Relu,
                               scale=1.0 / (XS * WS)).then_inc(relu_done, 1)
                act.wait_ge(hl_free, k + 1)
                act.wait_ge(gated, k + 1)
                act.activation(hh[:, u, :], hg[:, u % 2, :], ACT.Copy).then_inc(hi_done, 1)

            with act.Fori(0, STEPS - NT) as n:
                for u in range(UNITS):
                    unit(n, u)
                act.wait_ge(staged, n // NT * 16 + 32)
                act.activation(piece(wh, n), piece(stage, n), ACT.Copy, scale=WS).then_inc(split_hi, 1)
            with act.Fori(STEPS - NT, STEPS) as n:
                for u in range(UNITS):
                    unit(n, u)

        @block.vector
        def _(dve):
            dve.sem_inc(acc_free, DC)
            for i in range(NT):
                dve.wait_ge(split_hi, i + 1)
                dve.scalar_tensor_tensor(piece0(wl, i), piece0(stage, i), WS, piece0(wh, i), ALU.mult,
                                         ALU.subtract).then_inc(split_lo, 1)

            def unit(n, u):
                k = n * UNITS + u
                dve.wait_ge(relu_done, k + 1)
                dve.wait_ge(gate_sb, n * EG + u // MC + 1)
                dve.tensor_tensor(hg[:, u % 2, :], r[:, u % 2, :], g[:, u // MC, :], ALU.mult).then_inc(gate_r, 1)
                dve.wait_ge(gate_r, k + 1)
                dve.tensor_tensor(hg[:, u % 2, :], hg[:, u % 2, :], r[:, u % 2, :], ALU.mult).then_inc(gated, 1)
                dve.wait_ge(hi_done, k + 1)
                dve.tensor_tensor(hl[:, u, :], hg[:, u % 2, :], hh[:, u, :], ALU.subtract).then_inc(lo_done, 1)

            def split(n):
                dve.wait_ge(split_hi, n + NT + 1)
                dve.scalar_tensor_tensor(piece(wl, n), piece(stage, n), WS, piece(wh, n), ALU.mult,
                                         ALU.subtract).then_inc(split_lo, 1)

            def add_sums(n, tile):
                dve.wait_ge(hl_free, n * UNITS + 2 * UNITS)
                for c in range(DC):
                    acc = m.acc[:, c, bass.ds(tile * TT, TT)]
                    dve.scalar_tensor_tensor(acc, m.bank[:, A + c, :], 1.0 / (WS * HS), acc, ALU.mult,
                                             ALU.add).then_inc(acc_free, 1)

            unit(0, 0)
            unit(0, 1)
            with dve.Fori(0, STEPS - NT) as n:
                unit(n, 2)
                unit(n, 3)
                split(n)
                unit(n + 1, 0)
                unit(n + 1, 1)
                add_sums(n, n % NT)
            with dve.Fori(STEPS - NT, STEPS - 1) as n:
                unit(n, 2)
                unit(n, 3)
                unit(n + 1, 0)
                unit(n + 1, 1)
                add_sums(n, n % NT)
            unit(STEPS - 1, 2)
            unit(STEPS - 1, 3)
            add_sums(STEPS - 1, NT - 1)

        @block.tensor
        def _(pe):
            pe.sem_inc(hl_free, UNITS)

            def weights(buf, n, at, width):
                if isinstance(n, int):
                    return buf[:, n // NT % 2, at:at + width]
                return buf[:, :, :].rearrange("p a w -> p (a w)")[:, bass.ds(n // NT % 2 * (EG * WE) + at, width)]

            def up(n, u, first=False):
                e, c = u // MC, u % MC
                if not first:
                    pe.wait_ge(relu_done, n * UNITS + u - 1)
                if u == 0:
                    pe.wait_ge(split_lo, n // NT * NT + NT)
                tile = n % NT
                tok = bass.ds(tile * TT, TT)
                if c == 0:
                    sel = m.sel[:, bass.ds((n // NT * EG + e) * P, P)]
                    pe.matmul(m.bank[:, GB + e, :], sel, m.gates[:, tok], start=True, stop=True).then_inc(gate_bc, 1)
                for k in range(DC):
                    at = e * WE + k * M + c * P
                    mm = split_product(pe, m.bank[:, H + u % 2, :], weights(wh, n, at, P), weights(wl, n, at, P),
                                       m.xh[:, k, tok], m.xl[:, k, tok], k == 0, k == DC - 1)
                mm.then_inc(up_done, 1)

            def down(n, u):
                e, c = u // MC, u % MC
                pe.wait_ge(lo_done, n * UNITS + u + 1)
                for d in range(DC):
                    if u == 0:
                        pe.wait_ge(acc_free, n * DC + d + 1)
                    at = e * WE + DC * M + c * D + d * P
                    mm = split_product(pe, m.bank[:, A + d, :], weights(wh, n, at, P), weights(wl, n, at, P),
                                       hh[:, u, :], hl[:, u, :], u == 0, u == UNITS - 1)
                mm.then_inc(hl_free, 1)

            up(0, 0, first=True)
            up(0, 1, first=True)
            with pe.Fori(0, STEPS - 1) as n:
                up(n, 2)
                down(n, 0)
                up(n, 3)
                down(n, 1)
                up(n + 1, 0)
                down(n, 2)
                up(n + 1, 1)
                down(n, 3)
            n = STEPS - 1
            up(n, 2)
            down(n, 0)
            up(n, 3)
            down(n, 1)
            down(n, 2)
            down(n, 3)

H0, DK, CHUNK = 16, 32, 64
HALF = DK // 2
HG = P // DK
NB = T // P
TB = T // TT
AS = 4.0


def linear_attention(nc, m):
    ctx = ExitStack()
    with ctx:
        sb = lambda name, shape, dt=F32: ctx.enter_context(nc.sbuf_tensor("la_" + name, shape, dt))
        W = P + 1
        SW = P + HG
        BT = NB // TB
        f = sb("f", [P, 2, 2, D])
        wstage = [sb("wstage", [P, DC, D]), f[:, :, :, :].rearrange("p a b d -> p (a b) d")]
        w_hi = sb("w_hi", [P, 5, DC, D], F16)
        w_lo = sb("w_lo", [P, 5, DC, D], F16)
        rows = sb("rows", [P, 3, D])
        cols = sb("cols", [P, 2, DC])
        cos = sb("cos", [P, NB, HALF])
        sin = sb("sin", [P, NB, 2, HALF])
        mask = sb("mask", [P, P])
        a = sb("a", [P, 2, D])
        t1 = sb("t1", [P, 2, D])
        t2 = sb("t2", [P, 2, D])
        v = sb("v", [P, 2, DC, W])
        qT = sb("qT", [P, DC, P])
        S = sb("S", [P, 2, DC, SW])
        rden = sb("rden", [P, 2, 2, HG])
        aoh = sb("aoh", [P, DC, TT], F16)
        aol = sb("aol", [P, DC, TT], F16)
        gT = sb("gT", [P, DC, T])
        s = wstage[0][:, 0:2, :]
        ao = wstage[0][:, 2, :]
        ag = wstage[0][:, 3, :].rearrange("p (c t) -> p c t", c=DC)

        loaded, w_loaded = m.sem("la_loaded"), m.sem("la_w_loaded")
        whi, wlo = m.sem("la_whi"), m.sem("la_wlo")
        ones_set = m.sem("la_ones")
        silu_sig, silu_done = m.sem("la_silu_sig"), m.sem("la_silu_done")
        g_mm, g_sig = m.sem("la_g_mm"), m.sem("la_g_sig")
        proj_qk, proj_v = m.sem("la_proj_qk"), m.sem("la_proj_v")
        qk_biased, v_biased = m.sem("la_qk_biased"), m.sem("la_v_biased")
        cos_done, sin_done, turned = m.sem("la_cos_done"), m.sem("la_sin_done"), m.sem("la_turned")
        min_done, exp_done, mapped = m.sem("la_min_done"), m.sem("la_exp_done"), m.sem("la_mapped")
        qT_mm, qT_sb = m.sem("la_qT_mm"), m.sem("la_qT_sb")
        kv_done, state_set, num_done = m.sem("la_kv_done"), m.sem("la_state_set"), m.sem("la_num_done")
        den_eps, den_inv, divided, gated = (m.sem("la_" + n) for n in ("den_eps", "den_inv", "divided", "gated"))
        ao_mm, ao_hi, ao_lo = m.sem("la_ao_mm"), m.sem("la_ao_hi"), m.sem("la_ao_lo")
        o_mm, o_biased, o_gated, x_added = (m.sem("la_" + n) for n in ("o_mm", "o_biased", "o_gated", "x_added"))
        Q, V, NUM, QT, KV = 0, 2, 3, 5, 6
        LOADS = 3 + 1 + 1 + 2 + 1
        PIECE = 2 * D
        PIECES = DC * N // PIECE
        block = ctx.enter_context(nc.Block())

        def piece(i):
            return m.acc[:, :, :].rearrange("p c n -> p (c n)")[:, i * PIECE:(i + 1) * PIECE]

        def sigmoid(i):
            return (t1, t2)[i % 2][:, :, :].rearrange("p a d -> p (a d)")

        @block.sync
        def _(sp):
            for i, w in enumerate((m.d["g0"], m.d["q0"], m.d["k0"], m.d["v0"], m.d["o0"])):
                if i >= 2:
                    sp.wait_ge(whi, i - 1)
                    sp.wait_ge(wlo, i - 1)
                if i:
                    sp.wait_ge(w_loaded, 16 * i)
                sp.dma_start(wstage[i % 2][:, :, :], w.rearrange("(c p) n -> p c n", p=P)).then_inc(w_loaded, 16)
                if i == 0:
                    sp.dma_start(cols[:, 0, :], m.d["gbT"]).then_inc(loaded, 16)
                    sp.dma_start(cols[:, 1, :], m.d["obT"]).then_inc(loaded, 16)
                    for j, bias in enumerate((m.d["qb"], m.d["kb"], m.d["vb"])):
                        sp.dma_start(rows[:, j, :], bias.partition_broadcast(P)).then_inc(loaded, 16)
                    sp.dma_start(cos[:, :, :], m.d["cos0"]).then_inc(loaded, 16)
                    sp.dma_start(sin[:, :, :, :], m.d["sin0"]).then_inc(loaded, 16)
                    sp.dma_start(mask[:, :], m.d["block_mask"]).then_inc(loaded, 16)
            sp.wait_ge(w_loaded, 16 * 5)

        @block.gpsimd
        def _(pool):
            pool.memset(v[:, :, :, P:W], 1.0).then_inc(ones_set, 1)
            for i in range(PIECES):
                pool.wait_ge(silu_sig, i + 1)
                pool.tensor_tensor(piece(i), piece(i), sigmoid(i), ALU.mult).then_inc(silu_done, 1)
            pool.wait_ge(loaded, 16 * LOADS)
            with pool.Fori(0, B) as b:
                def sines(j):
                    pool.wait_ge(qk_biased, b * NB + j + 1)
                    heads = a[:, :, :].rearrange("p a (h r i) -> p (a h) r i", r=2, i=HALF)
                    out = t2[:, :, :].rearrange("p a (h r i) -> p (a h) r i", r=2, i=HALF)
                    for r in range(2):
                        sn = sin[:, j, r, :].unsqueeze(1).broadcast_to([P, 2 * H0, HALF])
                        ins = pool.tensor_tensor(out[:, :, r, :], heads[:, :, 1 - r, :], sn, ALU.mult)
                    ins.then_inc(sin_done, 1)

                def low(j):
                    pool.wait_ge(ao_hi, b * NB + j + 1)
                    at = (j % BT) * P
                    pool.tensor_tensor(aol[:, :, at:at + P], ag[:, :, :], aoh[:, :, at:at + P],
                                       ALU.subtract).then_inc(ao_lo, 1)

                sines(0)
                for j in range(NB):
                    if j + 1 < NB:
                        sines(j + 1)
                    if j:
                        low(j - 1)
                low(NB - 1)

        @block.scalar
        def _(act):
            def split(i):
                act.wait_ge(w_loaded, 16 * i + 16)
                act.activation(w_hi[:, i], wstage[i % 2][:, :, :], ACT.Copy, scale=WS).then_inc(whi, 1)

            def silu(i):
                if i >= 2:
                    act.wait_ge(silu_done, i - 1)
                act.activation(sigmoid(i), piece(i), ACT.Sigmoid).then_inc(silu_sig, 1)

            for i in range(5):
                for k in range(i * PIECES // 5, (i + 1) * PIECES // 5):
                    silu(k)
                split(i)
            act.wait_ge(loaded, 16 * LOADS)
            with act.Fori(0, B) as b:
                def exps(j):
                    act.wait_ge(min_done, b * NB + j + 1)
                    act.activation(t2[:, :, :], t1[:, :, :], ACT.Exp).then_inc(exp_done, 1)

                def high(j):
                    act.wait_ge(gated, b * NB + j + 1)
                    at = (j % BT) * P
                    act.activation(aoh[:, :, at:at + P], ag[:, :, :], ACT.Copy).then_inc(ao_hi, 1)

                def outputs(t):
                    i = b * TB + t
                    for c in range(DC):
                        act.wait_ge(o_mm, i * DC + c + 1)
                        if c >= 2:
                            act.wait_ge(x_added, i * DC + c - 1)
                        act.activation(s[:, c % 2, :], m.bank[:, c % 2, :], ACT.Identity, bias=cols[:, 1, c:c + 1],
                                       scale=1.0 / (AS * WS)).then_inc(o_biased, 1)

                for n in range(TB * DC):
                    t, c = n // DC, n % DC
                    act.wait_ge(g_mm, b * TB * DC + n + 1)
                    act.activation(gT[:, c, t * TT:(t + 1) * TT], m.bank[:, n % 2, :], ACT.Sigmoid,
                                   bias=cols[:, 0, c:c + 1], scale=1.0 / (XS * WS)).then_inc(g_sig, 1)
                exps(0)
                for j in range(NB):
                    act.wait_ge(qT_mm, b * NB + j + 1)
                    act.activation(qT[:, :, :], m.bank[:, QT, :].rearrange("p (c t) -> p c t", c=DC),
                                   ACT.Copy).then_inc(qT_sb, 1)
                    if j:
                        high(j - 1)
                    if j + 1 < NB:
                        exps(j + 1)
                    if j and j % BT == 0:
                        outputs(j // BT - 1)
                high(NB - 1)
                outputs(TB - 1)

        @block.vector
        def _(dve):
            for i in range(5):
                dve.wait_ge(whi, i + 1)
                dve.scalar_tensor_tensor(w_lo[:, i], wstage[i % 2][:, :, :], WS, w_hi[:, i], ALU.mult,
                                         ALU.subtract).then_inc(wlo, 1)
            dve.wait_ge(loaded, 16 * LOADS)
            dve.wait_ge(silu_done, PIECES)
            with dve.Fori(0, B) as b:
                at = lambda j: b * NB + j + 1

                def bias_qk(j):
                    dve.wait_ge(proj_qk, at(j))
                    dve.scalar_tensor_tensor(a[:, :, :], m.bank[:, Q:Q + 2, :], 1.0 / (XS * WS), rows[:, 0:2, :],
                                             ALU.mult, ALU.add).then_inc(qk_biased, 1)
                    dve.wait_ge(qk_biased, at(j))
                    cs = cos[:, j, :].unsqueeze(1).broadcast_to([P, 4 * H0, HALF])
                    dve.tensor_tensor(t1[:, :, :].rearrange("p a (h i) -> p (a h) i", i=HALF),
                                      a[:, :, :].rearrange("p a (h i) -> p (a h) i", i=HALF), cs,
                                      ALU.mult).then_inc(cos_done, 1)

                def bias_v(j):
                    dve.wait_ge(proj_v, at(j))
                    chunks = lambda x: x.rearrange("p (c e) -> p c e", c=DC)
                    dve.scalar_tensor_tensor(v[:, j % 2, :, 0:P], chunks(m.bank[:, V, :]), 1.0 / (XS * WS),
                                             chunks(rows[:, 2, :]), ALU.mult, ALU.add).then_inc(v_biased, 1)

                def turn(j):
                    dve.wait_ge(cos_done, at(j))
                    dve.wait_ge(sin_done, at(j))
                    dve.tensor_tensor(a[:, :, :], t1[:, :, :], t2[:, :, :], ALU.add).then_inc(turned, 1)
                    dve.wait_ge(turned, at(j))
                    dve.tensor_scalar(t1[:, :, :], a[:, :, :], 0.0, None, ALU.min).then_inc(min_done, 1)

                def map_qk(j):
                    dve.wait_ge(exp_done, at(j))
                    dve.scalar_tensor_tensor(f[:, j % 2], a[:, :, :], 0.0, t2[:, :, :], ALU.max,
                                             ALU.add).then_inc(mapped, 1)

                def state(j, h):
                    n = 2 * j + h
                    dve.wait_ge(kv_done, b * 2 * NB + n + 1)
                    sums = m.bank[:, KV:KV + 2, 0:2 * W].rearrange("p b (c e) -> p b c e", e=W)
                    to = S[:, h].rearrange("p (b c) e -> p b c e", b=2)
                    heads = mask[:, :].rearrange("p (h e) -> p h e", e=DK)[:, :, 0]
                    dve.tensor_tensor(to[:, :, :, 0:P], sums[:, :, :, 0:P],
                                      mask[:, :].unsqueeze(1).unsqueeze(1).broadcast_to([P, 2, 2, P]), ALU.mult)
                    dve.tensor_tensor(to[:, :, :, P:SW], sums[:, :, :, P:W].broadcast_to([P, 2, 2, HG]),
                                      heads.unsqueeze(1).unsqueeze(1).broadcast_to([P, 2, 2, HG]),
                                      ALU.mult).then_inc(state_set, 1)

                def divide(j):
                    dve.wait_ge(num_done, b * 2 * NB + 2 * j + 2)
                    out = m.bank[:, NUM:NUM + 2, 0:2 * SW].rearrange("p b (c e) -> p b c e", e=SW)
                    dve.tensor_scalar(rden[:, :, :, :], out[:, :, :, P:SW], 1e-6, None, ALU.add).then_inc(den_eps, 1)
                    dve.wait_ge(den_eps, at(j))
                    dve.reciprocal(rden[:, :, :, :], rden[:, :, :, :]).then_inc(den_inv, 1)
                    dve.wait_ge(den_inv, at(j))
                    to = ao[:, :].rearrange("p (b c h e) -> p b c h e", b=2, c=2, h=HG)
                    for i in range(2):
                        ins = dve.scalar_tensor_tensor(
                            to[:, i], out[:, i, :, 0:P].rearrange("p c (h e) -> p c h e", h=HG), AS,
                            rden[:, i].unsqueeze(3).broadcast_to([P, 2, HG, DK]), ALU.mult, ALU.mult)
                    ins.then_inc(divided, 1)

                def gate(j):
                    dve.wait_ge(ao_mm, at(j))
                    if j:
                        dve.wait_ge(ao_lo, at(j - 1))
                    dve.tensor_tensor(ag[:, :, :], m.bank[:, QT, :].rearrange("p (c t) -> p c t", c=DC),
                                      gT[:, :, j * P:(j + 1) * P], ALU.mult).then_inc(gated, 1)

                def add_x(t):
                    i = b * TB + t
                    for c in range(DC):
                        tok = bass.ds(i * TT, TT)
                        dve.wait_ge(o_biased, i * DC + c + 1)
                        dve.tensor_tensor(s[:, c % 2, :], s[:, c % 2, :], m.acc[:, c, tok], ALU.mult).then_inc(o_gated, 1)
                        dve.wait_ge(o_gated, i * DC + c + 1)
                        dve.tensor_tensor(m.x[:, c, tok], m.x[:, c, tok], s[:, c % 2, :], ALU.add).then_inc(x_added, 1)

                bias_qk(0)
                bias_v(0)
                turn(0)
                map_qk(0)
                for j in range(NB):
                    state(j, 0)
                    if j + 1 < NB:
                        bias_qk(j + 1)
                    if j:
                        gate(j - 1)
                    state(j, 1)
                    if j + 1 < NB:
                        turn(j + 1)
                        bias_v(j + 1)
                        map_qk(j + 1)
                    divide(j)
                    if j and j % BT == 0:
                        add_x(j // BT - 1)
                gate(NB - 1)
                add_x(TB - 1)

        @block.tensor
        def _(pe):
            pe.wait_ge(ones_set, 1)
            with pe.Fori(0, B) as b:
                at = lambda j: b * NB + j + 1

                def project(j, ws):
                    tok = bass.ds((b * NB + j) * P, P)
                    for w in ws:
                        if j:
                            pe.wait_ge(v_biased if w == 2 else qk_biased, at(j - 1))
                        for c in range(DC):
                            mm = split_product(pe, m.bank[:, Q + w, :], m.xh[:, c, tok], m.xl[:, c, tok],
                                               w_hi[:, 1 + w, c, :], w_lo[:, 1 + w, c, :], c == 0, c == DC - 1)
                        if w:
                            mm.then_inc(proj_qk if w == 1 else proj_v, 1)

                def turn_q(j):
                    pe.wait_ge(mapped, at(j))
                    if j >= 2:
                        pe.wait_ge(gated, at(j - 2))
                    for c in range(DC):
                        mm = pe.transpose(m.bank[:, QT, c * P:(c + 1) * P], f[:, j % 2, 0, c * P:(c + 1) * P],
                                          m.ident[:, :])
                    mm.then_inc(qT_mm, 1)

                def outer(j, h):
                    n = 2 * j + h
                    if n:
                        pe.wait_ge(state_set, b * 2 * NB + n)
                    lo, hi = h * CHUNK, (h + 1) * CHUNK
                    for c in range(DC):
                        mm = pe.matmul(m.bank[:, KV + c // 2, c % 2 * W:(c % 2 + 1) * W],
                                       f[lo:hi, j % 2, 1, c * P:(c + 1) * P], v[lo:hi, j % 2, c, :],
                                       start=(n == 0 and c % 2 == 0), stop=True, skip_group_check=True)
                    mm.then_inc(kv_done, 1)

                def outputs(j, h):
                    pe.wait_ge(state_set, b * 2 * NB + 2 * j + h + 1)
                    for c in range(DC):
                        lo, hi = h * CHUNK, (h + 1) * CHUNK
                        mm = pe.matmul(m.bank[lo:hi, NUM + c // 2, c % 2 * SW:(c % 2 + 1) * SW], qT[:, c, lo:hi],
                                       S[:, h, c, :], start=True, stop=True)
                    mm.then_inc(num_done, 1)

                def turn_outputs(j):
                    pe.wait_ge(divided, at(j))
                    pe.wait_ge(qT_sb, at(min(j + 1, NB - 1)))
                    for c in range(DC):
                        mm = pe.transpose(m.bank[:, QT, c * P:(c + 1) * P], ao[:, c * P:(c + 1) * P], m.ident[:, :])
                    mm.then_inc(ao_mm, 1)

                def project_out(t):
                    i = b * TB + t
                    pe.wait_ge(ao_lo, at(t * BT + BT - 1))
                    pe.wait_ge(qk_biased, at(min(t * BT + BT + 1, NB - 1)))
                    for c in range(DC):
                        if c >= 2:
                            pe.wait_ge(o_biased, i * DC + c - 1)
                        for k in range(DC):
                            mm = split_product(pe, m.bank[:, c % 2, :], w_hi[:, 4, k, c * P:(c + 1) * P],
                                               w_lo[:, 4, k, c * P:(c + 1) * P], aoh[:, k, :], aol[:, k, :],
                                               k == 0, k == DC - 1)
                        mm.then_inc(o_mm, 1)
                    pe.wait_ge(o_biased, i * DC + DC)

                pe.wait_ge(wlo, 1)
                for n in range(TB * DC):
                    t, c = n // DC, n % DC
                    tok = bass.ds(b * T + t * TT, TT)
                    if n >= 2:
                        pe.wait_ge(g_sig, b * TB * DC + n - 1)
                    for k in range(DC):
                        mm = split_product(pe, m.bank[:, n % 2, :], w_hi[:, 0, k, c * P:(c + 1) * P],
                                           w_lo[:, 0, k, c * P:(c + 1) * P], m.xh[:, k, tok], m.xl[:, k, tok],
                                           k == 0, k == DC - 1)
                    mm.then_inc(g_mm, 1)
                pe.wait_ge(g_sig, b * TB * DC + TB * DC)
                pe.wait_ge(wlo, 5)
                project(0, range(3))
                for j in range(NB):
                    turn_q(j)
                    pe.wait_ge(v_biased, at(j))
                    outer(j, 0)
                    if j + 1 < NB:
                        project(j + 1, (0, 1))
                    if j:
                        turn_outputs(j - 1)
                    outer(j, 1)
                    if j + 1 < NB:
                        project(j + 1, (2,))
                    if j:
                        pe.wait_ge(divided, at(j - 1))
                    pe.wait_ge(qT_sb, at(j))
                    outputs(j, 0)
                    outputs(j, 1)
                    if j and j % BT == 0:
                        project_out(j // BT - 1)
                turn_outputs(NB - 1)
                project_out(TB - 1)

F = 2048
FC = F // P
TERNARY = 0.7
H1, HKV, HD = 32, 8, 16
REP = H1 // HKV
HH = HD // 2
QS = 16.0
YS = 16.0
STACK = 3 * HD
FAR = 60000.0


def ternary_ffn(nc, m):
    ctx = ExitStack()
    with ctx:
        sb = lambda name, shape, dt=F32: ctx.enter_context(nc.sbuf_tensor("tf_" + name, shape, dt))
        W = DC * F
        stage = sb("stage", [P, W])
        w1 = sb("w1", [P, DC, F], F16)
        w2 = sb("w2", [P, FC, D], F16)
        b1 = sb("b1", [P, FC])
        b2 = sb("b2", [P, DC])
        part = sb("part", [P, W // P])
        whole = sb("whole", [P, 2])
        thr = sb("thr", [P, 2, 2])
        h = sb("h", [P, 2, TT])
        hh = sb("hh", [P, 4, TT], F16)
        hl = sb("hl", [P, 4, TT], F16)
        loaded, staged = m.sem("tf_loaded"), m.sem("tf_staged")
        summed, total = m.sem("tf_summed"), m.sem("tf_total")
        step, ternary = m.sem("tf_step"), m.sem("tf_ternary")
        up_done, gelu_done, hi_done, lo_done = (m.sem("tf_" + n) for n in ("up_done", "gelu_done", "hi_done", "lo_done"))
        down_done, sig_done, out_done = (m.sem("tf_" + n) for n in ("down_done", "sig_done", "out_done"))
        block = ctx.enter_context(nc.Block())

        @block.sync
        def _(sp):
            sp.dma_start(b1[:, :], m.d["b1T"]).then_inc(loaded, 16)
            sp.dma_start(b2[:, :], m.d["b2T"]).then_inc(loaded, 16)
            sp.dma_start(stage[:, :].rearrange("p (c f) -> p c f", f=F),
                         m.d["w1T"].rearrange("(c p) f -> p c f", p=P)).then_inc(staged, 16)
            sp.wait_ge(ternary, 1)
            sp.dma_start(stage[:, :].rearrange("p (c d) -> p c d", d=D),
                         m.d["w2T"].rearrange("(c p) d -> p c d", p=P)).then_inc(staged, 16)

        @block.scalar
        def _(act):
            act.wait_ge(loaded, 32)
            with act.Fori(0, NT) as t:
                for f in range(FC):
                    k = t * FC + f
                    act.wait_ge(up_done, k + 1)
                    if f >= 2:
                        act.wait_ge(lo_done, k - 1)
                    act.activation(h[:, f % 2, :], m.bank[:, f % 2, :], ACT.Gelu, bias=b1[:, f:f + 1],
                                   scale=1.0 / XS).then_inc(gelu_done, 1)
                    if f >= 4:
                        act.wait_ge(down_done, k - 3)
                    act.wait_ge(gelu_done, k + 1)
                    act.activation(hh[:, f % 4, :], h[:, f % 2, :], ACT.Copy).then_inc(hi_done, 1)
                act.wait_ge(down_done, t * FC + FC)
                act.wait_ge(lo_done, t * FC + FC)
                for d in range(DC):
                    if d >= 2:
                        act.wait_ge(out_done, t * DC + d - 1)
                    act.activation(h[:, d % 2, :], m.bank[:, 4 + d, :], ACT.Sigmoid,
                                   bias=b2[:, d:d + 1]).then_inc(sig_done, 1)
                act.wait_ge(out_done, t * DC + DC)

        @block.vector
        def _(dve):
            dve.wait_ge(loaded, 32)
            n = 0
            for i, q in enumerate((w1, w2)):
                dve.wait_ge(staged, 16 * i + 16)
                dve.tensor_reduce(part[:, :], stage[:, :].rearrange("p (a b) -> p a b", b=P), AX.X, ALU.add,
                                  apply_absolute_value=True).then_inc(step, 1)
                n += 1
                dve.wait_ge(step, n)
                dve.tensor_reduce(whole[:, i:i + 1], part[:, :], AX.X, ALU.add).then_inc(summed, 1)
                dve.wait_ge(total, i + 1)
                dve.tensor_scalar(thr[:, i, 0:1], m.bank[:, 0, 0:1], D / (F * D), TERNARY, ALU.mult,
                                  ALU.mult).then_inc(step, 1)
                n += 1
                dve.wait_ge(step, n)
                dve.tensor_scalar(thr[:, i, 1:2], thr[:, i, 0:1], -1.0, None, ALU.mult).then_inc(step, 1)
                n += 1
                dve.wait_ge(step, n)
                flat = q[:, :, :].rearrange("p a b -> p (a b)")
                dve.tensor_scalar(flat, stage[:, :], thr[:, i, 1:2], None, ALU.is_le).then_inc(step, 1)
                n += 1
                dve.wait_ge(step, n)
                dve.scalar_tensor_tensor(flat, stage[:, :], thr[:, i, 0:1], flat, ALU.is_ge,
                                         ALU.subtract).then_inc(ternary, 1)
            with dve.Fori(0, NT) as t:
                for f in range(FC):
                    k = t * FC + f
                    dve.wait_ge(hi_done, k + 1)
                    dve.tensor_tensor(hl[:, f % 4, :], h[:, f % 2, :], hh[:, f % 4, :], ALU.subtract).then_inc(lo_done, 1)
                for d in range(DC):
                    dve.wait_ge(sig_done, t * DC + d + 1)
                    dve.scalar_tensor_tensor(m.acc[:, d, bass.ds(t * TT, TT)], m.bank[:, 4 + d, :], b2[:, d:d + 1],
                                             h[:, d % 2, :], ALU.add, ALU.mult).then_inc(out_done, 1)

        @block.tensor
        def _(pe):
            for i in range(2):
                pe.wait_ge(summed, i + 1)
                pe.matmul(m.bank[:, 0, 0:1], m.mean_ones[:, :], whole[:, i:i + 1], start=True,
                          stop=True).then_inc(total, 1)
            pe.wait_ge(ternary, 2)
            with pe.Fori(0, NT) as t:
                def up(f):
                    k = t * FC + f
                    if f >= 2:
                        pe.wait_ge(gelu_done, k - 1)
                    tok = bass.ds(t * TT, TT)
                    for c in range(DC):
                        w = w1[:, c, f * P:(f + 1) * P]
                        pe.matmul(m.bank[:, f % 2, :], w, m.xh[:, c, tok], start=(c == 0), stop=False)
                        mm = pe.matmul(m.bank[:, f % 2, :], w, m.xl[:, c, tok], start=False, stop=(c == DC - 1))
                    mm.then_inc(up_done, 1)

                def down(f):
                    k = t * FC + f
                    pe.wait_ge(lo_done, k + 1)
                    for d in range(DC):
                        w = w2[:, f, d * P:(d + 1) * P]
                        pe.matmul(m.bank[:, 4 + d, :], w, hh[:, f % 4, :], start=(f == 0), stop=False)
                        mm = pe.matmul(m.bank[:, 4 + d, :], w, hl[:, f % 4, :], start=False, stop=(f == FC - 1))
                    mm.then_inc(down_done, 1)

                up(0)
                up(1)
                for f in range(FC):
                    if f + 2 < FC:
                        up(f + 2)
                    down(f)
                pe.wait_ge(out_done, t * DC + DC)


def project_qkv(nc, m):
    ctx = ExitStack()
    with ctx:
        sb = lambda name, shape, dt=F32: ctx.enter_context(nc.sbuf_tensor("pj_" + name, shape, dt))
        WN = D + 2 * HKV * HD
        stage = sb("stage", [P, DC, WN])
        w_hi = sb("w_hi", [P, DC, WN], F16)
        w_lo = sb("w_lo", [P, DC, WN], F16)
        cos = sb("cos", [P, T])
        sin = sb("sin", [P, T])
        t1 = sb("t1", [P, 2, 4, TT])
        ev = sb("ev", [P, 2, 2, TT])
        pr = sb("pr", [P, 2, 2, 2, TT], F16)
        v = sb("v", [P, 2, 4, P])
        loaded, whi, wlo = m.sem("pj_loaded"), m.sem("pj_whi"), m.sem("pj_wlo")
        proj, mults, turned, hi_done, lo_done = (m.sem("pj_" + n) for n in ("proj", "mults", "turned", "hi_done", "lo_done"))
        stored = [m.sem("pj_stored0"), m.sem("pj_stored1")]
        gate_stored = m.sem("pj_gate_stored")
        v_mm, v_sb, v_stored = m.sem("pj_v_mm"), m.sem("pj_v_sb"), m.sem("pj_v_stored")
        UN = NT * 3
        units = [(t, w) for t in range(NT) for w in range(3)]
        block = ctx.enter_context(nc.Block())

        @block.sync
        def _(sp):
            sp.dma_start(stage[:, :, :], m.d["wqkvT"].rearrange("(c p) n -> p c n", p=P)).then_inc(loaded, 16)
            sp.dma_start(cos[:, :], m.d["cos1"]).then_inc(loaded, 16)
            sp.dma_start(sin[:, :], m.d["sin1"]).then_inc(loaded, 16)
            sp.dma_start(m.f_dram, m.acc[:, :, :]).then_inc(gate_stored, 16)
            for n, (t, w) in enumerate(units):
                sp.wait_ge(lo_done, n + 1)
                rows = P if w < 2 else P // 2
                dst = (m.q_dram[w] if w < 2 else m.k_dram)[:, :, :, t * TT:(t + 1) * TT]
                sp.dma_start(dst.rearrange("a b p n -> p a b n"), pr[0:rows, n % 2]).then_inc(stored[n % 2], 16)
                if w == 2:
                    sp.wait_ge(v_sb, t + 1)
                    sp.dma_start(m.v_dram[t * 4:(t + 1) * 4].rearrange("j p e -> p j e"), v[:, t % 2]).then_inc(v_stored, 16)
                    sp.wait_ge(v_stored, 16 * t + 16)
            for s in stored:
                sp.wait_ge(s, UN // 2 * 16)
            sp.wait_ge(gate_stored, 16)

        @block.scalar
        def _(act):
            act.wait_ge(loaded, 48)
            act.activation(w_hi[:, :, :], stage[:, :, :], ACT.Copy, scale=WS).then_inc(whi, 1)
            for n, (t, w) in enumerate(units):
                rows = P if w < 2 else P // 2
                act.wait_ge(turned, n + 1)
                if n >= 2:
                    act.wait_ge(stored[n % 2], n // 2 * 16)
                act.activation(pr[0:rows, n % 2, 0], ev[0:rows, n % 2], ACT.Copy).then_inc(hi_done, 1)
                if w == 2:
                    act.wait_ge(v_mm, t + 1)
                    if t >= 2:
                        act.wait_ge(v_stored, 16 * (t - 1))
                    act.activation(v[:, t % 2], m.bank[:, 6 + t % 2, :].rearrange("p (j e) -> p j e", e=P), ACT.Copy,
                                   scale=1.0 / (XS * WS)).then_inc(v_sb, 1)

        @block.vector
        def _(dve):
            dve.wait_ge(whi, 1)
            dve.scalar_tensor_tensor(w_lo[:, :, :], stage[:, :, :], WS, w_hi[:, :, :], ALU.mult,
                                     ALU.subtract).then_inc(wlo, 1)
            for n, (t, w) in enumerate(units):
                rows, b = P if w < 2 else P // 2, n % 2
                dve.wait_ge(proj, n + 1)
                cs = cos[0:rows, (t % TB) * TT:(t % TB + 1) * TT]
                sn = sin[0:rows, (t % TB) * TT:(t % TB + 1) * TT]
                ev_, od = (m.bank[0:rows, 2 * b + i, :] for i in range(2))
                for i, (x, y) in enumerate(((ev_, cs), (od, sn), (ev_, sn), (od, cs))):
                    ins = dve.tensor_tensor(t1[0:rows, b, i, :], x, y, ALU.mult)
                ins.then_inc(mults, 1)
                dve.wait_ge(mults, n + 1)
                if n >= 2:
                    dve.wait_ge(lo_done, n - 1)
                dve.tensor_tensor(ev[0:rows, b, 0, :], t1[0:rows, b, 0, :], t1[0:rows, b, 1, :], ALU.subtract)
                dve.tensor_tensor(ev[0:rows, b, 1, :], t1[0:rows, b, 2, :], t1[0:rows, b, 3, :],
                                  ALU.add).then_inc(turned, 1)

        @block.gpsimd
        def _(pool):
            for n, (t, w) in enumerate(units):
                rows, b = P if w < 2 else P // 2, n % 2
                pool.wait_ge(hi_done, n + 1)
                pool.tensor_tensor(pr[0:rows, b, 1], ev[0:rows, b], pr[0:rows, b, 0], ALU.subtract).then_inc(lo_done, 1)

        @block.tensor
        def _(pe):
            pe.wait_ge(wlo, 1)
            for n, (t, w) in enumerate(units):
                rows = P if w < 2 else P // 2
                if n >= 2:
                    pe.wait_ge(mults, n - 1)
                at = 2 * P * w
                for i in range(2):
                    for c in range(DC):
                        ws = slice(at + i * rows, at + (i + 1) * rows)
                        mm = split_product(pe, m.bank[0:rows, 2 * (n % 2) + i, :], w_hi[:, c, ws], w_lo[:, c, ws],
                                           m.xh[:, c, t * TT:(t + 1) * TT], m.xl[:, c, t * TT:(t + 1) * TT],
                                           c == 0, c == DC - 1)
                mm.then_inc(proj, 1)
                if w == 2:
                    if t >= 2:
                        pe.wait_ge(v_sb, t - 1)
                    for j in range(4):
                        tok = slice(t * TT + j * P, t * TT + (j + 1) * P)
                        for c in range(DC):
                            ws = slice(D + HKV * HD, WN)
                            mm = split_product(pe, m.bank[:, 6 + t % 2, j * P:(j + 1) * P], m.xh[:, c, tok], m.xl[:, c, tok],
                                               w_hi[:, c, ws], w_lo[:, c, ws], c == 0, c == DC - 1)
                    mm.then_inc(v_mm, 1)


def softmax_attention(nc, m):
    ctx = ExitStack()
    with ctx:
        sb = lambda name, shape, dt=F32: ctx.enter_context(nc.sbuf_tensor("sa_" + name, shape, dt))
        qs = sb("qs", [P, H1, T], F16)
        ks = [sb(f"ks{b}", [P, HKV, T], F16) for b in range(B)]
        v = sb("v", [P, NJ, HKV, HD])
        vg = sb("vg", [P, NB, 2 * HD])
        pexp = sb("pexp", [P, 2, REP, TT])
        mx = sb("mx", [P, B, NB, H1])
        mx2 = sb("mx2", [P, B, NB // 2, H1])
        mh = sb("mh", [H1, B, 2, T], F16)
        far = sb("far", [P, 3, P], F16)
        ob = sb("ob", [P, 2, TT])
        rec = sb("rec", [P, 2, 4, REP])
        first_loaded, second_loaded = m.sem("sa_first_loaded"), m.sem("sa_second_loaded")
        rest_loaded = m.sem("sa_rest_loaded")
        ones_set, zeros_set = m.sem("sa_ones_set"), m.sem("sa_zeros_set")
        sc_done, max_done, max_joined = m.sem("sa_sc_done"), m.sem("sa_max_done"), m.sem("sa_max_joined")
        turned, mhi, mlo = m.sem("sa_turned"), m.sem("sa_mhi"), m.sem("sa_mlo")
        m_stored, m_loaded = m.sem("sa_m_stored"), m.sem("sa_m_loaded")
        st_done = m.sem("sa_st_done")
        exp_done = m.sem("sa_exp_done")
        pv_done = m.sem("sa_pv_done")
        out_free = m.sem("sa_out_free")
        vg_done, ob_done, ob_turned = m.sem("sa_vg_done"), m.sem("sa_ob_done"), m.sem("sa_ob_turned")
        rec_done = m.sem("sa_rec_done")
        MU = [(i, s) for i in range(NB) for s in range(2) if s * TT < (i + 1) * P]
        WU = [(th, i) for th in range(2) for i in range(NB) if i * P < (th + 1) * TT]
        NMU, NWU = len(MU), len(WU)
        RING, OUT = 3, 6
        AHEAD = 3
        GA = HKV // 2
        block = ctx.enter_context(nc.Block())
        SLOTS = ((0, 0), (1, 0), (0, 1))
        FIRST = 1 + 7 + B * 7
        SECOND = B * 6
        REST = 7 + NJ

        @block.sync
        def _(sp):
            flat = lambda x: x.rearrange("p h n -> p (h n)")

            def load_q(b, a, sem):
                for slot, (qp, _) in enumerate(SLOTS):
                    for i in range(2):
                        at = 64 * b + slot * HD + i * HH
                        sp.dma_start(qs[at:at + HH, a * 16:(a + 1) * 16, :], m.q_dram[a, qp, i, :, b * T:(b + 1) * T]
                                     .rearrange("(h i) n -> i h n", i=HH)).then_inc(sem, 16)

            def load_k(b, sem):
                for slot, (_, kp) in enumerate(SLOTS):
                    for i in range(2):
                        at = 64 * b + slot * HD + i * HH
                        sp.dma_start(ks[b][at:at + HH, :, :], m.k_dram[kp, i, :, b * T:(b + 1) * T]
                                     .rearrange("(h i) n -> i h n", i=HH)).then_inc(sem, 16)
                at = 64 * b + STACK
                sp.dma_start(flat(ks[b][at:at + 16]), m.d["units"].partition_broadcast(16)).then_inc(sem, 16)

            sp.dma_start(far[:, :, :], m.d["far"]).then_inc(first_loaded, 16)
            load_k(0, first_loaded)
            for b in range(B):
                load_q(b, 0, first_loaded)
                at = 64 * b + STACK
                sp.dma_start(flat(qs[at:at + 16]), m.d["zeros"].partition_broadcast(16)).then_inc(first_loaded, 16)
            for b in range(B):
                load_q(b, 1, second_loaded)
            load_k(1, rest_loaded)
            for j in range(NJ):
                sp.dma_start(v[:, j], m.v_dram[j].rearrange("p (h e) -> p h e", e=HD)).then_inc(rest_loaded, 16)
            for b in range(B):
                sp.wait_ge(mlo, 2 * b + 2)
                sp.dma_start(m.m_dram[b].rearrange("a h n -> h a n"), mh[:, b]).then_inc(m_stored, 16)
                sp.wait_ge(m_stored, 16 * b + 16)
                at = 64 * b + STACK
                sp.dma_start(qs[at:at + 2, :, :], m.m_dram[b]).then_inc(m_loaded, 16)

        @block.gpsimd
        def _(pool):
            pool.memset(vg[:, :, HD:2 * HD], 1.0).then_inc(ones_set, 1)
            pool.wait_ge(rest_loaded, REST * 16)
            for b in range(B):
                with pool.Fori(0, HKV) as g:
                    G = b * HKV + g
                    pool.wait_ge(pv_done, G * NWU + 2)
                    pool.tensor_copy(vg[:, :, 0:HD], v[:, b * NB:(b + 1) * NB, bass.ds(g, 1), :].squeeze(2)).then_inc(vg_done, 1)

        @block.tensor
        def _(pe):
            pe.wait_ge(ones_set, 1)
            pe.wait_ge(zeros_set, 2)
            pe.wait_ge(first_loaded, FIRST * 16)

            def maxima(b, g):
                for u, (i, s) in enumerate(MU):
                    pe.wait_ge(max_done, (b * HKV + g) * NMU + u + 1)
                    base, end = s * TT, min((i + 1) * P, (s + 1) * TT)
                    diagonal = end == (i + 1) * P
                    if diagonal:
                        end -= P
                    for r in range(REP):
                        q = qs[:, bass.ds(g * REP + r, 1), i * P:(i + 1) * P].squeeze(1)
                        k = lambda lo, hi: ks[b][:, bass.ds(g, 1), lo:hi].squeeze(1)
                        out = m.bank[:, u % 2 * REP + r, :]
                        if diagonal:
                            d = out[:, end - base:end - base + P]
                            pe.matmul(d, far[:, 0, :], far[:, 1, :], start=True, stop=False)
                            mm = pe.matmul(d, q, k(end, end + P), start=False, stop=True)
                        if end > base:
                            mm = pe.matmul(out[:, 0:end - base], q, k(base, end), start=True, stop=True)
                    mm.then_inc(sc_done, 1)

            def maxima_rows(b):
                for i in range(NB):
                    mm = pe.transpose(m.bank[0:H1, 2 * b + i // 4, (i % 4) * P:(i % 4 + 1) * P], mx[:, b, i, :], m.ident[:, :])
                mm.then_inc(turned, 1)

            def scores(b, g, n):
                th, i = WU[n]
                k = ks[b][:, bass.ds(g, 1), i * P:(i + 1) * P].squeeze(1)
                base, lo = th * TT, max(i * P, th * TT)
                for slot in range(2):
                    part = 2 * n + slot
                    pe.wait_ge(exp_done, (b * HKV + g) * 2 * NWU + part + 1)
                    for h in range(2):
                        q = lambda lo, hi: qs[:, bass.ds(g * REP + 2 * slot + h, 1), lo:hi].squeeze(1)
                        out, at = m.bank[:, part % RING * 2 + h, :], lo
                        if i * P >= base:
                            d = out[:, lo - base:lo - base + P]
                            pe.matmul(d, far[:, 0, :], far[:, 2, :], start=True, stop=False)
                            mm = pe.matmul(d, k, q(lo, lo + P), start=False, stop=True)
                            at += P
                        if at < base + TT:
                            mm = pe.matmul(out[:, at - base:TT], k, q(at, base + TT), start=True, stop=True)
                    mm.then_inc(st_done, 1)

            def values(b, g, n):
                th, i = WU[n]
                G = b * HKV + g
                if n == 0:
                    pe.wait_ge(vg_done, G + 1)
                if i == 0:
                    pe.wait_ge(out_free, 2 * G + th + 1)
                pe.wait_ge(exp_done, G * (2 * NWU) + 2 * n + 2 + RING)
                at = max(i * P - th * TT, 0)
                last = i == (th + 1) * 4 - 1
                for r in range(REP):
                    mm = pe.matmul(m.bank[32 * r:32 * r + 32, OUT + th, at:TT], vg[:, i, :], pexp[:, n % 2, r, at:TT],
                                   start=(i == 0), stop=last, skip_group_check=True)
                mm.then_inc(pv_done, 1)

            def turn(b, g, th):
                pe.wait_ge(ob_done, 2 * (b * HKV + g) + th + 1)
                for j in range(4):
                    mm = pe.transpose(m.bank[:, OUT + th, j * P:(j + 1) * P], ob[:, th, j * P:(j + 1) * P], m.ident[:, :])
                mm.then_inc(ob_turned, 1)

            def steps(b, g, ns, last=False):
                for n in ns:
                    if n + 1 < NWU:
                        scores(b, g, n + 1)
                    elif not last:
                        scores(b, g + 1, 0)
                    values(b, g, n)
                    if n == 6:
                        turn(b, g, 0)

            with pe.Fori(0, GA) as g:
                maxima(0, g)
            pe.wait_ge(second_loaded, SECOND * 16)
            with pe.Fori(GA, HKV) as g:
                maxima(0, g)
            pe.wait_ge(rest_loaded, REST * 16)
            with pe.Fori(0, HKV) as g:
                maxima(1, g)
            pe.wait_ge(max_joined, B)
            for b in range(B):
                maxima_rows(b)
            pe.wait_ge(mlo, 4)
            pe.wait_ge(m_loaded, 32)
            for b in range(B):
                scores(b, 0, 0)
                steps(b, 0, range(AHEAD))
                with pe.Fori(0, HKV - 1) as g:
                    steps(b, g, range(AHEAD, NWU))
                    steps(b, g + 1, range(AHEAD))
                    turn(b, g, 1)
                steps(b, HKV - 1, range(AHEAD, NWU), last=True)
                turn(b, HKV - 1, 1)

        @block.scalar
        def _(act):
            for b in range(B):
                act.wait_ge(turned, b + 1)
                for i in range(2):
                    act.activation(mh[:, b, 0, i * TT:(i + 1) * TT], m.bank[0:H1, 2 * b + i, :], ACT.Copy,
                                   scale=-1.0 / QS).then_inc(mhi, 1)
            for b in range(B):
                with act.Fori(0, HKV) as g:
                    for n, (th, i) in enumerate(WU):
                        G = b * HKV + g
                        at = max(i * P - th * TT, 0)
                        for slot in range(2):
                            part = 2 * n + slot
                            act.wait_ge(st_done, G * (2 * NWU) + part + 1)
                            act.wait_ge(pv_done, G * NWU + n + 1)
                            act.activation(pexp[:, n % 2, 2 * slot:2 * slot + 2, at:TT],
                                           m.bank[:, part % RING * 2:part % RING * 2 + 2, at:TT], ACT.Exp,
                                           scale=1.0 / (QS * QS * HD ** 0.5)).then_inc(exp_done, 1)

        @block.vector
        def _(dve):
            dve.sem_inc(out_free, 2)
            dve.sem_inc(max_done, 2)
            dve.sem_inc(exp_done, RING)
            dve.sem_inc(pv_done, 2)
            for b in range(B):
                other = 64 * (1 - b)
                dve.memset(ks[b][other:other + 64, :, :], 0.0).then_inc(zeros_set, 1)
            for b in range(B):
                with dve.Fori(0, HKV) as g:
                    for u, (i, s) in enumerate(MU):
                        dve.wait_ge(sc_done, (b * HKV + g) * NMU + u + 1)
                        to = mx[:, b, i] if s == 0 else mx2[:, b, i - NB // 2]
                        n = min((i + 1) * P, (s + 1) * TT) - s * TT
                        dve.tensor_reduce(to[:, bass.ds(g * REP, REP)], m.bank[:, u % 2 * REP:(u % 2 + 1) * REP, 0:n],
                                          AX.X, ALU.max).then_inc(max_done, 1)
                dve.wait_ge(max_done, (b + 1) * HKV * NMU + 2)
                late = mx[:, b, NB // 2:NB]
                dve.tensor_tensor(late, late, mx2[:, b], ALU.max).then_inc(max_joined, 1)
            for b in range(B):
                for i in range(2):
                    dve.wait_ge(mhi, 2 * b + i + 1)
                    dve.scalar_tensor_tensor(mh[:, b, 1, i * TT:(i + 1) * TT], m.bank[0:H1, 2 * b + i, :], -1.0 / QS,
                                             mh[:, b, 0, i * TT:(i + 1) * TT], ALU.mult, ALU.subtract).then_inc(mlo, 1)
            for b in range(B):
                with dve.Fori(0, HKV) as g:
                    for th in range(2):
                        G = b * HKV + g
                        n = 2 * G + th + 1
                        dve.wait_ge(pv_done, G * NWU + (4 if th == 0 else NWU) + 2)
                        dve.tensor_copy(ob[:, th, :], m.bank[:, OUT + th, :]).then_inc(ob_done, 1)
                        dve.wait_ge(ob_turned, n)
                        o = m.bank[:, OUT + th, :].rearrange("p (j r e) -> p j r e", r=REP, e=2 * HD)
                        dve.reciprocal(rec[:, th], o[:, :, :, HD]).then_inc(rec_done, 1)
                        dve.wait_ge(rec_done, n)
                        y = m.y[:, b * NB + th * 4:b * NB + th * 4 + 4, bass.ds(g * REP * HD, REP * HD)]
                        dve.tensor_tensor(y.rearrange("p j (r e) -> p j r e", e=HD), o[:, :, :, 0:HD],
                                          rec[:, th].unsqueeze(3).broadcast_to([P, 4, REP, HD]), ALU.mult).then_inc(out_free, 1)


def project_out(nc, m):
    ctx = ExitStack()
    with ctx:
        sb = lambda name, shape, dt=F32: ctx.enter_context(nc.sbuf_tensor("po_" + name, shape, dt))
        stage = sb("stage", [P, DC, D])
        w_hi = sb("w_hi", [P, DC, D], F16)
        w_lo = sb("w_lo", [P, DC, D], F16)
        yh = sb("yh", [P, DC, TT], F16)
        yl = sb("yl", [P, DC, TT], F16)
        s = sb("s", [P, 2, TT])
        gate = sb("gate", [P, NT, DC, TT])
        gate_loaded = [m.sem(f"po_gate_loaded{t}") for t in range(NT)]
        loaded, whi, wlo = m.sem("po_loaded"), m.sem("po_whi"), m.sem("po_wlo")
        turned, hi_done, lo_done = m.sem("po_turned"), m.sem("po_hi_done"), m.sem("po_lo_done")
        o_mm, scaled, added, stored = (m.sem("po_" + n) for n in ("o_mm", "scaled", "added", "stored"))
        block = ctx.enter_context(nc.Block())

        @block.sync
        def _(sp):
            sp.dma_start(stage[:, :, :], m.d["woT"].rearrange("(c p) n -> p c n", p=P)).then_inc(loaded, 16)
            for t in range(NT):
                sp.dma_start(gate[:, t], m.f_dram[:, :, t * TT:(t + 1) * TT]).then_inc(gate_loaded[t], 16)
            for t in range(NT):
                sp.wait_ge(added, DC * (t + 1))
                tok = slice(t * TT, (t + 1) * TT)
                sp.dma_start(m.outT[:, tok].rearrange("(c p) n -> p c n", p=P), m.x[:, :, tok]).then_inc(stored, 16)
            sp.wait_ge(stored, NT * 16)

        @block.scalar
        def _(act):
            act.wait_ge(loaded, 16)
            act.activation(w_hi[:, :, :], stage[:, :, :], ACT.Copy, scale=WS).then_inc(whi, 1)
            for t in range(NT):
                for c in range(DC):
                    act.wait_ge(turned, t * DC + c + 1)
                    if t:
                        act.wait_ge(o_mm, t * DC)
                    act.activation(yh[:, c, :], m.bank[:, c, :], ACT.Copy, scale=YS).then_inc(hi_done, 1)

        @block.vector
        def _(dve):
            dve.wait_ge(whi, 1)
            dve.scalar_tensor_tensor(w_lo[:, :, :], stage[:, :, :], WS, w_hi[:, :, :], ALU.mult,
                                     ALU.subtract).then_inc(wlo, 1)
            for t in range(NT):
                for c in range(DC):
                    dve.wait_ge(hi_done, t * DC + c + 1)
                    dve.scalar_tensor_tensor(yl[:, c, :], m.bank[:, c, :], YS, yh[:, c, :], ALU.mult,
                                             ALU.subtract).then_inc(lo_done, 1)
                dve.wait_ge(gate_loaded[t], 16)
                for c in range(DC):
                    n = t * DC + c
                    dve.wait_ge(o_mm, n + 1)
                    tok = slice(t * TT, (t + 1) * TT)
                    dve.scalar_tensor_tensor(s[:, c % 2, :], m.bank[:, 4 + c, :], 1.0 / (YS * WS), gate[:, t, c, :],
                                             ALU.mult, ALU.mult).then_inc(scaled, 1)
                    dve.wait_ge(scaled, n + 1)
                    dve.tensor_tensor(m.x[:, c, tok], m.x[:, c, tok], s[:, c % 2, :], ALU.add).then_inc(added, 1)

        @block.tensor
        def _(pe):
            pe.wait_ge(wlo, 1)
            for t in range(NT):
                for c in range(DC):
                    if t:
                        pe.wait_ge(lo_done, DC * (t - 1) + c + 1)
                    for j in range(4):
                        mm = pe.transpose(m.bank[:, c, j * P:(j + 1) * P], m.y[:, t * 4 + j, c * P:(c + 1) * P],
                                          m.ident[:, :])
                    mm.then_inc(turned, 1)
                pe.wait_ge(lo_done, DC * (t + 1))
                for c in range(DC):
                    if t:
                        pe.wait_ge(scaled, DC * (t - 1) + c + 1)
                    for k in range(DC):
                        mm = split_product(pe, m.bank[:, 4 + c, :], w_hi[:, k, c * P:(c + 1) * P],
                                           w_lo[:, k, c * P:(c + 1) * P], yh[:, k, :], yl[:, k, :], k == 0, k == DC - 1)
                    mm.then_inc(o_mm, 1)


def program(nc, d, outT):
    m = Shared()
    m.d, m.outT = d, outT
    with ExitStack() as ctx:
        def sb(name, shape, dt=F32, on=ctx):
            return on.enter_context(nc.sbuf_tensor("m_" + name, shape, dt))

        m.sem = lambda name: ctx.enter_context(nc.semaphore(name))
        m.bank = ctx.enter_context(nc.psum_tensor("bank", [P, 8, TT], F32))
        m.q_dram = nc.dram_tensor("q_scratch", (2, 2, 2, P, N), F16, kind="Internal").ap()
        m.k_dram = nc.dram_tensor("k_scratch", (2, 2, HKV * HH, N), F16, kind="Internal").ap()
        m.v_dram = nc.dram_tensor("v_scratch", (NJ, P, HKV * HD), F32, kind="Internal").ap()
        m.f_dram = nc.dram_tensor("f_scratch", (P, DC, N), F32, kind="Internal").ap()
        m.m_dram = nc.dram_tensor("m_scratch", (B, 2, H1, T), F16, kind="Internal").ap()
        m.x = sb("x", [P, DC, N])
        m.ident = sb("ident", [P, P])
        m.mean_ones = sb("mean_ones", [P, P])
        m.x_loaded = m.sem("x_loaded")
        m.const_loaded = m.sem("const_loaded")
        m.const_count = 3 * 16
        with ExitStack() as normed:
            m.acc = sb("acc", [P, DC, N], F32, normed)
            m.xh = sb("xh", [P, DC, N], F16, normed)
            m.xl = sb("xl", [P, DC, N], F16, normed)
            with ExitStack() as routed:
                m.gates = sb("gates", [P, N], F16, routed)
                m.sel = sb("sel", [P, EA * P], F16, routed)
                with nc.Block() as block:
                    @block.sync
                    def _(sp):
                        sp.dma_start(m.x[:, :, :], d["xT"].rearrange("(c p) n -> p c n", p=P)).then_inc(m.x_loaded, 16)
                        sp.dma_start(m.ident[:, :], d["ident"]).then_inc(m.const_loaded, 16)
                        sp.dma_start(m.mean_ones[:, :], d["mean_ones"]).then_inc(m.const_loaded, 16)
                        sp.dma_start(m.sel[:, :], d["sel"]).then_inc(m.const_loaded, 16)
                layer_norm(nc, m, "ln0")
                router(nc, m)
                experts(nc, m)
            linear_attention(nc, m)
            layer_norm(nc, m, "ln1")
            ternary_ffn(nc, m)
            project_qkv(nc, m)
        m.y = sb("y", [P, NJ, D])
        softmax_attention(nc, m)
        project_out(nc, m)


def constants():
    f = np.float32
    c = {"ident": np.eye(P, dtype=f), "mean_ones": np.full((P, P), 1.0 / D, f)}
    sel = np.zeros((P, EA, P), np.float16)
    for e in range(EA):
        sel[e, e] = sel[LO + e, e] = 1
    c["sel"] = sel.reshape(P, EA * P)
    c["block_mask"] = np.kron(np.eye(HG, dtype=f), np.ones((DK, DK), f))
    t = np.arange(T, dtype=f)[:, None]
    inv = (f(1.0) / f(10000.0) ** (np.arange(HALF, dtype=f) / f(HALF))).astype(f)
    ang = (t * inv[None, :]).astype(f)
    cos, sin = np.cos(ang).astype(f), np.sin(ang).astype(f)
    c["cos0"] = cos.reshape(NB, P, HALF).transpose(1, 0, 2)
    c["sin0"] = np.stack([-sin, sin], 1).reshape(NB, P, 2, HALF).transpose(1, 0, 2, 3)
    inv = (f(1.0) / f(10000.0) ** (np.arange(0, HD, 2, dtype=f) / f(HD))).astype(f)
    ang = (t * inv[None, :]).astype(f)
    scale = f(QS / (XS * WS))
    c["cos1"] = np.tile((np.cos(ang).astype(f) * scale).T, (P // HH, 1))
    c["sin1"] = np.tile((np.sin(ang).astype(f) * scale).T, (P // HH, 1))
    far = np.zeros((P, 3, P), np.float16)
    far[:, 0] = np.eye(P) * FAR
    far[:, 1] = np.triu(np.full((P, P), -FAR), 1)
    far[:, 2] = np.tril(np.full((P, P), -FAR), -1)
    c["far"] = far
    c["zeros"] = np.zeros(H1 * T, np.float16)
    c["units"] = np.full(HKV * T, QS, np.float16)
    return c


def layouts(i):
    t = {"xT": i["L0_attn_x"].reshape(N, D).T, "WrT": i["L0_ffn_Wr"].T,
         "br": np.broadcast_to(i["L0_ffn_br"], (P, E))}
    up = np.concatenate([i["L0_ffn_W1"], i["L0_ffn_Ws1"].reshape(SHARED, M, D)]).transpose(0, 2, 1)
    down = np.concatenate([i["L0_ffn_W2"].transpose(0, 2, 1), i["L0_ffn_Ws2"].T.reshape(SHARED, M, D)])
    up = up.reshape(NG, EG, DC, P, M).transpose(0, 3, 1, 2, 4).reshape(NG, P, EG, DC * M)
    down = down.reshape(NG, EG, MC, P, D).transpose(0, 3, 1, 2, 4).reshape(NG, P, EG, MC * D)
    t["WE"] = np.concatenate([up, down], 3).reshape(NG, P, EG * WE)
    for a in "qkvgo":
        t[a + "0"] = i[f"L0_attn_{a}w"]
    for a in "qkv":
        t[a + "b"] = i[f"L0_attn_{a}b"]
    for a in "go":
        t[a + "bT"] = i[f"L0_attn_{a}b"].reshape(DC, P).T
    t["w1T"], t["w2T"] = i["L1_ffn_w1"].T, i["L1_ffn_w2"].T
    t["b1T"], t["b2T"] = i["L1_ffn_b1"].reshape(FC, P).T, i["L1_ffn_b2"].reshape(DC, P).T
    q = i["L1_attn_wq"].reshape(2, 16, HH, 2, D).transpose(0, 3, 1, 2, 4).reshape(D, D)
    k = i["L1_attn_wk"].reshape(HKV, HH, 2, D).transpose(2, 0, 1, 3).reshape(HKV * HD, D)
    t["wqkvT"] = np.concatenate([q, k, i["L1_attn_wv"]]).T
    t["woT"] = i["L1_attn_wo"].T
    return t


def kernel(**inputs):
    import concourse.bacc as bacc
    from concourse.bass_utils import run_bass_kernel_spmd

    arrays = layouts({k: np.asarray(v) for k, v in inputs.items()}) | constants()
    arrays = {f"in_{k}": np.ascontiguousarray(v) for k, v in arrays.items()}
    nc = bacc.Bacc("TRN2", target_bir_lowering=False, num_devices=1)
    d = {
        k[3:]: nc.dram_tensor(k, v.shape, mybir.dt.from_np(v.dtype), kind="ExternalInput").ap()
        for k, v in arrays.items()}
    outT = nc.dram_tensor("outT", (D, N), F32, kind="ExternalOutput").ap()
    program(nc, d, outT)
    r = run_bass_kernel_spmd(nc, [arrays], core_ids=[0])
    return np.ascontiguousarray(r.results[0]["outT"].T).reshape(B, T, D)
```

```python
from contextlib import ExitStack

import numpy as np

import concourse.bass as bass
from concourse import mybir

F32 = mybir.dt.float32
F16 = mybir.dt.float16
ALU = mybir.AluOpType
ACT = mybir.ActivationFunctionType
AX = mybir.AxisListType

P = 128
B, T, D = 2, 1024, 512
N = B * T
DC = D // P
TT = 512
NT = N // TT
NJ = N // P
EPS = 1e-5

E, M = 32, 256
G, KG, K = 8, 4, 6
SHARED = 2
EA = E + SHARED
EG = 2
NG = EA // EG
MC = M // P
WE = DC * M + MC * D
LO = 64

SCALE_ROUTE = 2.5
XS = 16.0
WS = 64.0
GS = 64.0
HS = 1.0 / 16.0


class Shared:
    pass


def split_product(pe, out, w_hi, w_lo, x_hi, x_lo, start, stop, **kw):
    pe.matmul(out, w_hi, x_hi, start=start, stop=False, **kw)
    pe.matmul(out, w_hi, x_lo, start=False, stop=False, **kw)
    return pe.matmul(out, w_lo, x_hi, start=False, stop=stop, **kw)


def sum_magnitudes(dve, m, i):
    dve.wait_ge(m.staged, 16 * i + 16)
    dve.tensor_reduce(m.part[:, :], m.stage[:, :].rearrange("p (a b) -> p a b", a=P), AX.X, ALU.add,
                      apply_absolute_value=True).then_inc(m.parts, 1)
    dve.wait_ge(m.parts, i + 1)
    dve.tensor_reduce(m.whole[:, i:i + 1], m.part[:, :], AX.X, ALU.add).then_inc(m.summed, 1)


def layer_norm(nc, m, tag):
    ctx = ExitStack()
    with ctx:
        xc = ctx.enter_context(nc.sbuf_tensor(f"{tag}_centred", [P, NT, DC, TT], F32))
        place = m.w1[:, :, :].rearrange("p c f -> p (c f)").bitcast(F32) if tag == "ln1" else \
            m.acc[:, 0:2, :].rearrange("p c n -> p (c n)")
        sq = place.rearrange("p (a c n) -> p a c n", a=2, c=DC)
        var = ctx.enter_context(nc.sbuf_tensor(f"{tag}_var", [P, 2, TT], F32))
        root = ctx.enter_context(nc.sbuf_tensor(f"{tag}_root", [P, 2, TT], F32))
        tmp = ctx.enter_context(nc.sbuf_tensor(f"{tag}_tmp", [P, 2, TT], F32))
        rstd = ctx.enter_context(nc.sbuf_tensor(f"{tag}_rstd", [P, 2, TT], F32))
        mean_done = m.sem(f"{tag}_mean_done")
        centred = m.sem(f"{tag}_centred_done")
        squared = m.sem(f"{tag}_squared")
        var_done = m.sem(f"{tag}_var_done")
        eps_added = m.sem(f"{tag}_eps_added")
        log_done = m.sem(f"{tag}_log_done")
        root_done = m.sem(f"{tag}_root_done")
        newton = m.sem(f"{tag}_newton")
        normed = m.sem(f"{tag}_normed")
        hi_done = m.sem(f"{tag}_hi_done")
        lo_done = m.sem(f"{tag}_lo_done")
        if tag == "ln1":
            w_loaded, w_scaled, w_hi = (m.sem(f"{tag}_{n}") for n in ("w_loaded", "w_scaled", "w_hi"))
        block = ctx.enter_context(nc.Block())

        @block.tensor
        def _(pe):
            def mean(t):
                if tag == "ln0":
                    pe.wait_ge(m.x_loaded[t], 16)
                for c in range(DC):
                    mm = pe.matmul(m.bank[:, t, :], m.mean_ones[:, :],
                                   m.x[:, c, t * TT:(t + 1) * TT], start=(c == 0), stop=(c == DC - 1))
                mm.then_inc(mean_done, 1)

            def variance(t):
                pe.wait_ge(squared, t + 1)
                for c in range(DC):
                    mm = pe.matmul(m.bank[:, NT + t, :], m.mean_ones[:, :], sq[:, t % 2, c, :],
                                   start=(c == 0), stop=(c == DC - 1))
                mm.then_inc(var_done, 1)

            if tag == "ln0":
                pe.wait_ge(m.const_loaded, m.const_count)
            mean(0)
            for t in range(NT):
                if t + 1 < NT:
                    mean(t + 1)
                variance(t)

        @block.vector
        def _(dve):
            def centre(t):
                if tag == "ln0":
                    dve.wait_ge(m.x_loaded[t], 16)
                dve.wait_ge(mean_done, t + 1)
                mean = m.bank[:, t, :].unsqueeze(1).broadcast_to([P, DC, TT])
                dve.tensor_tensor(xc[:, t], m.x[:, :, t * TT:(t + 1) * TT], mean,
                                  ALU.subtract).then_inc(centred, 1)

            def add_eps(t):
                dve.wait_ge(var_done, t + 1)
                dve.tensor_scalar(var[:, t % 2], m.bank[:, NT + t, :], EPS, None, ALU.add).then_inc(eps_added, 1)

            def scale(t):
                b = t % 2
                dve.wait_ge(root_done, t + 1)
                dve.tensor_tensor(tmp[:, b], root[:, b], root[:, b], ALU.mult).then_inc(newton, 1)
                dve.wait_ge(newton, 3 * t + 1)
                dve.tensor_tensor(tmp[:, b], tmp[:, b], var[:, b], ALU.mult).then_inc(newton, 1)
                dve.wait_ge(newton, 3 * t + 2)
                dve.tensor_scalar(tmp[:, b], tmp[:, b], -0.5 * XS, 1.5 * XS, ALU.mult, ALU.add).then_inc(newton, 1)
                dve.wait_ge(newton, 3 * t + 3)
                dve.tensor_tensor(rstd[:, b], tmp[:, b], root[:, b], ALU.mult).then_inc(normed, 1)
                dve.wait_ge(normed, 2 * t + 1)
                dve.wait_ge(squared, t + 1)
                dve.tensor_tensor(xc[:, t], xc[:, t], rstd[:, b].unsqueeze(1).broadcast_to([P, DC, TT]),
                                  ALU.mult).then_inc(normed, 1)

            centre(0)
            centre(1)
            for t in range(NT):
                add_eps(t)
                if t + 2 < NT:
                    centre(t + 2)
                scale(t)
            if tag == "ln1":
                sum_magnitudes(dve, m, 0)

        if tag == "ln1":
            @block.sync
            def _(sp):
                sp.dma_start(m.wqkv[:, :, :], m.d["wqkvT"].rearrange("(c p) n -> p c n", p=P)).then_inc(w_loaded, 16)
                sp.dma_start(m.stage[:, :].rearrange("p (c f) -> p c f", c=DC),
                             m.d["w1T"].rearrange("(c p) f -> p c f", p=P)).then_inc(m.staged, 16)

        @block.scalar
        def _(act):
            def square(t):
                act.wait_ge(centred, t + 1)
                if t >= 2:
                    act.wait_ge(var_done, t - 1)
                act.activation(sq[:, t % 2], xc[:, t], ACT.Square).then_inc(squared, 1)

            def high(t):
                act.wait_ge(normed, 2 * t + 2)
                act.activation(m.xh[:, :, t * TT:(t + 1) * TT], xc[:, t], ACT.Copy).then_inc(hi_done, 1)

            def split_wqkv():
                act.wait_ge(w_loaded, 16)
                act.activation(m.wqkv[:, :, :], m.wqkv[:, :, :], ACT.Copy, scale=WS).then_inc(w_scaled, 1)
                act.wait_ge(w_scaled, 1)
                act.activation(m.wqkv_hi[:, :, :], m.wqkv[:, :, :], ACT.Copy).then_inc(w_hi, 1)

            square(0)
            square(1)
            for t in range(NT):
                act.wait_ge(eps_added, t + 1)
                if t >= 2:
                    act.wait_ge(normed, 2 * (t - 2) + 1)
                act.activation(root[:, t % 2], var[:, t % 2], ACT.Ln).then_inc(log_done, 1)
                act.wait_ge(log_done, t + 1)
                act.activation(root[:, t % 2], root[:, t % 2], ACT.Exp, scale=-0.5).then_inc(root_done, 1)
                if t + 2 < NT:
                    square(t + 2)
                if t:
                    high(t - 1)
                if t == 2 and tag == "ln1":
                    split_wqkv()
            high(NT - 1)

        @block.gpsimd
        def _(pool):
            for t in range(NT):
                if t == 2 and tag == "ln1":
                    pool.wait_ge(w_hi, 1)
                    pool.tensor_tensor(m.wqkv_lo[:, :, :], m.wqkv[:, :, :], m.wqkv_hi[:, :, :], ALU.subtract)
                pool.wait_ge(hi_done, t + 1)
                tile = m.xh[:, :, t * TT:(t + 1) * TT]
                pool.tensor_tensor(m.xl[:, :, t * TT:(t + 1) * TT], xc[:, t], tile,
                                   ALU.subtract).then_inc(lo_done, 1)


def router(nc, m):
    ctx = ExitStack()
    with ctx:
        sb = lambda name, shape, dt=F32: ctx.enter_context(nc.sbuf_tensor("rt_" + name, shape, dt))
        wr = sb("wr", [P, DC, E])
        wr_hi = sb("wr_hi", [P, DC, E], F16)
        wr_lo = sb("wr_lo", [P, DC, E], F16)
        br = sb("br", [P, E])
        logit = sb("logit", [P, NJ, E])
        s = sb("s", [P, NJ, E])
        pair = sb("pair", [P, 4, NJ, G])
        gw = sb("gw", [P, NJ, G + 4])
        top = sb("top", [P, NJ, 8])
        kept = sb("kept", [P, NJ, G])
        mx = sb("mx", [P, NJ, E + 2])
        gate = sb("gate", [P, NJ, EA])
        total = sb("total", [P, NJ])
        loaded = m.sem("rt_loaded")
        split = m.sem("rt_split")
        ex_hi = m.sem("rt_ex_hi")
        logits_done = m.sem("rt_logits_done")
        step = m.sem("rt_step")
        sig = m.sem("rt_sig")
        gate_done = m.sem("rt_gate_done")
        turned = m.sem("rt_turned")
        gate_hi = m.sem("rt_gate_hi")
        gate_zero = m.sem("rt_gate_zero")
        block = ctx.enter_context(nc.Block())

        @block.sync
        def _(sp):
            sp.dma_start(wr[:, :, :], m.d["WrT"].rearrange("(c p) e -> p c e", p=P)).then_inc(loaded, 16)
            sp.dma_start(br[:, :], m.d["br"]).then_inc(loaded, 16)

        @block.gpsimd
        def _(pool):
            pool.memset(m.gates[:, :], 0.0).then_inc(gate_zero, 1)
            pool.memset(m.acc[:, :, :], 0.0)

        @block.scalar
        def _(act):
            act.wait_ge(loaded, 32)
            act.activation(wr_hi[:, :, :], wr[:, :, :], ACT.Copy, scale=WS).then_inc(split, 1)
            act.wait_ge(m.ex_staged, 32)
            for i in range(NT):
                piece = slice(i * EG * WE // NT, (i + 1) * EG * WE // NT)
                act.activation(m.ex_hi[:, 0, piece], m.ex_stage[:, 0, piece], ACT.Copy, scale=WS).then_inc(ex_hi, 1)
            act.wait_ge(step, 1)
            act.activation(s[:, :, :], logit[:, :, :], ACT.Sigmoid).then_inc(sig, 1)
            act.wait_ge(gate_zero, 1)
            for t in range(NT):
                act.wait_ge(turned, 4 * (t + 1))
                act.activation(m.gates[0:EA, t * TT:(t + 1) * TT], m.bank[0:EA, 1 + t, :],
                               ACT.Copy).then_inc(gate_hi, 1)

        @block.tensor
        def _(pe):
            pe.wait_ge(split, 2)
            for j in range(NJ):
                for c in range(DC):
                    xh, xl = (v[:, c, j * P:(j + 1) * P] for v in (m.xh, m.xl))
                    mm = split_product(pe, m.bank[:, 0, j * E:(j + 1) * E], xh, xl, wr_hi[:, c, :],
                                       wr_lo[:, c, :], c == 0, c == DC - 1)
            mm.then_inc(logits_done, 1)
            pe.wait_ge(gate_done, 1)
            for j in range(NJ):
                pe.transpose(m.bank[0:EA, 1 + j // 4, (j % 4) * P:(j % 4 + 1) * P], gate[:, j, :],
                             m.ident[:, :]).then_inc(turned, 1)

        @block.vector
        def _(dve):
            n = [0]

            def then(ins):
                n[0] += 1
                ins.then_inc(step, 1)
                dve.wait_ge(step, n[0])

            dve.wait_ge(loaded, 32)
            dve.wait_ge(split, 1)
            dve.scalar_tensor_tensor(wr_lo[:, :, :], wr[:, :, :], WS, wr_hi[:, :, :], ALU.mult,
                                     ALU.subtract).then_inc(split, 1)
            for i in range(4):
                dve.memset(gw[:, :, G + i], -2.0 - i)
            for i in range(2):
                dve.memset(mx[:, :, E + i], -2.0 - i)
            dve.memset(gate[:, :, E:EA], GS)
            for i in range(NT):
                piece = slice(i * EG * WE // NT, (i + 1) * EG * WE // NT)
                dve.wait_ge(ex_hi, i + 1)
                dve.scalar_tensor_tensor(m.ex_lo[:, 0, piece], m.ex_stage[:, 0, piece], WS, m.ex_hi[:, 0, piece],
                                         ALU.mult, ALU.subtract)
            dve.wait_ge(logits_done, 1)
            then(dve.scalar_tensor_tensor(
                logit[:, :, :], m.bank[:, 0, :].rearrange("p (j e) -> p j e", e=E), 1.0 / (XS * WS),
                br[:, :].unsqueeze(1).broadcast_to([P, NJ, E]), ALU.mult, ALU.add))
            dve.wait_ge(sig, 1)
            q = s[:, :, :].rearrange("p j (g i) -> p j g i", i=4)
            dve.tensor_tensor(pair[:, 0], q[:, :, :, 0], q[:, :, :, 1], ALU.add)
            dve.tensor_tensor(pair[:, 1], q[:, :, :, 2], q[:, :, :, 3], ALU.add)
            dve.tensor_tensor(pair[:, 2], q[:, :, :, 0], q[:, :, :, 1], ALU.max)
            then(dve.tensor_tensor(pair[:, 3], q[:, :, :, 2], q[:, :, :, 3], ALU.max))
            then(dve.tensor_tensor(pair[:, 0], pair[:, 0], pair[:, 1], ALU.max))
            then(dve.tensor_tensor(pair[:, 2], pair[:, 2], pair[:, 3], ALU.add))
            then(dve.tensor_tensor(gw[:, :, 0:G], pair[:, 0], pair[:, 2], ALU.max))
            for j in range(NJ):
                last = dve.max(top[:, j, :], gw[:, j, :])
            then(last)
            for i in range(4):
                last = dve.memset(top[:, :, KG + i], -2.0 - i)
            then(last)
            for j in range(NJ):
                last = dve.match_replace(gw[:, j, :], top[:, j, :], gw[:, j, :], -9.0)
            then(last)
            then(dve.tensor_scalar(kept[:, :, :], gw[:, :, 0:G], -9.0, None, ALU.is_equal))
            then(dve.tensor_tensor(mx[:, :, 0:E].rearrange("p j (g i) -> p j g i", i=4), q,
                                   kept[:, :, :].unsqueeze(3).broadcast_to([P, NJ, G, 4]), ALU.mult))
            for j in range(NJ):
                last = dve.max(top[:, j, :], mx[:, j, :])
            then(last)
            for i in range(2):
                last = dve.memset(top[:, :, K + i], -2.0 - i)
            then(last)
            for j in range(NJ):
                last = dve.match_replace(mx[:, j, :], top[:, j, :], mx[:, j, :], -9.0)
            then(last)
            then(dve.tensor_scalar(mx[:, :, 0:E], mx[:, :, 0:E], -9.0, None, ALU.is_equal))
            then(dve.tensor_tensor(s[:, :, :], s[:, :, :], mx[:, :, 0:E], ALU.mult))
            then(dve.tensor_reduce(total[:, :], s[:, :, :], AX.X, ALU.add))
            then(dve.tensor_scalar(total[:, :], total[:, :], 1e-20, None, ALU.add))
            then(dve.reciprocal(total[:, :], total[:, :]))
            then(dve.tensor_scalar(total[:, :], total[:, :], SCALE_ROUTE * GS, None, ALU.mult))
            dve.tensor_tensor(gate[:, :, 0:E], s[:, :, :],
                              total[:, :].unsqueeze(2).broadcast_to([P, NJ, E]), ALU.mult).then_inc(gate_done, 1)
            for t in range(NT):
                dve.wait_ge(gate_hi, t + 1)
                dve.tensor_tensor(m.gates[LO:LO + EA, t * TT:(t + 1) * TT], m.bank[0:EA, 1 + t, :],
                                  m.gates[0:EA, t * TT:(t + 1) * TT], ALU.subtract)


def experts(nc, m):
    UNITS = EG * MC
    STEPS = NG * NT
    PIECE = EG * WE // NT
    ctx = ExitStack()
    with ctx:
        sb = lambda name, shape, dt=F32: ctx.enter_context(nc.sbuf_tensor("ex_" + name, shape, dt))
        stage, wh, wl = m.ex_stage, m.ex_hi, m.ex_lo
        r = sb("relu", [P, 2, TT])
        g = sb("gate", [P, 2, TT])
        hg = sb("gated", [P, 2, TT])
        hh = sb("hidden_hi", [P, UNITS, TT], F16)
        hl = sb("hidden_lo", [P, UNITS, TT], F16)
        staged = m.ex_staged
        split_hi = m.sem("ex_split_hi")
        split_lo = m.sem("ex_split_lo")
        gate_bc = m.sem("ex_gate_bc")
        gate_sb = m.sem("ex_gate_sb")
        up_done = m.sem("ex_up_done")
        relu_done = m.sem("ex_relu_done")
        gate_r = m.sem("ex_gate_r")
        gated = m.sem("ex_gated")
        hi_done = m.sem("ex_hi_done")
        lo_done = m.sem("ex_lo_done")
        hl_free = m.sem("ex_hl_free")
        acc_free = m.sem("ex_acc_free")
        H, GB, A = 0, 2, 4

        block = ctx.enter_context(nc.Block())

        @block.sync
        def _(sp):
            with sp.Fori(2, NG) as p:
                sp.wait_ge(staged, 16 * p)
                sp.wait_ge(split_lo, NT * p - NT)
                sp.wait_ge(split_hi, NT * p - NT)
                sp.dma_start(stage[:, bass.ds(p % 2, 1), :],
                             m.d["WE"][bass.ds(p, 1)].rearrange("a p w -> p a w")).then_inc(staged, 16)
            sp.wait_ge(staged, 16 * NG)

        def piece(buf, n):
            return buf[:, :, :].rearrange("p a w -> p (a w)")[:, bass.ds((n // NT + 1) % 2 * (EG * WE) + n % NT * PIECE, PIECE)]

        @block.scalar
        def _(act):
            def unit(n, u):
                k = n * UNITS + u
                if u % MC == 0:
                    e = u // MC
                    act.wait_ge(gate_bc, n * EG + e + 1)
                    act.activation(g[:, e, :], m.bank[:, GB + e, :], ACT.Copy, scale=HS / GS).then_inc(gate_sb, 1)
                act.wait_ge(up_done, k + 1)
                act.activation(r[:, u % 2, :], m.bank[:, H + u % 2, :], ACT.Relu,
                               scale=1.0 / (XS * WS)).then_inc(relu_done, 1)
                act.wait_ge(hl_free, k + 1)
                act.wait_ge(gated, k + 1)
                act.activation(hh[:, u, :], hg[:, u % 2, :], ACT.Copy).then_inc(hi_done, 1)

            with act.Fori(0, STEPS - NT) as n:
                for u in range(UNITS):
                    unit(n, u)
                    if u == 1:
                        act.wait_ge(staged, n // NT * 16 + 32)
                        act.activation(piece(wh, n), piece(stage, n), ACT.Copy, scale=WS).then_inc(split_hi, 1)
            with act.Fori(STEPS - NT, STEPS) as n:
                for u in range(UNITS):
                    unit(n, u)

        @block.vector
        def _(dve):
            dve.sem_inc(acc_free, DC)
            for split in (split_hi, split_lo):
                dve.sem_inc(split, NT)

            def unit(n, u):
                k = n * UNITS + u
                dve.wait_ge(relu_done, k + 1)
                dve.wait_ge(gate_sb, n * EG + u // MC + 1)
                dve.tensor_tensor(hg[:, u % 2, :], r[:, u % 2, :], g[:, u // MC, :], ALU.mult).then_inc(gate_r, 1)
                dve.wait_ge(gate_r, k + 1)
                dve.tensor_tensor(hg[:, u % 2, :], hg[:, u % 2, :], r[:, u % 2, :], ALU.mult).then_inc(gated, 1)
                dve.wait_ge(hi_done, k + 1)
                dve.tensor_tensor(hl[:, u, :], hg[:, u % 2, :], hh[:, u, :], ALU.subtract).then_inc(lo_done, 1)

            def split(n):
                dve.wait_ge(split_hi, n + NT + 1)
                dve.scalar_tensor_tensor(piece(wl, n), piece(stage, n), WS, piece(wh, n), ALU.mult,
                                         ALU.subtract).then_inc(split_lo, 1)

            def add_sums(n, tile):
                dve.wait_ge(hl_free, n * UNITS + 2 * UNITS)
                for c in range(DC):
                    acc = m.acc[:, c, bass.ds(tile * TT, TT)]
                    dve.scalar_tensor_tensor(acc, m.bank[:, A + c, :], 1.0 / (WS * HS), acc, ALU.mult,
                                             ALU.add).then_inc(acc_free, 1)

            unit(0, 0)
            unit(0, 1)
            with dve.Fori(0, STEPS - NT) as n:
                unit(n, 2)
                split(n)
                unit(n, 3)
                unit(n + 1, 0)
                unit(n + 1, 1)
                add_sums(n, n % NT)
            with dve.Fori(STEPS - NT, STEPS - 1) as n:
                unit(n, 2)
                unit(n, 3)
                unit(n + 1, 0)
                unit(n + 1, 1)
                add_sums(n, n % NT)
            unit(STEPS - 1, 2)
            unit(STEPS - 1, 3)
            add_sums(STEPS - 1, NT - 1)

        @block.tensor
        def _(pe):
            pe.sem_inc(hl_free, UNITS)

            def weights(buf, n, at, width):
                if isinstance(n, int):
                    return buf[:, n // NT % 2, at:at + width]
                return buf[:, :, :].rearrange("p a w -> p (a w)")[:, bass.ds(n // NT % 2 * (EG * WE) + at, width)]

            def up(n, u, first=False):
                e, c = u // MC, u % MC
                if not first:
                    pe.wait_ge(relu_done, n * UNITS + u - 1)
                if u == 0:
                    pe.wait_ge(split_lo, n // NT * NT + NT)
                tile = n % NT
                tok = bass.ds(tile * TT, TT)
                if c == 0:
                    sel = m.sel[:, bass.ds((n // NT * EG + e) * P, P)]
                    pe.matmul(m.bank[:, GB + e, :], sel, m.gates[:, tok], start=True, stop=True).then_inc(gate_bc, 1)
                for k in range(DC):
                    at = e * WE + k * M + c * P
                    mm = split_product(pe, m.bank[:, H + u % 2, :], weights(wh, n, at, P), weights(wl, n, at, P),
                                       m.xh[:, k, tok], m.xl[:, k, tok], k == 0, k == DC - 1)
                mm.then_inc(up_done, 1)

            def down(n, u):
                e, c = u // MC, u % MC
                pe.wait_ge(lo_done, n * UNITS + u + 1)
                for d in range(DC):
                    if u == 0:
                        pe.wait_ge(acc_free, n * DC + d + 1)
                    at = e * WE + DC * M + c * D + d * P
                    mm = split_product(pe, m.bank[:, A + d, :], weights(wh, n, at, P), weights(wl, n, at, P),
                                       hh[:, u, :], hl[:, u, :], u == 0, u == UNITS - 1)
                mm.then_inc(hl_free, 1)

            up(0, 0, first=True)
            up(0, 1, first=True)
            with pe.Fori(0, STEPS - 1) as n:
                up(n, 2)
                down(n, 0)
                up(n, 3)
                down(n, 1)
                up(n + 1, 0)
                down(n, 2)
                up(n + 1, 1)
                down(n, 3)
            n = STEPS - 1
            up(n, 2)
            down(n, 0)
            up(n, 3)
            down(n, 1)
            down(n, 2)
            down(n, 3)

H0, DK, CHUNK = 16, 32, 64
HALF = DK // 2
HG = P // DK
NB = T // P
TB = T // TT
AS = 4.0


def linear_attention(nc, m):
    ctx = ExitStack()
    with ctx:
        sb = lambda name, shape, dt=F32: ctx.enter_context(nc.sbuf_tensor("la_" + name, shape, dt))
        W = P + 1
        SW = P + HG
        BT = NB // TB
        f = sb("f", [P, 2, 2, D])
        wstage = [m.la_stage, f[:, :, :, :].rearrange("p a b d -> p (a b) d")]
        w_hi = sb("w_hi", [P, 5, DC, D], F16)
        w_lo = sb("w_lo", [P, 5, DC, D], F16)
        rows = sb("rows", [P, 3, D])
        cols = sb("cols", [P, 2, DC])
        cos = sb("cos", [P, NB, HALF])
        sin = sb("sin", [P, NB, 2, HALF])
        mask = sb("mask", [P, P])
        a = sb("a", [P, 2, D])
        t1 = sb("t1", [P, 2, D])
        t2 = sb("t2", [P, 2, D])
        v = sb("v", [P, 2, DC, W])
        qT = sb("qT", [P, DC, P])
        S = sb("S", [P, 2, DC, SW])
        rden = sb("rden", [P, 2, 2, HG])
        aoh = sb("aoh", [P, DC, TT], F16)
        aol = sb("aol", [P, DC, TT], F16)
        gT = sb("gT", [P, DC, T])
        s = wstage[0][:, 0:2, :]
        ao = wstage[0][:, 2, :]
        ag = wstage[0][:, 3, :].rearrange("p (c t) -> p c t", c=DC)

        loaded, w_loaded = m.sem("la_loaded"), m.la_loaded
        whi, wlo = m.sem("la_whi"), m.sem("la_wlo")
        ones_set = m.sem("la_ones")
        silu_sig, silu_done = m.sem("la_silu_sig"), [m.sem(f"la_silu_done{i}") for i in range(2)]
        g_mm, g_sig = m.sem("la_g_mm"), m.sem("la_g_sig")
        proj_qk, proj_v = m.sem("la_proj_qk"), m.sem("la_proj_v")
        qk_biased, v_biased = m.sem("la_qk_biased"), m.sem("la_v_biased")
        cos_done, sin_done, turned = m.sem("la_cos_done"), m.sem("la_sin_done"), m.sem("la_turned")
        min_done, exp_done, mapped = m.sem("la_min_done"), m.sem("la_exp_done"), m.sem("la_mapped")
        qT_mm, qT_sb = m.sem("la_qT_mm"), m.sem("la_qT_sb")
        kv_done, state_set, num_done = m.sem("la_kv_done"), m.sem("la_state_set"), m.sem("la_num_done")
        den_eps, den_inv, divided, gated = (m.sem("la_" + n) for n in ("den_eps", "den_inv", "divided", "gated"))
        ao_mm, ao_hi, ao_lo = m.sem("la_ao_mm"), m.sem("la_ao_hi"), m.sem("la_ao_lo")
        o_mm, o_biased, o_gated, x_added = (m.sem("la_" + n) for n in ("o_mm", "o_biased", "o_gated", "x_added"))
        Q, V, NUM, QT, KV = 0, 2, 3, 5, 6
        LOADS = 3 + 1 + 1 + 2 + 1
        PIECE = 2 * D
        PIECES = DC * N // PIECE
        block = ctx.enter_context(nc.Block())

        def piece(i):
            return m.acc[:, :, :].rearrange("p c n -> p (c n)")[:, i * PIECE:(i + 1) * PIECE]

        def sigmoid(i):
            return (t1, t2)[i % 2][:, :, :].rearrange("p a d -> p (a d)")

        def pieces_after(i):
            return range(max(i - 1, 0) * PIECES // 4, i * PIECES // 4)

        @block.sync
        def _(sp):
            for i, w in enumerate((m.d["g0"], m.d["q0"], m.d["k0"], m.d["v0"], m.d["o0"])):
                if i >= 2:
                    sp.wait_ge(whi, i - 1)
                    sp.wait_ge(wlo, i - 1)
                if i:
                    sp.wait_ge(w_loaded, 16 * i)
                if i:
                    sp.dma_start(wstage[i % 2][:, :, :], w.rearrange("(c p) n -> p c n", p=P)).then_inc(w_loaded, 16)
                if i == 1:
                    sp.dma_start(cols[:, 0, :], m.d["gbT"]).then_inc(loaded, 16)
                    sp.dma_start(cols[:, 1, :], m.d["obT"]).then_inc(loaded, 16)
                    for j, bias in enumerate((m.d["qb"], m.d["kb"], m.d["vb"])):
                        sp.dma_start(rows[:, j, :], bias.partition_broadcast(P)).then_inc(loaded, 16)
                    sp.dma_start(cos[:, :, :], m.d["cos0"]).then_inc(loaded, 16)
                    sp.dma_start(sin[:, :, :, :], m.d["sin0"]).then_inc(loaded, 16)
                    sp.dma_start(mask[:, :], m.d["block_mask"]).then_inc(loaded, 16)
            sp.wait_ge(w_loaded, 16 * 5)

        @block.gpsimd
        def _(pool):
            pool.memset(v[:, :, :, P:W], 1.0).then_inc(ones_set, 1)
            for i in range(0, PIECES, 2):
                pool.wait_ge(silu_sig, i + 1)
                pool.tensor_tensor(piece(i), piece(i), sigmoid(i), ALU.mult).then_inc(silu_done[0], 1)
            pool.wait_ge(loaded, 16 * LOADS)
            with pool.Fori(0, B) as b:
                def sines(j):
                    pool.wait_ge(qk_biased, b * NB + j + 1)
                    heads = a[:, :, :].rearrange("p a (h r i) -> p (a h) r i", r=2, i=HALF)
                    out = t2[:, :, :].rearrange("p a (h r i) -> p (a h) r i", r=2, i=HALF)
                    for r in range(2):
                        sn = sin[:, j, r, :].unsqueeze(1).broadcast_to([P, 2 * H0, HALF])
                        ins = pool.tensor_tensor(out[:, :, r, :], heads[:, :, 1 - r, :], sn, ALU.mult)
                    ins.then_inc(sin_done, 1)

                def low(j):
                    pool.wait_ge(ao_hi, b * NB + j + 1)
                    at = (j % BT) * P
                    pool.tensor_tensor(aol[:, :, at:at + P], ag[:, :, :], aoh[:, :, at:at + P],
                                       ALU.subtract).then_inc(ao_lo, 1)

                sines(0)
                for j in range(NB):
                    if j + 1 < NB:
                        sines(j + 1)
                    if j:
                        low(j - 1)
                low(NB - 1)

        @block.scalar
        def _(act):
            def split(i):
                act.wait_ge(w_loaded, 16 * i + 16)
                act.activation(w_hi[:, i], wstage[i % 2][:, :, :], ACT.Copy, scale=WS).then_inc(whi, 1)

            def silu(i):
                if i >= 2:
                    act.wait_ge(silu_done[i % 2], i // 2)
                act.activation(sigmoid(i), piece(i), ACT.Sigmoid).then_inc(silu_sig, 1)

            for i in range(5):
                split(i)
                for k in pieces_after(i):
                    silu(k)
            act.wait_ge(loaded, 16 * LOADS)
            with act.Fori(0, B) as b:
                def exps(j):
                    act.wait_ge(min_done, b * NB + j + 1)
                    act.activation(t2[:, :, :], t1[:, :, :], ACT.Exp).then_inc(exp_done, 1)

                def high(j):
                    act.wait_ge(gated, b * NB + j + 1)
                    at = (j % BT) * P
                    act.activation(aoh[:, :, at:at + P], ag[:, :, :], ACT.Copy).then_inc(ao_hi, 1)

                def outputs(t):
                    i = b * TB + t
                    for c in range(DC):
                        act.wait_ge(o_mm, i * DC + c + 1)
                        if c >= 2:
                            act.wait_ge(x_added, i * DC + c - 1)
                        act.activation(s[:, c % 2, :], m.bank[:, c % 2, :], ACT.Identity, bias=cols[:, 1, c:c + 1],
                                       scale=1.0 / (AS * WS)).then_inc(o_biased, 1)

                for n in range(TB * DC):
                    t, c = n // DC, n % DC
                    act.wait_ge(g_mm, b * TB * DC + n + 1)
                    act.activation(gT[:, c, t * TT:(t + 1) * TT], m.bank[:, n, :], ACT.Sigmoid,
                                   bias=cols[:, 0, c:c + 1], scale=1.0 / (XS * WS)).then_inc(g_sig, 1)
                exps(0)
                for j in range(NB):
                    act.wait_ge(qT_mm, b * NB + j + 1)
                    act.activation(qT[:, :, :], m.bank[:, QT, :].rearrange("p (c t) -> p c t", c=DC),
                                   ACT.Copy).then_inc(qT_sb, 1)
                    if j:
                        high(j - 1)
                    if j + 1 < NB:
                        exps(j + 1)
                    if j and j % BT == 0:
                        outputs(j // BT - 1)
                high(NB - 1)
                outputs(TB - 1)

        @block.vector
        def _(dve):
            for i in range(5):
                dve.wait_ge(whi, i + 1)
                dve.scalar_tensor_tensor(w_lo[:, i], wstage[i % 2][:, :, :], WS, w_hi[:, i], ALU.mult,
                                         ALU.subtract).then_inc(wlo, 1)
                for k in pieces_after(i):
                    if k % 2:
                        dve.wait_ge(silu_sig, k + 1)
                        dve.tensor_tensor(piece(k), piece(k), sigmoid(k), ALU.mult).then_inc(silu_done[1], 1)
            dve.wait_ge(loaded, 16 * LOADS)
            for done in silu_done:
                dve.wait_ge(done, PIECES // 2)
            with dve.Fori(0, B) as b:
                at = lambda j: b * NB + j + 1

                def bias_qk(j):
                    dve.wait_ge(proj_qk, at(j))
                    if j:
                        dve.wait_ge(mapped, at(j - 1))
                    dve.scalar_tensor_tensor(a[:, :, :], m.bank[:, Q:Q + 2, :], 1.0 / (XS * WS), rows[:, 0:2, :],
                                             ALU.mult, ALU.add).then_inc(qk_biased, 1)
                    dve.wait_ge(qk_biased, at(j))
                    cs = cos[:, j, :].unsqueeze(1).broadcast_to([P, 4 * H0, HALF])
                    dve.tensor_tensor(t1[:, :, :].rearrange("p a (h i) -> p (a h) i", i=HALF),
                                      a[:, :, :].rearrange("p a (h i) -> p (a h) i", i=HALF), cs,
                                      ALU.mult).then_inc(cos_done, 1)

                def bias_v(j):
                    dve.wait_ge(proj_v, at(j))
                    chunks = lambda x: x.rearrange("p (c e) -> p c e", c=DC)
                    dve.scalar_tensor_tensor(v[:, j % 2, :, 0:P], chunks(m.bank[:, V, :]), 1.0 / (XS * WS),
                                             chunks(rows[:, 2, :]), ALU.mult, ALU.add).then_inc(v_biased, 1)

                def turn(j):
                    dve.wait_ge(cos_done, at(j))
                    dve.wait_ge(sin_done, at(j))
                    dve.tensor_tensor(a[:, :, :], t1[:, :, :], t2[:, :, :], ALU.add).then_inc(turned, 1)
                    dve.wait_ge(turned, at(j))
                    dve.tensor_scalar(t1[:, :, :], a[:, :, :], 0.0, None, ALU.min).then_inc(min_done, 1)

                def map_qk(j):
                    dve.wait_ge(exp_done, at(j))
                    dve.scalar_tensor_tensor(f[:, j % 2], a[:, :, :], 0.0, t2[:, :, :], ALU.max,
                                             ALU.add).then_inc(mapped, 1)

                def state(j, h):
                    n = 2 * j + h
                    dve.wait_ge(kv_done, b * 2 * NB + n + 1)
                    sums = m.bank[:, KV:KV + 2, 0:2 * W].rearrange("p b (c e) -> p b c e", e=W)
                    to = S[:, h].rearrange("p (b c) e -> p b c e", b=2)
                    heads = mask[:, :].rearrange("p (h e) -> p h e", e=DK)[:, :, 0]
                    dve.tensor_tensor(to[:, :, :, 0:P], sums[:, :, :, 0:P],
                                      mask[:, :].unsqueeze(1).unsqueeze(1).broadcast_to([P, 2, 2, P]), ALU.mult)
                    dve.tensor_tensor(to[:, :, :, P:SW], sums[:, :, :, P:W].broadcast_to([P, 2, 2, HG]),
                                      heads.unsqueeze(1).unsqueeze(1).broadcast_to([P, 2, 2, HG]),
                                      ALU.mult).then_inc(state_set, 1)

                def divide(j):
                    dve.wait_ge(num_done, b * 2 * NB + 2 * j + 2)
                    out = m.bank[:, NUM:NUM + 2, 0:2 * SW].rearrange("p b (c e) -> p b c e", e=SW)
                    dve.tensor_scalar(rden[:, :, :, :], out[:, :, :, P:SW], 1e-6, None, ALU.add).then_inc(den_eps, 1)
                    dve.wait_ge(den_eps, at(j))
                    dve.reciprocal(rden[:, :, :, :], rden[:, :, :, :]).then_inc(den_inv, 1)
                    dve.wait_ge(den_inv, at(j))
                    to = ao[:, :].rearrange("p (b c h e) -> p b c h e", b=2, c=2, h=HG)
                    for i in range(2):
                        ins = dve.scalar_tensor_tensor(
                            to[:, i], out[:, i, :, 0:P].rearrange("p c (h e) -> p c h e", h=HG), AS,
                            rden[:, i].unsqueeze(3).broadcast_to([P, 2, HG, DK]), ALU.mult, ALU.mult)
                    ins.then_inc(divided, 1)

                def gate(j):
                    dve.wait_ge(ao_mm, at(j))
                    if j:
                        dve.wait_ge(ao_lo, at(j - 1))
                    dve.tensor_tensor(ag[:, :, :], m.bank[:, QT, :].rearrange("p (c t) -> p c t", c=DC),
                                      gT[:, :, j * P:(j + 1) * P], ALU.mult).then_inc(gated, 1)

                def add_x(t):
                    i = b * TB + t
                    for c in range(DC):
                        tok = bass.ds(i * TT, TT)
                        dve.wait_ge(o_biased, i * DC + c + 1)
                        dve.tensor_tensor(s[:, c % 2, :], s[:, c % 2, :], m.acc[:, c, tok], ALU.mult).then_inc(o_gated, 1)
                        dve.wait_ge(o_gated, i * DC + c + 1)
                        dve.tensor_tensor(m.x[:, c, tok], m.x[:, c, tok], s[:, c % 2, :], ALU.add).then_inc(x_added, 1)

                bias_qk(0)
                bias_v(0)
                turn(0)
                map_qk(0)
                for j in range(NB):
                    if j + 1 < NB:
                        bias_qk(j + 1)
                    state(j, 0)
                    if j:
                        gate(j - 1)
                    state(j, 1)
                    if j + 1 < NB:
                        turn(j + 1)
                        bias_v(j + 1)
                        map_qk(j + 1)
                    divide(j)
                    if j and j % BT == 0:
                        add_x(j // BT - 1)
                gate(NB - 1)
                add_x(TB - 1)

        @block.tensor
        def _(pe):
            pe.wait_ge(ones_set, 1)
            with pe.Fori(0, B) as b:
                at = lambda j: b * NB + j + 1

                def project(j, ws, chunks=range(DC)):
                    tok = bass.ds((b * NB + j) * P, P)
                    for w in ws:
                        if j and 0 in chunks:
                            pe.wait_ge(v_biased if w == 2 else qk_biased, at(j - 1))
                        for c in chunks:
                            mm = split_product(pe, m.bank[:, Q + w, :], m.xh[:, c, tok], m.xl[:, c, tok],
                                               w_hi[:, 1 + w, c, :], w_lo[:, 1 + w, c, :], c == 0, c == DC - 1)
                        if w and DC - 1 in chunks:
                            mm.then_inc(proj_qk if w == 1 else proj_v, 1)

                def turn_q(j):
                    pe.wait_ge(mapped, at(j))
                    if j >= 2:
                        pe.wait_ge(gated, at(j - 2))
                    for c in range(DC):
                        mm = pe.transpose(m.bank[:, QT, c * P:(c + 1) * P], f[:, j % 2, 0, c * P:(c + 1) * P],
                                          m.ident[:, :])
                    mm.then_inc(qT_mm, 1)

                def outer(j, h):
                    n = 2 * j + h
                    if n:
                        pe.wait_ge(state_set, b * 2 * NB + n)
                    lo, hi = h * CHUNK, (h + 1) * CHUNK
                    for c in range(DC):
                        mm = pe.matmul(m.bank[:, KV + c // 2, c % 2 * W:(c % 2 + 1) * W],
                                       f[lo:hi, j % 2, 1, c * P:(c + 1) * P], v[lo:hi, j % 2, c, :],
                                       start=(n == 0 and c % 2 == 0), stop=True, skip_group_check=True)
                    mm.then_inc(kv_done, 1)

                def outputs(j, h):
                    pe.wait_ge(state_set, b * 2 * NB + 2 * j + h + 1)
                    for c in range(DC):
                        lo, hi = h * CHUNK, (h + 1) * CHUNK
                        mm = pe.matmul(m.bank[lo:hi, NUM + c // 2, c % 2 * SW:(c % 2 + 1) * SW], qT[:, c, lo:hi],
                                       S[:, h, c, :], start=True, stop=True)
                    mm.then_inc(num_done, 1)

                def turn_outputs(j):
                    pe.wait_ge(divided, at(j))
                    pe.wait_ge(qT_sb, at(min(j + 1, NB - 1)))
                    for c in range(DC):
                        mm = pe.transpose(m.bank[:, QT, c * P:(c + 1) * P], ao[:, c * P:(c + 1) * P], m.ident[:, :])
                    mm.then_inc(ao_mm, 1)

                def project_out(t):
                    i = b * TB + t
                    pe.wait_ge(wlo, 5)
                    pe.wait_ge(ao_lo, at(t * BT + BT - 1))
                    pe.wait_ge(qk_biased, at(min(t * BT + BT + 1, NB - 1)))
                    for c in range(DC):
                        if c >= 2:
                            pe.wait_ge(o_biased, i * DC + c - 1)
                        for k in range(DC):
                            mm = split_product(pe, m.bank[:, c % 2, :], w_hi[:, 4, k, c * P:(c + 1) * P],
                                               w_lo[:, 4, k, c * P:(c + 1) * P], aoh[:, k, :], aol[:, k, :],
                                               k == 0, k == DC - 1)
                        mm.then_inc(o_mm, 1)
                    pe.wait_ge(o_biased, i * DC + DC)

                pe.wait_ge(wlo, 1)
                for n in range(TB * DC):
                    t, c = n // DC, n % DC
                    tok = bass.ds(b * T + t * TT, TT)
                    for k in range(DC):
                        mm = split_product(pe, m.bank[:, n, :], w_hi[:, 0, k, c * P:(c + 1) * P],
                                           w_lo[:, 0, k, c * P:(c + 1) * P], m.xh[:, k, tok], m.xl[:, k, tok],
                                           k == 0, k == DC - 1)
                    mm.then_inc(g_mm, 1)
                pe.wait_ge(g_sig, b * TB * DC + TB * DC)
                pe.wait_ge(wlo, 4)
                project(0, range(3))
                for j in range(NB):
                    if j + 1 < NB:
                        project(j + 1, (0, 1))
                    turn_q(j)
                    pe.wait_ge(v_biased, at(j))
                    outer(j, 0)
                    if j:
                        turn_outputs(j - 1)
                    if j + 1 < NB:
                        project(j + 1, (2,), range(DC // 2))
                    outer(j, 1)
                    if j + 1 < NB:
                        project(j + 1, (2,), range(DC // 2, DC))
                    if j:
                        pe.wait_ge(divided, at(j - 1))
                    pe.wait_ge(qT_sb, at(j))
                    outputs(j, 0)
                    outputs(j, 1)
                    if j and j % BT == 0:
                        project_out(j // BT - 1)
                turn_outputs(NB - 1)
                project_out(TB - 1)

F = 2048
FC = F // P
TERNARY = 0.7
H1, HKV, HD = 32, 8, 16
REP = H1 // HKV
HH = HD // 2
QS = 16.0
YS = 16.0
WN = D + 2 * HKV * HD
STACK = 3 * HD
FAR = 60000.0


def project_qkv(nc, m):
    ctx = ExitStack()
    with ctx:
        sb = lambda name, shape, dt=F32: ctx.enter_context(nc.sbuf_tensor("pj_" + name, shape, dt))
        w_hi, w_lo = m.wqkv_hi, m.wqkv_lo
        cos = sb("cos", [P, T])
        sin = sb("sin", [P, T])
        t1 = sb("t1", [P, 2, 4, TT])
        ev = sb("ev", [P, 2, 2, TT])
        pr = sb("pr", [P, 2, 2, 2, TT], F16)
        v = sb("v", [P, 2, 4, P])
        loaded = m.sem("pj_loaded")
        proj, mults, turned, hi_done, lo_done = (m.sem("pj_" + n) for n in ("proj", "mults", "turned", "hi_done", "lo_done"))
        stored = [m.sem("pj_stored0"), m.sem("pj_stored1")]
        thr = sb("thr", [P, 2, 2])
        total, thr_done = m.sem("pj_total"), m.sem("pj_thr_done")
        below, ternary = m.sem("pj_below"), m.sem("pj_ternary")
        v_mm, v_sb, v_stored = m.sem("pj_v_mm"), m.sem("pj_v_sb"), m.sem("pj_v_stored")
        UN = NT * 3
        units = [(t, w) for t in range(NT) for w in range(3)]
        QP = 4
        W2_STAGED, W2_FROM = QP - 1, 7
        block = ctx.enter_context(nc.Block())

        @block.sync
        def _(sp):
            sp.dma_start(cos[:, :], m.d["cos1"]).then_inc(loaded, 16)
            sp.dma_start(sin[:, :], m.d["sin1"]).then_inc(loaded, 16)
            for n, (t, w) in enumerate(units):
                if n == W2_STAGED:
                    sp.wait_ge(ternary, QP)
                    sp.dma_start(m.stage[:, :].rearrange("p (c d) -> p c d", d=D),
                                 m.d["w2T"].rearrange("(c p) d -> p c d", p=P)).then_inc(m.staged, 16)
                sp.wait_ge(lo_done, n + 1)
                rows = P if w < 2 else P // 2
                dst = (m.q_dram[w] if w < 2 else m.k_dram)[:, :, :, t * TT:(t + 1) * TT]
                sp.dma_start(dst.rearrange("a b p n -> p a b n"), pr[0:rows, n % 2]).then_inc(stored[n % 2], 16)
                if w == 2:
                    sp.wait_ge(v_sb, t + 1)
                    sp.dma_start(m.v_dram[t * 4:(t + 1) * 4].rearrange("j p e -> p j e"), v[:, t % 2]).then_inc(v_stored, 16)
                    sp.wait_ge(v_stored, 16 * t + 16)
            for s in stored:
                sp.wait_ge(s, UN // 2 * 16)

        @block.scalar
        def _(act):
            for n, (t, w) in enumerate(units):
                rows = P if w < 2 else P // 2
                act.wait_ge(turned, n + 1)
                if n >= 2:
                    act.wait_ge(stored[n % 2], n // 2 * 16)
                act.activation(pr[0:rows, n % 2, 0], ev[0:rows, n % 2], ACT.Copy).then_inc(hi_done, 1)
                if w == 2:
                    act.wait_ge(v_mm, t + 1)
                    if t >= 2:
                        act.wait_ge(v_stored, 16 * (t - 1))
                    act.activation(v[:, t % 2], m.bank[:, 6 + t % 2, :].rearrange("p (j e) -> p j e", e=P), ACT.Copy,
                                   scale=1.0 / (XS * WS)).then_inc(v_sb, 1)

        @block.vector
        def _(dve):
            dve.wait_ge(loaded, 32)

            def threshold(i):
                dve.wait_ge(total, i + 1)
                dve.tensor_scalar(thr[:, i, 0:1], m.bank[:, 4, 0:1], D / (F * D), TERNARY, ALU.mult,
                                  ALU.mult).then_inc(thr_done, 1)
                dve.wait_ge(thr_done, 2 * i + 1)
                dve.tensor_scalar(thr[:, i, 1:2], thr[:, i, 0:1], -1.0, None, ALU.mult).then_inc(thr_done, 1)
                dve.wait_ge(thr_done, 2 * i + 2)

            def quantise(i, k):
                size = DC * F // QP
                q = (m.w1, m.w2)[i][:, :, :].rearrange("p a b -> p (a b)")[:, k * size:(k + 1) * size]
                w = m.stage[:, k * size:(k + 1) * size]
                dve.tensor_scalar(q, w, thr[:, i, 1:2], None, ALU.is_le).then_inc(below, 1)
                dve.wait_ge(below, i * QP + k + 1)
                dve.scalar_tensor_tensor(q, w, thr[:, i, 0:1], q, ALU.is_ge, ALU.subtract).then_inc(ternary, 1)

            for n, (t, w) in enumerate(units):
                if n == 0:
                    threshold(0)
                if n == W2_FROM:
                    sum_magnitudes(dve, m, 1)
                if n == W2_FROM + 1:
                    threshold(1)
                if n < QP:
                    quantise(0, n)
                if W2_FROM + 2 <= n < UN - 1:
                    quantise(1, n - W2_FROM - 2)
                rows, b = P if w < 2 else P // 2, n % 2
                dve.wait_ge(proj, n + 1)
                if n >= 2:
                    dve.wait_ge(turned, n - 1)
                cs = cos[0:rows, (t % TB) * TT:(t % TB + 1) * TT]
                sn = sin[0:rows, (t % TB) * TT:(t % TB + 1) * TT]
                ev_, od = (m.bank[0:rows, 2 * b + i, :] for i in range(2))
                for i, (x, y) in enumerate(((ev_, cs), (od, sn), (ev_, sn), (od, cs))):
                    ins = dve.tensor_tensor(t1[0:rows, b, i, :], x, y, ALU.mult)
                ins.then_inc(mults, 1)
            for k in range(UN - 1 - W2_FROM - 2, QP):
                quantise(1, k)

        @block.gpsimd
        def _(pool):
            for n, (t, w) in enumerate(units):
                rows, b = P if w < 2 else P // 2, n % 2
                pool.wait_ge(mults, n + 1)
                if n >= 2:
                    pool.wait_ge(lo_done, n - 1)
                pool.tensor_tensor(ev[0:rows, b, 0, :], t1[0:rows, b, 0, :], t1[0:rows, b, 1, :], ALU.subtract)
                pool.tensor_tensor(ev[0:rows, b, 1, :], t1[0:rows, b, 2, :], t1[0:rows, b, 3, :],
                                   ALU.add).then_inc(turned, 1)
                pool.wait_ge(turned, n + 1)
                pool.wait_ge(hi_done, n + 1)
                pool.tensor_tensor(pr[0:rows, b, 1], ev[0:rows, b], pr[0:rows, b, 0], ALU.subtract).then_inc(lo_done, 1)

        @block.tensor
        def _(pe):
            def mean(i):
                pe.wait_ge(m.summed, i + 1)
                pe.matmul(m.bank[:, 4, 0:1], m.mean_ones[:, :], m.whole[:, i:i + 1], start=True,
                          stop=True).then_inc(total, 1)

            mean(0)
            for n, (t, w) in enumerate(units):
                if n == W2_FROM + 2:
                    mean(1)
                rows = P if w < 2 else P // 2
                if n >= 2:
                    pe.wait_ge(mults, n - 1)
                at = 2 * P * w
                for i in range(2):
                    for c in range(DC):
                        ws = slice(at + i * rows, at + (i + 1) * rows)
                        mm = split_product(pe, m.bank[0:rows, 2 * (n % 2) + i, :], w_hi[:, c, ws], w_lo[:, c, ws],
                                           m.xh[:, c, t * TT:(t + 1) * TT], m.xl[:, c, t * TT:(t + 1) * TT],
                                           c == 0, c == DC - 1)
                mm.then_inc(proj, 1)
                if w == 2:
                    if t >= 2:
                        pe.wait_ge(v_sb, t - 1)
                    for j in range(4):
                        tok = slice(t * TT + j * P, t * TT + (j + 1) * P)
                        for c in range(DC):
                            ws = slice(D + HKV * HD, WN)
                            mm = split_product(pe, m.bank[:, 6 + t % 2, j * P:(j + 1) * P], m.xh[:, c, tok], m.xl[:, c, tok],
                                               w_hi[:, c, ws], w_lo[:, c, ws], c == 0, c == DC - 1)
                    mm.then_inc(v_mm, 1)


def softmax_maxima_and_ffn(nc, m, ctx):
    keep = lambda name, shape, dt=F32: ctx.enter_context(nc.sbuf_tensor("sa_" + name, shape, dt))
    m.qs = qs = keep("qs", [P, H1, T], F16)
    m.ks = ks = keep("ks", [P, B * HKV, T], F16)
    m.mx = mx = keep("mx", [P, NB, B * H1])
    m.mx2 = mx2 = keep("mx2", [P, NB // 2, B * H1])
    m.far = far = keep("far", [P, 3, P], F16)
    MU = [(i, s) for i in range(NB) for s in range(2) if s * TT < (i + 1) * P]
    NMU = len(MU)
    GT = B * HKV // NT
    FG = FC // GT
    assert FG == REP
    with ExitStack() as own:
        sb = lambda name, shape, dt=F32: own.enter_context(nc.sbuf_tensor("tf_" + name, shape, dt))
        b1 = sb("b1", [P, FC])
        b2 = sb("b2", [P, DC])
        h = sb("h", [P, 2, TT])
        hh = sb("hh", [P, 2, TT], F16)
        hl = sb("hl", [P, 2, TT], F16)
        out = [x[:, :, :].rearrange("p a n -> p (a n)").bitcast(F32) for x in (hh, hl)] + [h[:, 0, :], h[:, 1, :]]
        loaded, q_loaded, zeros_set = m.sem("tf_loaded"), m.sem("sa_q_loaded"), m.sem("sa_zeros_set")
        q8_loaded, rest_loaded = m.sem("sa_q8_loaded"), m.sem("sa_rest_loaded")
        sc_done = m.sem("sa_sc_done")
        max_done = m.sem("sa_max_done")
        up_done, gelu_done, hi_done, lo_done = (m.sem("tf_" + n) for n in ("up_done", "gelu_done", "hi_done", "lo_done"))
        down_done, sig_done, out_done = (m.sem("tf_" + n) for n in ("down_done", "sig_done", "out_done"))
        out_stored = [m.sem(f"tf_out_stored{d}") for d in range(DC)]
        UP, MAX, DOWN, RING = 0, 1, 4, 3
        SLOTS = ((0, 0), (1, 0), (0, 1))
        block = own.enter_context(nc.Block())

        @block.sync
        def _(sp):
            flat = lambda x: x.rearrange("p h n -> p (h n)")

            def load_q(b, part, sem):
                count = H1 // 4
                a, h = divmod(part * count, 16)
                heads = slice(part * count, (part + 1) * count)
                for slot, (qp, _) in enumerate(SLOTS):
                    for i in range(2):
                        at = 64 * b + slot * HD + i * HH
                        sp.dma_start(qs[at:at + HH, heads, :], m.q_dram[a, qp, i, :, b * T:(b + 1) * T]
                                     .rearrange("(h i) n -> i h n", i=HH)[:, h:h + count, :]).then_inc(sem, 16)
                at = 64 * b + STACK
                sp.dma_start(flat(qs[at:at + 16, heads, :]), m.d["zeros"].partition_broadcast(16)).then_inc(sem, 16)

            def load_k(b, sem):
                keys = ks[:, b * HKV:(b + 1) * HKV, :]
                for slot, (_, kp) in enumerate(SLOTS):
                    for i in range(2):
                        at = 64 * b + slot * HD + i * HH
                        sp.dma_start(keys[at:at + HH], m.k_dram[kp, i, :, b * T:(b + 1) * T]
                                     .rearrange("(h i) n -> i h n", i=HH)).then_inc(sem, 16)
                at = 64 * b + STACK
                sp.dma_start(flat(keys[at:at + 16]), m.d["units"].partition_broadcast(16)).then_inc(sem, 16)

            sp.dma_start(b1[:, :], m.d["b1T"]).then_inc(loaded, 16)
            sp.dma_start(b2[:, :], m.d["b2T"]).then_inc(loaded, 16)
            sp.dma_start(far[:, :, :], m.d["far"]).then_inc(q_loaded, 16)
            load_k(0, q_loaded)
            for b in range(B):
                load_q(b, 0, q_loaded)
            for part in range(1, 4):
                for b in range(B):
                    load_q(b, part, q8_loaded if part == 1 else rest_loaded)
            load_k(1, rest_loaded)
            with sp.Fori(0, NT) as t:
                for d in range(DC):
                    sp.wait_ge(out_done, t * DC + d + 1 + DC)
                    sp.dma_start(m.f_dram[bass.ds(t, 1), :, d, :].rearrange("a p n -> p (a n)"), out[d]).then_inc(out_stored[d], 16)
            for stored in out_stored:
                sp.wait_ge(stored, NT * 16 + 16)
        FIRST, SECOND, REST = 1 + 7 + B * 7, B * 7, 2 * B * 7 + 7

        @block.scalar
        def _(act):
            act.wait_ge(loaded, 32)
            with act.Fori(0, NT) as t:
                for f in range(FC):
                    k = t * FC + f
                    act.wait_ge(up_done, k + 1)
                    if f >= 2:
                        act.wait_ge(lo_done, k - 1)
                    else:
                        act.wait_ge(out_stored[2 + f], t * 16 + 16)
                    act.activation(h[:, f % 2, :], m.bank[:, UP, :], ACT.Gelu, bias=b1[:, f:f + 1],
                                   scale=1.0 / XS).then_inc(gelu_done, 1)
                    if f >= 2:
                        act.wait_ge(down_done, k - 1)
                    else:
                        act.wait_ge(out_stored[0], t * 16 + 16)
                    act.wait_ge(gelu_done, k + 1)
                    act.activation(hh[:, f % 2, :], h[:, f % 2, :], ACT.Copy).then_inc(hi_done, 1)
                act.wait_ge(down_done, t * FC + FC)
                act.wait_ge(lo_done, t * FC + FC)
                for d in range(DC):
                    if d >= 2:
                        act.wait_ge(out_done, t * DC + d - 1 + DC)
                    act.activation(h[:, d % 2, :], m.bank[:, DOWN + d, :], ACT.Sigmoid,
                                   bias=b2[:, d:d + 1]).then_inc(sig_done, 1)

        @block.gpsimd
        def _(pool):
            with pool.Fori(0, NT) as t:
                for f in range(FC):
                    pool.wait_ge(hi_done, t * FC + f + 1)
                    if f < 2:
                        pool.wait_ge(out_stored[1], t * 16 + 16)
                    pool.tensor_tensor(hl[:, f % 2, :], h[:, f % 2, :], hh[:, f % 2, :], ALU.subtract).then_inc(lo_done, 1)

        @block.vector
        def _(dve):
            dve.sem_inc(max_done, RING)
            dve.sem_inc(out_done, DC)
            for stored in out_stored:
                dve.sem_inc(stored, 16)
            for b in range(B):
                other = 64 * (1 - b)
                dve.memset(ks[other:other + 64, b * HKV:(b + 1) * HKV, :], 0.0).then_inc(zeros_set, 1)
            dve.wait_ge(loaded, 32)
            with dve.Fori(0, NT) as t:
                for f in range(FC):
                    k = t * FC + f
                    for u, (i, s) in enumerate(MU):
                        dve.wait_ge(sc_done, k * NMU + u + 1)
                        to = mx[:, i] if s == 0 else mx2[:, i - NB // 2]
                        n = min((i + 1) * P, (s + 1) * TT) - s * TT
                        dve.tensor_reduce(to[:, bass.ds(k, 1)], m.bank[:, MAX + u % RING, 0:n], AX.X, ALU.max).then_inc(max_done, 1)
                for d in range(DC):
                    dve.wait_ge(sig_done, t * DC + d + 1)
                    dve.scalar_tensor_tensor(out[d], m.bank[:, DOWN + d, :], b2[:, d:d + 1],
                                             h[:, d % 2, :], ALU.add, ALU.mult).then_inc(out_done, 1)

        @block.tensor
        def _(pe):
            pe.wait_ge(zeros_set, B)
            pe.wait_ge(q_loaded, FIRST * 16)

            def up(t, f, i):
                k = t * FC + f
                if i == 0 and f:
                    pe.wait_ge(gelu_done, k)
                c = i // 2
                mm = pe.matmul(m.bank[:, UP, :], m.w1[:, c, f * P:(f + 1) * P],
                               (m.xh, m.xl)[i % 2][:, c, bass.ds(t * TT, TT)], start=(i == 0), stop=(i == 2 * DC - 1))
                if i == 2 * DC - 1:
                    mm.then_inc(up_done, 1)

            def down(t, f, i):
                if i == 0:
                    pe.wait_ge(lo_done, t * FC + f + 1)
                    if f == 0:
                        pe.wait_ge(out_done, t * DC + DC)
                d = i // 2
                mm = pe.matmul(m.bank[:, DOWN + d, :], m.w2[:, f, d * P:(d + 1) * P], (hh, hl)[i % 2][:, f % 2, :],
                               start=(f == 0 and i % 2 == 0), stop=(f == FC - 1 and i % 2 == 1))
                if i == 2 * DC - 1:
                    mm.then_inc(down_done, 1)

            def maxima(t, f, u):
                k = t * FC + f
                i, s = MU[u]
                pe.wait_ge(max_done, k * NMU + u + 1)
                q = qs[:, bass.ds(k % H1, 1), i * P:(i + 1) * P].squeeze(1)
                keys = lambda lo, hi: ks[:, bass.ds(t * GT + f // FG, 1), lo:hi].squeeze(1)
                base, end = s * TT, min((i + 1) * P, (s + 1) * TT)
                to = m.bank[:, MAX + u % RING, :]
                if end == (i + 1) * P:
                    end -= P
                    d = to[:, end - base:end - base + P]
                    pe.matmul(d, far[:, 0, :], far[:, 1, :], start=True, stop=False)
                    mm = pe.matmul(d, q, keys(end, end + P), start=False, stop=True)
                if end > base:
                    mm = pe.matmul(to[:, 0:end - base], q, keys(base, end), start=True, stop=True)
                mm.then_inc(sc_done, 1)

            def share(f):
                if f == 0:
                    return 0, 4 * 2 * DC
                return f + 2, (4 if f + 2 < FC else 2) * DC

            with pe.Fori(0, NT) as t:
                for f in range(FC):
                    first, count = share(f)
                    for u in range(NMU):
                        maxima(t, f, u)
                        for n in range(u * count // NMU, (u + 1) * count // NMU):
                            if n < count - 2 * DC:
                                up(t, first + n // (2 * DC), n % (2 * DC))
                            else:
                                down(t, f, n % (2 * DC))
                    if f == 0:
                        pe.wait_ge(q8_loaded, SECOND * 16)
                pe.wait_ge(rest_loaded, REST * 16)


def softmax_weights(nc, m):
    ctx = ExitStack()
    with ctx:
        sb = lambda name, shape, dt=F32: ctx.enter_context(nc.sbuf_tensor("sw_" + name, shape, dt))
        qs, mx, far = m.qs, m.mx, m.far
        vg = sb("vg", [P, NB, 2 * HD])
        ob = sb("ob", [P, TT])
        rec = sb("rec", [P, 4, REP])
        pexp = m.w1[:, :, :].rearrange("p c f -> p (c f)").bitcast(F32).rearrange("p (a r n) -> p a r n", a=2, r=REP)
        places = m.w2[:, :, :].rearrange("p c d -> p (c d)")
        half = FC * D // 2
        mh = places[0:H1, 0:half].rearrange("p (b a n) -> p b a n", b=B, a=2)
        v = places[:, half:2 * half].bitcast(F32).rearrange("p (j h e) -> p j h e", j=NJ, h=HKV)
        v_loaded, ones_set = m.sem("sw_v_loaded"), m.sem("sw_ones_set")
        max_joined, turned, mhi, mlo = (m.sem("sw_" + n) for n in ("max_joined", "turned", "mhi", "mlo"))
        m_stored, m_loaded = [m.sem(f"sw_m_stored{b}") for b in range(B)], m.sem("sw_m_loaded")
        st_done = m.sem("sw_st_done")
        exp_done = m.sem("sw_exp_done")
        pv_done = m.sem("sw_pv_done")
        out_free = m.sem("sw_out_free")
        vg_done, ob_done, ob_turned = m.sem("sw_vg_done"), m.sem("sw_ob_done"), m.sem("sw_ob_turned")
        rec_done = m.sem("sw_rec_done")
        wo_loaded, wo_scaled, wo_hi, wo_lo = (m.sem("sw_wo_" + n) for n in ("loaded", "scaled", "hi", "lo"))
        WU = [(th, i) for th in range(2) for i in range(NB) if i * P < (th + 1) * TT]
        NWU = len(WU)
        RING, OUT = 3, 6
        AHEAD = 3
        block = ctx.enter_context(nc.Block())

        @block.sync
        def _(sp):
            sp.dma_start(m.wo[:, :, :], m.d["woT"].rearrange("(c p) n -> p c n", p=P)).then_inc(wo_loaded, 16)
            for j in range(NJ):
                sp.dma_start(v[:, j], m.v_dram[j].rearrange("p (h e) -> p h e", e=HD)).then_inc(v_loaded, 16)
            for b in range(B):
                sp.wait_ge(mlo, 2 * b + 2)
                sp.dma_start(m.m_dram[b].rearrange("a h n -> h a n"), mh[:, b]).then_inc(m_stored[b], 16)
            for b in range(B):
                sp.wait_ge(m_stored[b], 16)
                at = 64 * b + STACK
                sp.dma_start(qs[at:at + 2, :, :], m.m_dram[b]).then_inc(m_loaded, 16)

        @block.gpsimd
        def _(pool):
            pool.memset(vg[:, :, HD:2 * HD], 1.0).then_inc(ones_set, 1)
            pool.wait_ge(wo_hi, 1)
            pool.tensor_tensor(m.wo_lo[:, :, :], m.wo[:, :, :], m.wo_hi[:, :, :], ALU.subtract).then_inc(wo_lo, 1)
            pool.wait_ge(v_loaded, NJ * 16)
            for b in range(B):
                with pool.Fori(0, HKV) as g:
                    G = b * HKV + g
                    pool.wait_ge(pv_done, G * NWU + 2)
                    pool.tensor_copy(vg[:, :, 0:HD], v[:, b * NB:(b + 1) * NB, bass.ds(g, 1), :].squeeze(2)).then_inc(vg_done, 1)


        @block.tensor
        def _(pe):
            pe.wait_ge(ones_set, 1)

            def scores(b, g, n):
                th, i = WU[n]
                k = m.ks[:, bass.ds(b * HKV + g, 1), i * P:(i + 1) * P].squeeze(1)
                base, lo = th * TT, max(i * P, th * TT)
                for slot in range(2):
                    part = 2 * n + slot
                    pe.wait_ge(exp_done, (b * HKV + g) * 2 * NWU + part + 1)
                    for h in range(2):
                        q = lambda lo, hi: qs[:, bass.ds(g * REP + 2 * slot + h, 1), lo:hi].squeeze(1)
                        out, at = m.bank[:, part % RING * 2 + h, :], lo
                        if i * P >= base:
                            d = out[:, lo - base:lo - base + P]
                            pe.matmul(d, far[:, 0, :], far[:, 2, :], start=True, stop=False)
                            mm = pe.matmul(d, k, q(lo, lo + P), start=False, stop=True)
                            at += P
                        if at < base + TT:
                            mm = pe.matmul(out[:, at - base:TT], k, q(at, base + TT), start=True, stop=True)
                    mm.then_inc(st_done, 1)

            def values(b, g, n):
                th, i = WU[n]
                G = b * HKV + g
                if n == 0:
                    pe.wait_ge(vg_done, G + 1)
                if i == 0:
                    pe.wait_ge(out_free, 2 * G + th + 1)
                pe.wait_ge(exp_done, G * (2 * NWU) + 2 * n + 2 + RING)
                at = max(i * P - th * TT, 0)
                last = i == (th + 1) * 4 - 1
                for r in range(REP):
                    mm = pe.matmul(m.bank[32 * r:32 * r + 32, OUT + th, at:TT], vg[:, i, :], pexp[:, n % 2, r, at:TT],
                                   start=(i == 0), stop=last, skip_group_check=True)
                mm.then_inc(pv_done, 1)

            def turn(b, g, th):
                pe.wait_ge(ob_done, 2 * (b * HKV + g) + th + 1)
                for j in range(4):
                    mm = pe.transpose(m.bank[:, OUT + th, j * P:(j + 1) * P], ob[:, j * P:(j + 1) * P], m.ident[:, :])
                mm.then_inc(ob_turned, 1)

            def steps(b, g, ns, last=False):
                for n in ns:
                    if n + 1 < NWU:
                        scores(b, g, n + 1)
                    elif not last:
                        scores(b, g + 1, 0)
                    values(b, g, n)
                    if n == 6:
                        turn(b, g, 0)

            pe.wait_ge(max_joined, 1)
            for b in range(B):
                for i in range(NB):
                    mm = pe.transpose(m.bank[0:H1, 2 * b + i // 4, (i % 4) * P:(i % 4 + 1) * P],
                                      mx[:, i, b * H1:(b + 1) * H1], m.ident[:, :])
                mm.then_inc(turned, 1)
            pe.wait_ge(mlo, 4)
            pe.wait_ge(m_loaded, 32)
            for b in range(B):
                scores(b, 0, 0)
                steps(b, 0, range(AHEAD))
                with pe.Fori(0, HKV - 1) as g:
                    steps(b, g, range(AHEAD, NWU))
                    steps(b, g + 1, range(AHEAD))
                    turn(b, g, 1)
                steps(b, HKV - 1, range(AHEAD, NWU), last=True)
                turn(b, HKV - 1, 1)

        @block.scalar
        def _(act):
            for b in range(B):
                act.wait_ge(turned, b + 1)
                for i in range(2):
                    act.activation(mh[:, b, 0, i * TT:(i + 1) * TT], m.bank[0:H1, 2 * b + i, :], ACT.Copy,
                                   scale=-1.0 / QS).then_inc(mhi, 1)
            act.activation(m.mx2[:, 0, 0:1], m.ident[:, 0:1], ACT.Exp)
            act.wait_ge(wo_loaded, 16)
            act.activation(m.wo[:, :, :], m.wo[:, :, :], ACT.Copy, scale=WS).then_inc(wo_scaled, 1)
            act.wait_ge(wo_scaled, 1)
            act.activation(m.wo_hi[:, :, :], m.wo[:, :, :], ACT.Copy).then_inc(wo_hi, 1)
            for b in range(B):
                with act.Fori(0, HKV) as g:
                    for n, (th, i) in enumerate(WU):
                        G = b * HKV + g
                        at = max(i * P - th * TT, 0)
                        for slot in range(2):
                            part = 2 * n + slot
                            act.wait_ge(st_done, G * (2 * NWU) + part + 1)
                            act.wait_ge(pv_done, G * NWU + n + 1)
                            act.activation(pexp[:, n % 2, 2 * slot:2 * slot + 2, at:TT],
                                           m.bank[:, part % RING * 2:part % RING * 2 + 2, at:TT], ACT.Exp,
                                           scale=1.0 / (QS * QS * HD ** 0.5)).then_inc(exp_done, 1)

        @block.vector
        def _(dve):
            dve.sem_inc(out_free, 2)
            dve.sem_inc(exp_done, RING)
            dve.sem_inc(pv_done, 2)
            late = mx[:, NB // 2:NB]
            dve.tensor_tensor(late, late, m.mx2[:, :, :], ALU.max).then_inc(max_joined, 1)
            for b in range(B):
                for i in range(2):
                    dve.wait_ge(mhi, 2 * b + i + 1)
                    dve.scalar_tensor_tensor(mh[:, b, 1, i * TT:(i + 1) * TT], m.bank[0:H1, 2 * b + i, :], -1.0 / QS,
                                             mh[:, b, 0, i * TT:(i + 1) * TT], ALU.mult, ALU.subtract).then_inc(mlo, 1)
            dve.wait_ge(wo_lo, 1)
            for b in range(B):
                with dve.Fori(0, HKV) as g:
                    for th in range(2):
                        G = b * HKV + g
                        n = 2 * G + th + 1
                        dve.wait_ge(pv_done, G * NWU + (4 if th == 0 else NWU) + 2)
                        dve.tensor_copy(ob[:, :], m.bank[:, OUT + th, :]).then_inc(ob_done, 1)
                        dve.wait_ge(ob_turned, n)
                        o = m.bank[:, OUT + th, :].rearrange("p (j r e) -> p j r e", r=REP, e=2 * HD)
                        dve.reciprocal(rec[:, :, :], o[:, :, :, HD]).then_inc(rec_done, 1)
                        dve.wait_ge(rec_done, n)
                        y = m.y[:, b * NB + th * 4:b * NB + th * 4 + 4, bass.ds(g * REP * HD, REP * HD)]
                        dve.tensor_tensor(y.rearrange("p j (r e) -> p j r e", e=HD), o[:, :, :, 0:HD],
                                          rec[:, :, :].unsqueeze(3).broadcast_to([P, 4, REP, HD]), ALU.mult).then_inc(out_free, 1)


def project_out(nc, m):
    ctx = ExitStack()
    with ctx:
        w_hi, w_lo = m.wo_hi, m.wo_lo
        place = m.qs[:, :, :].rearrange("p h n -> p (h n)")
        tile = DC * TT
        gate = place[:, 0:2 * NT * tile].bitcast(F32).rearrange("p (t c n) -> p t c n", t=NT, c=DC)
        yh, yl = (place[:, (2 * NT + i) * tile:(2 * NT + i + 2) * tile].rearrange("p (a c n) -> p a c n", a=2, c=DC)
                  for i in (0, 2))
        s = place[:, (2 * NT + 4) * tile:(2 * NT + 5) * tile]
        s = s.bitcast(F32).rearrange("p (a n) -> p a n", a=2)
        gate_loaded = [m.sem(f"po_gate_loaded{t}") for t in range(NT)]
        turned, hi_done, lo_done = m.sem("po_turned"), m.sem("po_hi_done"), m.sem("po_lo_done")
        o_mm, scaled, added, stored = (m.sem("po_" + n) for n in ("o_mm", "scaled", "added", "stored"))
        block = ctx.enter_context(nc.Block())

        @block.sync
        def _(sp):
            for t in range(NT):
                sp.dma_start(gate[:, t], m.f_dram[t]).then_inc(gate_loaded[t], 16)
            for t in range(NT):
                for c in range(DC):
                    sp.wait_ge(added, t * DC + c + 1)
                    tok = slice(t * TT, (t + 1) * TT)
                    sp.dma_start(m.outT[c * P:(c + 1) * P, tok], m.x[:, c, tok]).then_inc(stored, 16)
            sp.wait_ge(stored, NT * DC * 16)

        @block.scalar
        def _(act):
            for t in range(NT):
                for c in range(DC):
                    act.wait_ge(turned, t * DC + c + 1)
                    if t >= 2:
                        act.wait_ge(o_mm, (t - 1) * DC)
                    act.activation(yh[:, t % 2, c, :], m.bank[:, c, :], ACT.Copy, scale=YS).then_inc(hi_done, 1)

        @block.vector
        def _(dve):
            def low(t):
                for c in range(DC):
                    dve.wait_ge(hi_done, t * DC + c + 1)
                    dve.scalar_tensor_tensor(yl[:, t % 2, c, :], m.bank[:, c, :], YS, yh[:, t % 2, c, :], ALU.mult,
                                             ALU.subtract).then_inc(lo_done, 1)

            low(0)
            for t in range(NT):
                if t + 1 < NT:
                    low(t + 1)
                dve.wait_ge(gate_loaded[t], 16)
                for c in range(DC):
                    n = t * DC + c
                    dve.wait_ge(o_mm, n + 1)
                    tok = slice(t * TT, (t + 1) * TT)
                    dve.scalar_tensor_tensor(s[:, c % 2, :], m.bank[:, 4 + c, :], 1.0 / (YS * WS), gate[:, t, c, :],
                                             ALU.mult, ALU.mult).then_inc(scaled, 1)
                    dve.wait_ge(scaled, n + 1)
                    dve.tensor_tensor(m.x[:, c, tok], m.x[:, c, tok], s[:, c % 2, :], ALU.add).then_inc(added, 1)

        @block.tensor
        def _(pe):
            def turn(t):
                for c in range(DC):
                    if t:
                        pe.wait_ge(lo_done, DC * (t - 1) + c + 1)
                    for j in range(4):
                        mm = pe.transpose(m.bank[:, c, j * P:(j + 1) * P], m.y[:, t * 4 + j, c * P:(c + 1) * P],
                                          m.ident[:, :])
                    mm.then_inc(turned, 1)

            turn(0)
            for t in range(NT):
                if t + 1 < NT:
                    turn(t + 1)
                pe.wait_ge(lo_done, DC * (t + 1))
                for c in range(DC):
                    if t:
                        pe.wait_ge(scaled, DC * (t - 1) + c + 1)
                    for k in range(DC):
                        mm = split_product(pe, m.bank[:, 4 + c, :], w_hi[:, k, c * P:(c + 1) * P],
                                           w_lo[:, k, c * P:(c + 1) * P], yh[:, t % 2, k, :], yl[:, t % 2, k, :],
                                           k == 0, k == DC - 1)
                    mm.then_inc(o_mm, 1)


def program(nc, d, outT):
    m = Shared()
    m.d, m.outT = d, outT
    with ExitStack() as ctx:
        def sb(name, shape, dt=F32, on=ctx):
            return on.enter_context(nc.sbuf_tensor("m_" + name, shape, dt))

        m.sem = lambda name: ctx.enter_context(nc.semaphore(name))
        m.bank = ctx.enter_context(nc.psum_tensor("bank", [P, 8, TT], F32))
        m.q_dram = nc.dram_tensor("q_scratch", (2, 2, 2, P, N), F16, kind="Internal").ap()
        m.k_dram = nc.dram_tensor("k_scratch", (2, 2, HKV * HH, N), F16, kind="Internal").ap()
        m.v_dram = nc.dram_tensor("v_scratch", (NJ, P, HKV * HD), F32, kind="Internal").ap()
        m.f_dram = nc.dram_tensor("f_scratch", (NT, P, DC, TT), F32, kind="Internal").ap()
        m.m_dram = nc.dram_tensor("m_scratch", (B, 2, H1, T), F16, kind="Internal").ap()
        m.x = sb("x", [P, DC, N])
        m.y = sb("y", [P, NJ, D])
        pair = m.y[:, :, :].rearrange("p j d -> p (j d)").bitcast(F16).rearrange("p (a c n) -> p a c n", a=2, c=DC)
        m.xh, m.xl = pair[:, 0], pair[:, 1]
        m.ident = sb("ident", [P, P])
        m.mean_ones = sb("mean_ones", [P, P])
        m.x_loaded = [m.sem(f"x_loaded{t}") for t in range(NT)]
        m.const_loaded = m.sem("const_loaded")
        m.const_count = 3 * 16
        with ExitStack() as first:
            m.acc = sb("acc", [P, DC, N], F32, first)
            m.la_stage = sb("la_stage", [P, DC, D], F32, first)
            m.la_loaded = m.sem("la_w_loaded")
            with ExitStack() as routed:
                m.gates = sb("gates", [P, N], F16, routed)
                m.sel = sb("sel", [P, EA * P], F16, routed)
                m.ex_stage = sb("ex_stage", [P, 2, EG * WE], F32, routed)
                m.ex_staged = m.sem("ex_staged")
                with nc.Block() as block:
                    @block.sync
                    def _(sp):
                        for t in range(NT):
                            tok = slice(t * TT, (t + 1) * TT)
                            sp.dma_start(m.x[:, :, tok], d["xT"].rearrange("(c p) n -> p c n", p=P)[:, :, tok]).then_inc(m.x_loaded[t], 16)
                            if t == 0:
                                sp.dma_start(m.ident[:, :], d["ident"]).then_inc(m.const_loaded, 16)
                                sp.dma_start(m.mean_ones[:, :], d["mean_ones"]).then_inc(m.const_loaded, 16)
                                sp.dma_start(m.sel[:, :], d["sel"]).then_inc(m.const_loaded, 16)
                        for p in range(2):
                            sp.dma_start(m.ex_stage[:, p, :], d["WE"][p]).then_inc(m.ex_staged, 16)
                        sp.dma_start(m.la_stage[:, :, :], d["g0"].rearrange("(c p) n -> p c n", p=P)).then_inc(m.la_loaded, 16)
                layer_norm(nc, m, "ln0")
                m.ex_hi = sb("ex_hi", [P, 2, EG * WE], F16, routed)
                m.ex_lo = sb("ex_lo", [P, 2, EG * WE], F16, routed)
                router(nc, m)
                experts(nc, m)
            linear_attention(nc, m)
        with ExitStack() as late:
            m.w1 = sb("w1", [P, DC, F], F16, late)
            m.w2 = sb("w2", [P, FC, D], F16, late)
            m.staged, m.parts, m.summed = m.sem("staged"), m.sem("parts"), m.sem("summed")
            with ExitStack() as staged:
                m.wqkv = sb("wqkv", [P, DC, WN], F32, staged)
                m.wqkv_hi = sb("wqkv_hi", [P, DC, WN], F16, staged)
                m.wqkv_lo = sb("wqkv_lo", [P, DC, WN], F16, staged)
                m.stage = sb("stage", [P, DC * F], F32, staged)
                m.part = sb("part", [P, P], F32, staged)
                m.whole = sb("whole", [P, 2], F32, staged)
                layer_norm(nc, m, "ln1")
                project_qkv(nc, m)
            softmax_maxima_and_ffn(nc, m, late)
            m.wo = m.y[:, NB:NB + DC, :]
            m.wo_hi = sb("wo_hi", [P, DC, D], F16, late)
            m.wo_lo = sb("wo_lo", [P, DC, D], F16, late)
            softmax_weights(nc, m)
            project_out(nc, m)


def constants():
    f = np.float32
    c = {"ident": np.eye(P, dtype=f), "mean_ones": np.full((P, P), 1.0 / D, f)}
    sel = np.zeros((P, EA, P), np.float16)
    for e in range(EA):
        sel[e, e] = sel[LO + e, e] = 1
    c["sel"] = sel.reshape(P, EA * P)
    c["block_mask"] = np.kron(np.eye(HG, dtype=f), np.ones((DK, DK), f))
    t = np.arange(T, dtype=f)[:, None]
    inv = (f(1.0) / f(10000.0) ** (np.arange(HALF, dtype=f) / f(HALF))).astype(f)
    ang = (t * inv[None, :]).astype(f)
    cos, sin = np.cos(ang).astype(f), np.sin(ang).astype(f)
    c["cos0"] = cos.reshape(NB, P, HALF).transpose(1, 0, 2)
    c["sin0"] = np.stack([-sin, sin], 1).reshape(NB, P, 2, HALF).transpose(1, 0, 2, 3)
    inv = (f(1.0) / f(10000.0) ** (np.arange(0, HD, 2, dtype=f) / f(HD))).astype(f)
    ang = (t * inv[None, :]).astype(f)
    scale = f(QS / (XS * WS))
    c["cos1"] = np.tile((np.cos(ang).astype(f) * scale).T, (P // HH, 1))
    c["sin1"] = np.tile((np.sin(ang).astype(f) * scale).T, (P // HH, 1))
    far = np.zeros((P, 3, P), np.float16)
    far[:, 0] = np.eye(P) * FAR
    far[:, 1] = np.triu(np.full((P, P), -FAR), 1)
    far[:, 2] = np.tril(np.full((P, P), -FAR), -1)
    c["far"] = far
    c["zeros"] = np.zeros(H1 * T // 4, np.float16)
    c["units"] = np.full(HKV * T, QS, np.float16)
    return c


def layouts(i):
    t = {"xT": i["L0_attn_x"].reshape(N, D).T, "WrT": i["L0_ffn_Wr"].T,
         "br": np.broadcast_to(i["L0_ffn_br"], (P, E))}
    up = np.concatenate([i["L0_ffn_W1"], i["L0_ffn_Ws1"].reshape(SHARED, M, D)]).transpose(0, 2, 1)
    down = np.concatenate([i["L0_ffn_W2"].transpose(0, 2, 1), i["L0_ffn_Ws2"].T.reshape(SHARED, M, D)])
    up = up.reshape(NG, EG, DC, P, M).transpose(0, 3, 1, 2, 4).reshape(NG, P, EG, DC * M)
    down = down.reshape(NG, EG, MC, P, D).transpose(0, 3, 1, 2, 4).reshape(NG, P, EG, MC * D)
    t["WE"] = np.concatenate([up, down], 3).reshape(NG, P, EG * WE)
    for a in "qkvgo":
        t[a + "0"] = i[f"L0_attn_{a}w"]
    for a in "qkv":
        t[a + "b"] = i[f"L0_attn_{a}b"]
    for a in "go":
        t[a + "bT"] = i[f"L0_attn_{a}b"].reshape(DC, P).T
    t["w1T"], t["w2T"] = i["L1_ffn_w1"].T, i["L1_ffn_w2"].T
    t["b1T"], t["b2T"] = i["L1_ffn_b1"].reshape(FC, P).T, i["L1_ffn_b2"].reshape(DC, P).T
    q = i["L1_attn_wq"].reshape(2, 16, HH, 2, D).transpose(0, 3, 1, 2, 4).reshape(D, D)
    k = i["L1_attn_wk"].reshape(HKV, HH, 2, D).transpose(2, 0, 1, 3).reshape(HKV * HD, D)
    t["wqkvT"] = np.concatenate([q, k, i["L1_attn_wv"]]).T
    t["woT"] = i["L1_attn_wo"].T
    return t


def kernel(**inputs):
    import concourse.bacc as bacc
    from concourse.bass_utils import run_bass_kernel_spmd

    arrays = layouts({k: np.asarray(v) for k, v in inputs.items()}) | constants()
    arrays = {f"in_{k}": np.ascontiguousarray(v) for k, v in arrays.items()}
    nc = bacc.Bacc("TRN2", target_bir_lowering=False, num_devices=1)
    d = {
        k[3:]: nc.dram_tensor(k, v.shape, mybir.dt.from_np(v.dtype), kind="ExternalInput").ap()
        for k, v in arrays.items()}
    outT = nc.dram_tensor("outT", (D, N), F32, kind="ExternalOutput").ap()
    program(nc, d, outT)
    r = run_bass_kernel_spmd(nc, [arrays], core_ids=[0])
    return np.ascontiguousarray(r.results[0]["outT"].T).reshape(B, T, D)
```
